# Optimizing a Trainium2 kernel written in Bass

```python
import numpy as np
import jax
import jax.numpy as jnp

def _softmax(x, axis=-1):
    return jax.nn.softmax(x, axis=axis)

def _gelu(x):
    return jax.nn.gelu(x, approximate=True)

def _silu(x):
    return jax.nn.silu(x)

def _sigmoid(x):
    return jax.nn.sigmoid(x)

def _layernorm(x, axis=-1, eps=1e-05):
    m = jnp.mean(x, axis=axis, keepdims=True)
    v = jnp.var(x, axis=axis, keepdims=True)
    return (x - m) / jnp.sqrt(v + eps)

def _scatter_add(tgt, idx, src, axis=0):
    return tgt.at[idx].add(src)

def _segment_sum(src, seg, n):
    return jax.ops.segment_sum(src, seg, n)
kernel_name = 'mk_gnn_preln_d4_gnn_r32_5782df'

def setup_inputs(seed: int=0):
    np.random.seed(seed)
    _w = jnp.asarray

    def _rec_inputs():
        import jax
        import jax.numpy as jnp
        _gk = jax.random.key(seed)
        x = -0.000202 + 1 * jax.random.normal(jax.random.fold_in(_gk, 1), (3125, 64), jnp.float32)
        _s = jax.random.randint(jax.random.fold_in(_gk, 2), (50000,), 0, 3125, jnp.int32)
        _d = jax.random.randint(jax.random.fold_in(_gk, 3), (50000,), 0, 3125, jnp.int32)
        _loop = jnp.arange(3125, dtype=jnp.int32)
        src = jnp.concatenate([_s, _d, _loop])
        dst = jnp.concatenate([_d, _s, _loop])
        _o = jnp.argsort(dst, stable=True)
        src = src[_o]
        dst = dst[_o]
        edge_attr_64 = -5.16925e-05 + 1.00005 * jax.random.normal(jax.random.fold_in(_gk, 13), (103125, 64), jnp.float32)
        edge_weight = jax.random.uniform(jax.random.fold_in(_gk, 15), (103125,), jnp.float32, 0.0, 0.999999)
        return (x, src, dst, edge_attr_64, edge_weight)
    x, src, dst, edge_attr_64, edge_weight = _rec_inputs()

    def _L0_gnn_setup():
        import jax, jax.numpy as jnp
        import numpy as np
        N_NODES = 3125
        N_EDGES = 50000
        D_FEAT = 64
        key = jax.random.key(seed)
        k1, k2, k3 = jax.random.split(key, 3)
        x = jax.random.normal(k1, (N_NODES, D_FEAT), dtype=jnp.float32)
        edge_index = jax.random.randint(k2, (2, N_EDGES), 0, N_NODES, dtype=jnp.int64)
        edge_attr = jax.random.uniform(k3, (N_EDGES,), dtype=jnp.float32)
        return {'x': x, 'edge_index': edge_index, 'edge_attr': edge_attr}
    _L0_gnn_all = _L0_gnn_setup()
    _L0_gnn_in = {k: v for k, v in _L0_gnn_all.items() if k in ()}
    del _L0_gnn_all

    def _L1_gnn_setup():
        import jax, jax.numpy as jnp
        import numpy as np
        N_NODES = 3125
        N_EDGES = 50000
        D_FEAT = 64
        OUT_FEATS = 64
        key = jax.random.key(seed)
        k1, k2, k3, k4, k5 = jax.random.split(key, 5)
        features = jax.random.normal(k1, (N_NODES, D_FEAT), dtype=jnp.float32)
        src = jax.random.randint(k2, (N_EDGES,), 0, N_NODES, dtype=jnp.int32)
        dst = jax.random.randint(k3, (N_EDGES,), 0, N_NODES, dtype=jnp.int32)
        W = jax.random.normal(k4, (D_FEAT, OUT_FEATS), dtype=jnp.float32) / np.sqrt(D_FEAT)
        b = jnp.zeros((OUT_FEATS,), dtype=jnp.float32)
        return {'features': features, 'W': W, 'b': b, 'src': src, 'dst': dst}
    _L1_gnn_all = _L1_gnn_setup()
    _L1_gnn_in = {k: v for k, v in _L1_gnn_all.items() if k in ('W', 'b')}
    del _L1_gnn_all

    def _L2_gnn_setup():
        import jax, jax.numpy as jnp
        import numpy as np
        N_NODES = 3125
        N_EDGES = 50000
        D = 64
        HIDDEN = 128
        D_OUT = 64
        key = jax.random.key(seed)
        ks = jax.random.split(key, 8)
        x = jax.random.normal(ks[0], (N_NODES, D), dtype=jnp.float32)
        edge_index = jax.random.randint(ks[1], (2, N_EDGES), 0, N_NODES, dtype=jnp.int64)
        edge_attr = jax.random.normal(ks[2], (N_EDGES, D), dtype=jnp.float32)
        u = jax.random.normal(ks[3], (1, D), dtype=jnp.float32)
        batch = jnp.zeros((N_NODES,), dtype=jnp.int64)
        s1 = 1.0 / np.sqrt(2 * D)
        s2 = 1.0 / np.sqrt(HIDDEN)
        W1 = jax.random.uniform(ks[4], (2 * D, HIDDEN), jnp.float32, -s1, s1)
        b1 = jax.random.uniform(ks[5], (HIDDEN,), jnp.float32, -s1, s1)
        W2 = jax.random.uniform(ks[6], (HIDDEN, D_OUT), jnp.float32, -s2, s2)
        b2 = jax.random.uniform(ks[7], (D_OUT,), jnp.float32, -s2, s2)
        return {'x': x, 'edge_index': edge_index, 'edge_attr': edge_attr, 'u': u, 'batch': batch, 'W1': W1, 'b1': b1, 'W2': W2, 'b2': b2}
    _L2_gnn_all = _L2_gnn_setup()
    _L2_gnn_in = {k: v for k, v in _L2_gnn_all.items() if k in ('u', 'W1', 'b1', 'W2', 'b2')}
    del _L2_gnn_all

    def _L3_gnn_setup():
        import jax, jax.numpy as jnp
        import numpy as np
        N_NODES = 50000
        N_EDGES = 25000
        D_NODE = 64
        HID = 64
        N_TGT = 64

        def _init_linear(key, fan_in, fan_out):
            kw, kb = jax.random.split(key)
            bound = 1.0 / np.sqrt(fan_in)
            W = jax.random.uniform(kw, (fan_in, fan_out), minval=-bound, maxval=bound, dtype=jnp.float32)
            b = jax.random.uniform(kb, (fan_out,), minval=-bound, maxval=bound, dtype=jnp.float32)
            return (W, b)
        key = jax.random.key(seed)
        ks = jax.random.split(key, 8)
        x = jax.random.normal(ks[0], (N_NODES, D_NODE), dtype=jnp.float32)
        edge_index = jax.random.randint(ks[1], (2, N_EDGES), 0, N_NODES, dtype=jnp.int64)
        edge_attr = jax.random.normal(ks[2], (N_EDGES, HID), dtype=jnp.float32)
        u = jax.random.normal(ks[3], (1, 16), dtype=jnp.float32)
        batch = jnp.zeros((N_NODES,), dtype=jnp.int64)
        W1a, b1a = _init_linear(ks[4], D_NODE + HID, HID)
        W1b, b1b = _init_linear(ks[5], HID, HID)
        W2a, b2a = _init_linear(ks[6], D_NODE + HID, HID)
        W2b, b2b = _init_linear(ks[7], HID, N_TGT)
        return {'x': x, 'edge_index': edge_index, 'edge_attr': edge_attr, 'u': u, 'batch': batch, 'W1a': W1a, 'b1a': b1a, 'W1b': W1b, 'b1b': b1b, 'W2a': W2a, 'b2a': b2a, 'W2b': W2b, 'b2b': b2b}
    _L3_gnn_all = _L3_gnn_setup()
    _L3_gnn_in = {k: v for k, v in _L3_gnn_all.items() if k in ('u', 'W1a', 'b1a', 'W1b', 'b1b', 'W2a', 'b2a', 'W2b', 'b2b')}
    del _L3_gnn_all
    return {'x': x, 'src': src, 'dst': dst, 'edge_attr_64': edge_attr_64, 'edge_weight': edge_weight, 'L1_gnn_W': _L1_gnn_in['W'], 'L1_gnn_b': _L1_gnn_in['b'], 'L2_gnn_u': _L2_gnn_in['u'], 'L2_gnn_W1': _L2_gnn_in['W1'], 'L2_gnn_b1': _L2_gnn_in['b1'], 'L2_gnn_W2': _L2_gnn_in['W2'], 'L2_gnn_b2': _L2_gnn_in['b2'], 'L3_gnn_u': _L3_gnn_in['u'], 'L3_gnn_W1a': _L3_gnn_in['W1a'], 'L3_gnn_b1a': _L3_gnn_in['b1a'], 'L3_gnn_W1b': _L3_gnn_in['W1b'], 'L3_gnn_b1b': _L3_gnn_in['b1b'], 'L3_gnn_W2a': _L3_gnn_in['W2a'], 'L3_gnn_b2a': _L3_gnn_in['b2a'], 'L3_gnn_W2b': _L3_gnn_in['W2b'], 'L3_gnn_b2b': _L3_gnn_in['b2b']}

def reference(x, src, dst, edge_attr_64, edge_weight, L1_gnn_W, L1_gnn_b, L2_gnn_u, L2_gnn_W1, L2_gnn_b1, L2_gnn_W2, L2_gnn_b2, L3_gnn_u, L3_gnn_W1a, L3_gnn_b1a, L3_gnn_W1b, L3_gnn_b1b, L3_gnn_W2a, L3_gnn_b2a, L3_gnn_W2b, L3_gnn_b2b):
    import jax
    import jax.numpy as jnp

    def _L0_gnn_ref(x, edge_index, edge_attr):
        import jax, jax.numpy as jnp
        import numpy as np
        N_NODES = 3125
        N_EDGES = 50000
        D_FEAT = 64
        row, col = (edge_index[0], edge_index[1])
        B = jnp.exp(-edge_attr)
        msgs = B[:, None] * x[col]
        out = jax.ops.segment_sum(msgs, row, num_segments=N_NODES)
        return out

    def _L1_gnn_ref(features, W, b, src, dst):
        import jax, jax.numpy as jnp
        import numpy as np
        N_NODES = 3125
        N_EDGES = 50000
        D_FEAT = 64
        OUT_FEATS = 64
        msgs = features[src]
        summed = jax.ops.segment_sum(msgs, dst, num_segments=N_NODES)
        deg = jax.ops.segment_sum(jnp.ones_like(dst, dtype=features.dtype), dst, num_segments=N_NODES)
        h_neigh = summed / jnp.maximum(deg, 1.0)[:, None]
        h = h_neigh @ W + b
        return jax.nn.relu(h)

    def _L2_gnn_ref(x, edge_index, edge_attr, u, batch, W1, b1, W2, b2):
        import jax, jax.numpy as jnp
        import numpy as np
        N_NODES = 3125
        N_EDGES = 50000
        D = 64
        HIDDEN = 128
        D_OUT = 64
        row = edge_index[0]
        aggr_msg = jax.ops.segment_sum(edge_attr, row, num_segments=x.shape[0])
        h = jnp.concatenate([x, aggr_msg], axis=-1)
        h = jax.nn.relu(h @ W1 + b1)
        out = h @ W2 + b2
        return out

    def _L3_gnn_ref(x, edge_index, edge_attr, u, batch, W1a, b1a, W1b, b1b, W2a, b2a, W2b, b2b):
        import jax, jax.numpy as jnp
        import numpy as np
        N_NODES = 50000
        N_EDGES = 25000
        D_NODE = 64
        HID = 64
        N_TGT = 64

        def _init_linear(key, fan_in, fan_out):
            kw, kb = jax.random.split(key)
            bound = 1.0 / np.sqrt(fan_in)
            W = jax.random.uniform(kw, (fan_in, fan_out), minval=-bound, maxval=bound, dtype=jnp.float32)
            b = jax.random.uniform(kb, (fan_out,), minval=-bound, maxval=bound, dtype=jnp.float32)
            return (W, b)
        row, col = (edge_index[0], edge_index[1])
        msg = jnp.concatenate([x[col], edge_attr], axis=1)
        msg = jnp.maximum(msg @ W1a + b1a, 0.0) @ W1b + b1b
        summed = jax.ops.segment_sum(msg, row, num_segments=x.shape[0])
        counts = jax.ops.segment_sum(jnp.ones((row.shape[0],), msg.dtype), row, num_segments=x.shape[0])
        agg = summed / jnp.maximum(counts, 1.0)[:, None]
        h = jnp.concatenate([x, agg], axis=1)
        out = jnp.maximum(h @ W2a + b2a, 0.0) @ W2b + b2b
        return out
    edge_index = jnp.stack([src, dst])
    batch0 = jnp.zeros((3125,), jnp.int32)
    h = jnp.maximum(_layernorm(x, axis=-1), 0.0)
    x = x + _L0_gnn_ref(h, edge_index, edge_weight)
    h = jnp.maximum(_layernorm(x, axis=-1), 0.0)
    x = x + _L1_gnn_ref(h, L1_gnn_W, L1_gnn_b, src, dst)
    h = jnp.maximum(_layernorm(x, axis=-1), 0.0)
    x = x + _L2_gnn_ref(h, edge_index, edge_attr_64, L2_gnn_u, batch0, L2_gnn_W1, L2_gnn_b1, L2_gnn_W2, L2_gnn_b2)
    h = jnp.maximum(_layernorm(x, axis=-1), 0.0)
    x = x + _L3_gnn_ref(h, edge_index, edge_attr_64, L3_gnn_u, batch0, L3_gnn_W1a, L3_gnn_b1a, L3_gnn_W1b, L3_gnn_b1b, L3_gnn_W2a, L3_gnn_b2a, L3_gnn_W2b, L3_gnn_b2b)
    return x

_drawn_inputs = setup_inputs


def setup_inputs(seed=0):
    import zlib

    import numpy as np

    out = dict(_drawn_inputs(seed))
    spreads = {'L1_gnn_b': (0.0, 0.8)}
    factors = {'L2_gnn_b1': 8.0,
     'L2_gnn_b2': 8.0,
     'L3_gnn_W1a': 8.0,
     'L3_gnn_b1a': 8.0,
     'L3_gnn_W1b': 8.0,
     'L3_gnn_b1b': 8.0,
     'L3_gnn_W2a': 5.058,
     'L3_gnn_b2a': 8.0,
     'L3_gnn_W2b': 4.351,
     'L3_gnn_b2b': 22.311}
    for name, (base, spread) in spreads.items():
        noise = np.random.default_rng([zlib.crc32(name.encode()), seed]).standard_normal(out[name].shape)
        drawn = base * np.exp(spread * noise) if base else spread * noise
        out[name] = jnp.asarray(drawn.astype(out[name].dtype))
    for name, factor in factors.items():
        out[name] = (out[name] * factor).astype(out[name].dtype)
    return out
```

```python
from contextlib import ExitStack

import concourse.bass as bass
from concourse import mybir
from concourse.alu_op_type import AluOpType as ALU

F32 = mybir.dt.float32
BF16 = mybir.dt.bfloat16
F16 = mybir.dt.float16
I32 = mybir.dt.int32
U16 = mybir.dt.uint16
ACT = mybir.ActivationFunctionType
AX = mybir.AxisListType

N_NODES, N_EDGES, D = 3125, 103125, 64
NT = 25
NP = N_NODES // NT
EP = 125
ET = N_EDGES // EP
CENTRE = (N_NODES - 1) // 2
EPS = 1e-5
MAGIC = 12582912.0

EA_W = (3 * D + 2) // 2
M_SRC, M_DST, M_W, M_KEY = 0, 1, 2, 5
STEP = 8192
META = 6
ROW = EA_W + META + D
PAD_ROWS = 256
N_ROWS = N_EDGES + PAD_ROWS

WIN = 256
NW = NT + 1
RING = NW // 2
HALF = 16
KW = 640
CHUNK, SUB = 11, 3
HB = 3


def layer_norm_relu(nc, dve, link, act_sqrt_ready, act_sqrt_done, n_before, x, h, centred, stat, std):
    link(nc.vector.tensor_reduce(stat[:], x[:], AX.X, ALU.add))
    link(nc.vector.tensor_scalar(stat[:], stat[:], 1.0 / D, None, ALU.mult))
    link(nc.vector.tensor_tensor(centred[:], x[:], stat[:].unsqueeze(2).to_broadcast([NP, NT, D]), ALU.subtract))
    link(nc.vector.tensor_tensor(h[:], centred[:], centred[:], ALU.mult))
    link(nc.vector.tensor_reduce(stat[:], h[:], AX.X, ALU.add))
    nc.vector.tensor_scalar(stat[:], stat[:], 1.0 / D, EPS, ALU.mult, ALU.add).then_inc(act_sqrt_ready, 1)
    dve.wait_ge(act_sqrt_done, n_before + 1)
    link(nc.vector.reciprocal(std[:], std[:]))
    link(nc.vector.tensor_tensor(centred[:], centred[:], std[:].unsqueeze(2).to_broadcast([NP, NT, D]), ALU.mult))
    link(nc.vector.tensor_scalar(h[:], centred[:], 0.0, None, ALU.max))


def split3(nc, link, whole, hi, mid, lo, rest):
    link(nc.vector.tensor_copy(hi, whole))
    link(nc.vector.tensor_tensor(rest, whole, hi, ALU.subtract))
    link(nc.vector.tensor_copy(mid, rest))
    link(nc.vector.tensor_tensor(lo, rest, mid, ALU.subtract))


def linker(engine, sem):
    count = [0]

    def link(ins):
        count[0] += 1
        ins.then_inc(sem, 1)
        engine.wait_ge(sem, count[0])

    return link


def build(nc, x_in, src_in, dst_in, ea_in, ew_in, gW, gb, W1, b1, W2, b2, W1a, b1a, W1b, b1b, W2a, b2a, W2b, b2b,
          c_ident, c_node, c_key, c_step, c_tri, c_hmask, c_hfold, out):
    ctx = ExitStack()
    with ctx:
        def sb(name, shape, dt=F32):
            return ctx.enter_context(nc.sbuf_tensor(name, shape, dt))

        def dram(name, shape, dt):
            return nc.dram_tensor(name, shape, dt, kind="Internal").ap()

        rows = dram("sorted_rows", [N_ROWS, ROW], I32)
        tab = dram("window_starts_by_src", [NT, 32], I32)
        tab_t = dram("window_starts_by_dst", [NT, 32], I32)

        ident = sb("ident", [128, 128])
        node_iota = sb("node_iota", [128, NT, 128], F16)
        tile_steps = sb("tile_steps", [128, NT])
        tri = sb("tri", [NP, NP])
        x = sb("x", [NP, NT, D])
        h = sb("h", [NP, NT, D])
        centred = sb("centred", [NP, NT, D])
        stat = sb("stat", [NP, NT])
        std = sb("std", [NP, NT])
        rounds_i = sb("rounds", [1, 1], I32)
        wa_bot2 = sb("w1a_bot_twice", [128, 128])
        b1a_bc = sb("b1a_on_all", [EP, D])

        w = {"gW": sb("gW", [D, D]), "W1": sb("W1", [2 * D, 128]), "W2": sb("W2", [128, D]), "W1a": sb("W1a_top", [D, D]),
             "W1b": sb("W1b_and_b1b", [D + 1, D]), "W2a_top": sb("W2a_top", [D, D]), "W2a_bot": sb("W2a_bot", [D, D]),
             "W2b": sb("W2b", [D, D]), "b1": sb("b1", [128, 1]), "b2a": sb("b2a", [D, 1]),
             "gb": sb("gb_on_all", [NP, D]), "b2": sb("b2_on_all", [NP, D]), "b2b": sb("b2b_on_all", [NP, D])}
        weights_in = ctx.enter_context(nc.semaphore("weights_in"))
        passed = ctx.enter_context(nc.semaphore("passed"))
        consts_in = ctx.enter_context(nc.semaphore("consts_in"))

        g = dict(locals())
        prep(nc, g)
        g["agg_t"] = sb("agg_t", [D, NT, 128])
        g["agg_e"] = sb("agg_e", [NP, NT, D])
        g["agg_1"] = sb("agg_1", [NP, NT, D])
        g["cnt_src"] = sb("cnt_src", [NP, NT])
        g["cnt_dst"] = sb("cnt_dst", [NP, NT])
        g["hs"] = sb("h_parts", [NP, NT, 3 * D + 1], BF16)
        rounds = nc.values_load(rounds_i[0:1, 0:1], min_val=1, max_val=-(-N_EDGES // WIN))
        pass_by_src(nc, g, rounds)
        after_l0(nc, g)
        pass_by_dst(nc, g, rounds)
        after_l1(nc, g)
        pass_messages(nc, g, rounds)
        finish(nc, g)


def prep(nc, g):
    tri, ident, node_iota, x, h = g["tri"], g["ident"], g["node_iota"], g["x"], g["h"]
    with ExitStack() as ctx:
        def sb(name, shape, dt=F32):
            return ctx.enter_context(nc.sbuf_tensor(name, shape, dt))

        def sem(name):
            return ctx.enter_context(nc.semaphore(name))

        meta = sb("meta", [EP, ET, META])
        pos_i = sb("pos_i", [EP, ET], I32)

        with ExitStack() as c1:
            def sb1(name, shape, dt=F32):
                return c1.enter_context(nc.sbuf_tensor(name, shape, dt))

            def ps1(name, shape, dt=F32):
                return c1.enter_context(nc.psum_tensor(name, shape, dt))

            def sem1(name):
                return c1.enter_context(nc.semaphore(name))

            src_i, dst_i, nxt_i = (sb1(n, [EP, ET], I32) for n in ("src_i", "dst_i", "nxt_i"))
            ew = sb1("ew", [EP, ET])
            q_f, p_f, tmp = sb1("q_f", [EP, ET]), sb1("p_f", [EP, ET]), sb1("tmp", [EP, ET])
            q16, p16, key16 = sb1("q16", [EP, ET], F16), sb1("p16", [EP, ET], F16), sb1("key16", [EP, ET], F16)
            wpart = sb1("wpart", [EP, ET], BF16)
            mask = sb1("mask", [EP, ET], BF16)
            ones_w = sb1("ones_w", [EP, ET], BF16)
            scan = sb1("scan", [EP, ET])
            keys = sb1("keys", [EP, KW])
            tot, col, incl, off = (sb1(n, [EP, KW]) for n in ("tot", "col", "incl", "off"))
            oh_q, oh_p = sb1("oh_q", [EP, NT, ET], BF16), sb1("oh_p", [EP, NT, ET], BF16)
            ones_m = sb1("ones_m", [EP, EP])
            viol, flag, mul, nkeys_f = (sb1(n, [EP, 1]) for n in ("viol", "flag", "mul", "nkeys_f"))
            nkeys_i = sb1("nkeys_i", [1, 1], I32)
            hmask, hfold = sb1("hmask", [NT * HB, NT * HB]), sb1("hfold", [NT * HB, NT])
            h75 = sb1("h75", [NT * HB, NT * HB])
            cnt, start, half = sb1("cnt", [NT, NT]), sb1("start", [NT, NT]), sb1("half", [NT, NT])
            row, base, diag = sb1("row", [NT, 1]), sb1("base", [NT, 1]), sb1("diag", [NT, 1])
            r_row, r_max = sb1("r_row", [1, NT]), sb1("r_max", [1, 1])
            tab_i, tab_ti = sb1("tab_i", [NT, 32], I32), sb1("tab_ti", [NT, 32], I32)

            ps_excl = ps1("ps_excl", [EP, 2, 512])
            ps_col = ps1("ps_col", [EP, 2, 512])
            ps_hist = ps1("ps_hist", [NT * HB, NT * HB])
            ps_small = ps1("ps_small", [EP, 512])

            ints_in, next_in, ew_in, tables_out = (sem1(n) for n in ("ints_in", "next_in", "ew_in", "tables_out"))
            next_pad, exp_done, flag_in, flag_sum, tot_ready, off_ready, onehots, hist_done = (sem1(n) for n in (
                "next_pad", "exp_done", "flag_in", "flag_sum", "tot_ready", "off_ready", "onehots", "hist_done"))
            h75_ready, folded, row_ready, base_ready, start_ready, starts_t, rmax_ready, rmax_t, tabs_ready = (
                sem1(n) for n in ("h75_ready", "folded", "row_ready", "base_ready", "start_ready", "starts_t",
                                  "rmax_ready", "rmax_t", "tabs_ready"))
            dch = sem1("dve_chain_order")
            sqrt_in, sqrt_out = sem1("sqrt_in0"), sem1("sqrt_out0")
            hoh = sem1("histogram_onehot")
            kcount = sem1("key_counted")
            counts = {}

            with nc.Block() as block:
                @block.sync
                def _(sp):
                    sp.dma_start(src_i[:], g["src_in"].rearrange("(i t) -> i t", t=ET)).then_inc(ints_in, 16)
                    sp.dma_start(dst_i[:], g["dst_in"].rearrange("(i t) -> i t", t=ET)).then_inc(ints_in, 16)
                    sp.wait_ge(next_pad, 1)
                    body = (EP - 1) * ET
                    sp.dma_start(nxt_i[0:EP - 1, :], g["dst_in"][1:1 + body].rearrange("(i t) -> i t", t=ET)).then_inc(next_in, 16)
                    sp.dma_start(nxt_i[EP - 1:EP, 0:ET - 1], g["dst_in"][1 + body:N_EDGES].unsqueeze(0)).then_inc(next_in, 16)
                    sp.dma_start(ew[:], g["ew_in"].rearrange("(i t) -> i t", t=ET)).then_inc(ew_in, 16)
                    for to, of in ((ident[:], g["c_ident"]), (tri[:], g["c_tri"]), (hmask[:], g["c_hmask"]),
                                   (hfold[:], g["c_hfold"]), (keys[:], g["c_key"].to_broadcast([EP, KW])),
                                   (node_iota[:], g["c_node"].rearrange("o (k j) -> o k j", k=NT).to_broadcast([128, NT, 128])),
                                   (g["tile_steps"][:], g["c_step"].to_broadcast([128, NT])),
                                   (x[:], g["x_in"].rearrange("(k i) d -> i k d", i=NP)),
                                   (g["b1a_bc"][:], g["b1a"].unsqueeze(0).to_broadcast([EP, D]))):
                        sp.dma_start(to, of).then_inc(g["consts_in"], 16)
                    w = g["w"]
                    on_all = lambda b: b.unsqueeze(0).to_broadcast([NP, D])
                    for to, of in ((w["gW"][:], g["gW"]), (w["W1"][:], g["W1"]), (w["W2"][:], g["W2"]),
                                   (w["W1a"][:], g["W1a"][0:D, :]), (w["W1b"][0:D, :], g["W1b"]),
                                   (w["W1b"][D:D + 1, :], g["b1b"].unsqueeze(0)), (w["W2a_top"][:], g["W2a"][0:D, :]),
                                   (w["W2a_bot"][:], g["W2a"][D:2 * D, :]), (w["W2b"][:], g["W2b"]),
                                   (w["b1"][:], g["b1"].unsqueeze(1)), (w["b2a"][:], g["b2a"].unsqueeze(1)),
                                   (w["gb"][:], on_all(g["gb"])), (w["b2"][:], on_all(g["b2"])),
                                   (w["b2b"][:], on_all(g["b2b"]))):
                        sp.dma_start(to, of).then_inc(g["weights_in"], 16)
                    sp.wait_ge(tabs_ready, 1)
                    sp.dma_start(g["tab"], tab_i[:]).then_inc(tables_out, 16)
                    sp.dma_start(g["tab_t"], tab_ti[:]).then_inc(tables_out, 16)
                    sp.wait_ge(tables_out, 32)
                    sp.wait_ge(g["weights_in"], 16 * 14)

                @block.scalar
                def _(act):
                    act.wait_ge(ew_in, 16)
                    nc.scalar.activation(ew[:], ew[:], ACT.Exp, scale=-1.0).then_inc(exp_done, 1)
                    act.wait_ge(sqrt_in, 1)
                    nc.scalar.activation(g["std"][:], g["stat"][:], ACT.Sqrt).then_inc(sqrt_out, 1)

                @block.vector
                def _(dve):
                    link = linker(dve, dch)
                    nc.vector.memset(nxt_i[:, ET - 1:ET], N_NODES - 1).then_inc(next_pad, 1)
                    nc.vector.memset(ones_m[:], 1.0)
                    nc.vector.memset(ones_w[:], 1.0)
                    nc.vector.memset(tab_i[:], 0)
                    nc.vector.memset(tab_ti[:], 0)
                    link(nc.vector.memset(tot[:], 0.0))
                    dve.wait_ge(ints_in, 32)

                    def tile_of(tile_f, node_i, centre_to=None):
                        link(nc.vector.tensor_copy(tmp[:], node_i[:]))
                        if centre_to is not None:
                            nc.vector.tensor_scalar(centre_to, tmp[:], -float(CENTRE), None, ALU.add)
                        link(nc.vector.tensor_scalar(tile_f[:], tmp[:], -float(NP // 2), 1.0 / NP, ALU.add, ALU.mult))
                        link(nc.vector.tensor_scalar(tile_f[:], tile_f[:], MAGIC, None, ALU.add))
                        link(nc.vector.tensor_scalar(tile_f[:], tile_f[:], -MAGIC, None, ALU.add))

                    tile_of(q_f, src_i, meta[:, :, M_SRC])
                    tile_of(p_f, dst_i, meta[:, :, M_DST])
                    dve.wait_ge(next_in, 32)
                    tile_of(scan, nxt_i)
                    link(nc.vector.tensor_tensor(tmp[:], p_f[:], scan[:], ALU.is_gt))
                    nc.vector.tensor_reduce(viol[:], tmp[:], AX.X, ALU.max).then_inc(flag_in, 1)
                    nc.vector.tensor_copy(q16[:], q_f[:])
                    nc.vector.scalar_tensor_tensor(meta[:, :, M_KEY], p_f[:], float(STEP), meta[:, :, M_SRC], ALU.mult, ALU.add)
                    link(nc.vector.tensor_copy(p16[:], p_f[:]))
                    dve.wait_ge(g["consts_in"], 16 * 9)
                    with dve.Fori(0, NT) as k:
                        nc.vector.tensor_scalar(oh_q[:, bass.ds(k, 1), :].rearrange("p o t -> p (o t)"), q16[:],
                                                keys[:, bass.ds(k, 1)], None, ALU.is_equal)
                        nc.vector.tensor_scalar(oh_p[:, bass.ds(k, 1), :].rearrange("p o t -> p (o t)"), p16[:],
                                                keys[:, bass.ds(k, 1)], None, ALU.is_equal).then_inc(hoh, 1)
                    dve.wait_ge(flag_sum, 1)
                    link(nc.vector.tensor_scalar(flag[:], ps_small[:, 0:1], 1.0, None, ALU.min))
                    nc.vector.tensor_scalar(nkeys_f[:], flag[:], float(NT * NT - NT), float(NT), ALU.mult, ALU.add)
                    link(nc.vector.tensor_scalar(mul[:], flag[:], float(NT - 1), 1.0, ALU.mult, ALU.add))
                    link(nc.vector.tensor_copy(nkeys_i[:], nkeys_f[0:1, :]))
                    link(nc.vector.tensor_scalar(tmp[:], p_f[:], flag[:], None, ALU.mult))
                    link(nc.vector.tensor_scalar(scan[:], q_f[:], mul[:], None, ALU.mult))
                    link(nc.vector.tensor_tensor(key16[:], tmp[:], scan[:], ALU.add))
                    n_keys = dve.value_load(nkeys_i[0:1, 0:1], min_val=NT, max_val=NT * NT)
                    with dve.Fori(0, n_keys) as k:
                        nc.vector.tensor_scalar(mask[:], key16[:], keys[:, bass.ds(k, 1)], 0.0, ALU.is_equal, ALU.add,
                                                accum_out=tot[:, bass.ds(k, 1)]).then_inc(kcount, 1)
                        dve.wait_ge(kcount, k + 1)
                    dve.sem_inc(tot_ready, 1)
                    dve.wait_ge(off_ready, 1)
                    for c in range(2):
                        link(nc.vector.tensor_copy(col[:, c * 320:c * 320 + 320], ps_col[:, c, 0:320]))
                    link(nc.vector.tensor_tensor_scan(incl[:], ones_w[:, 0:KW], col[:], 0.0, ALU.mult, ALU.add))
                    link(nc.vector.tensor_tensor(incl[:], incl[:], col[:], ALU.subtract))
                    for c in range(2):
                        sl = slice(c * 320, c * 320 + 320)
                        link(nc.vector.scalar_tensor_tensor(off[:, sl], incl[:, sl], -1.0, ps_excl[:, c, 0:320],
                                                            ALU.add, ALU.add))
                    with dve.Fori(0, n_keys) as k:
                        nc.vector.tensor_scalar(mask[:], key16[:], keys[:, bass.ds(k, 1)], None,
                                                ALU.is_equal).then_inc(kcount, 1)
                        dve.wait_ge(kcount, n_keys + k * 3 + 1)
                        nc.vector.tensor_tensor_scan(scan[:], ones_w[:], mask[:], off[:, bass.ds(k, 1)],
                                                     ALU.mult, ALU.add).then_inc(kcount, 1)
                        dve.wait_ge(kcount, n_keys + k * 3 + 2)
                        alone(dve, g)
                        nc.vector.copy_predicated(tmp[:], mask[:].bitcast(U16), scan[:]).then_inc(kcount, 1)
                        dve.wait_ge(kcount, n_keys + k * 3 + 3)
                    link(nc.vector.tensor_copy(pos_i[:], tmp[:]))
                    dve.wait_ge(exp_done, 1)
                    link(nc.vector.tensor_copy(wpart[:], ew[:]))
                    nc.vector.tensor_copy(meta[:, :, M_W], wpart[:])
                    link(nc.vector.tensor_tensor(tmp[:], ew[:], wpart[:], ALU.subtract))
                    link(nc.vector.tensor_copy(wpart[:], tmp[:]))
                    nc.vector.tensor_copy(meta[:, :, M_W + 1], wpart[:])
                    link(nc.vector.tensor_tensor(meta[:, :, M_W + 2], tmp[:], wpart[:], ALU.subtract))
                    dve.wait_ge(hist_done, 1)
                    nc.vector.tensor_tensor(h75[:], ps_hist[:], hmask[:], ALU.mult).then_inc(h75_ready, 1)
                    dve.wait_ge(folded, 1)
                    link(nc.vector.tensor_reduce(cnt[:], ps_small[0:NT, 128:128 + NT * HB].rearrange("q (p b) -> q p b", b=HB),
                                                 AX.X, ALU.add))
                    nc.vector.tensor_reduce(row[:], cnt[:], AX.X, ALU.add).then_inc(row_ready, 1)
                    dve.wait_ge(base_ready, 1)
                    link(nc.vector.tensor_copy(base[:], ps_small[0:NT, 256:257]))
                    link(nc.vector.tensor_tensor_scan(start[:], ones_w[0:NT, 0:NT], cnt[:], base[:], ALU.mult, ALU.add))
                    link(nc.vector.tensor_tensor(start[:], start[:], cnt[:], ALU.subtract))
                    link(nc.vector.tensor_tensor(half[:], start[:], ident[0:NT, 0:NT], ALU.mult))
                    link(nc.vector.tensor_reduce(diag[:], half[:], AX.X, ALU.add))
                    last = HALF + NW - 1 - RING
                    nc.vector.tensor_scalar(tab_i[:, last:last + 1], diag[:], float(WIN), None, ALU.add)
                    nc.vector.tensor_scalar(tab_ti[:, last:last + 1], diag[:], float(WIN), None, ALU.add)
                    nc.vector.tensor_copy(tab_i[:, 0:RING], start[:, 0:RING])
                    nc.vector.tensor_copy(tab_i[:, HALF:HALF + NT - RING], start[:, RING:NT]).then_inc(start_ready, 1)
                    link(nc.vector.tensor_scalar(half[:], ident[0:NT, 0:NT], -0.5, 1.0, ALU.mult, ALU.add))
                    link(nc.vector.tensor_tensor(half[:], half[:], cnt[:], ALU.mult))
                    nc.vector.tensor_reduce(row[:], half[:], AX.X, ALU.max).then_inc(rmax_ready, 1)
                    dve.wait_ge(starts_t, 1)
                    nc.vector.tensor_copy(tab_ti[:, 0:RING], ps_small[0:NT, 320:320 + RING])
                    nc.vector.tensor_copy(tab_ti[:, HALF:HALF + NT - RING], ps_small[0:NT, 320 + RING:320 + NT]).then_inc(tabs_ready, 1)
                    dve.wait_ge(rmax_t, 1)
                    link(nc.vector.tensor_reduce(r_max[:], ps_small[0:1, 384:384 + NT], AX.X, ALU.max))
                    link(nc.vector.tensor_scalar(r_max[:], r_max[:], WIN / 2 - 0.25, 1.0 / WIN, ALU.add, ALU.mult))
                    link(nc.vector.tensor_scalar(r_max[:], r_max[:], MAGIC, None, ALU.add))
                    link(nc.vector.tensor_scalar(r_max[:], r_max[:], -MAGIC, 1.0, ALU.add, ALU.max))
                    link(nc.vector.tensor_copy(g["rounds_i"][:], r_max[:]))
                    layer_norm_relu(nc, dve, link, sqrt_in, sqrt_out, 0, x, h, g["centred"], g["stat"], g["std"])

                @block.tensor
                def _(pe):
                    pe.wait_ge(flag_in, 1)
                    nc.tensor.matmul(ps_small[:, 0:1], ones_m[:], viol[:], start=True, stop=True).then_inc(flag_sum, 1)

                    def pairs(t, first, last):
                        one_q, one_p = (o[:].rearrange("i k (b t) -> i (k b) t", b=HB)[:, :, bass.ds(t, 1)]
                                        .rearrange("i m o -> i (m o)") for o in (oh_q, oh_p))
                        return nc.tensor.matmul(ps_hist[:], one_q, one_p, start=first, stop=last)

                    pe.wait_ge(hoh, NT)
                    per = ET // HB // NT
                    for j in range(per):
                        pairs(j, j == 0, False)
                    with pe.Fori(1, NT - 1) as i:
                        for j in range(per):
                            pairs(i * per + j, False, False)
                    for j in range(per):
                        hist = pairs((NT - 1) * per + j, False, j == per - 1)
                    hist.then_inc(hist_done, 1)
                    pe.wait_ge(tot_ready, 1)
                    for c in range(2):
                        nc.tensor.matmul(ps_excl[:, c, 0:320], tri[:], tot[:, c * 320:c * 320 + 320], start=True, stop=True)
                        last = nc.tensor.matmul(ps_col[:, c, 0:320], ones_m[:], tot[:, c * 320:c * 320 + 320], start=True, stop=True)
                    last.then_inc(off_ready, 1)
                    pe.wait_ge(h75_ready, 1)
                    nc.tensor.matmul(ps_small[0:NT, 128:128 + NT * HB], hfold[:], h75[:], start=True, stop=True).then_inc(folded, 1)
                    pe.wait_ge(row_ready, 1)
                    nc.tensor.matmul(ps_small[0:NT, 256:257], tri[0:NT, 0:NT], row[:], start=True, stop=True).then_inc(base_ready, 1)
                    pe.wait_ge(start_ready, 1)
                    nc.tensor.transpose(ps_small[0:NT, 320:320 + NT], start[:], ident[0:NT, 0:NT]).then_inc(starts_t, 1)
                    pe.wait_ge(rmax_ready, 1)
                    pe.wait_ge(tabs_ready, 1)
                    nc.tensor.transpose(ps_small[0:1, 384:384 + NT], row[:], ident[0:NT, 0:NT]).then_inc(rmax_t, 1)

        with ExitStack() as c2:
            def sb2(name, shape, dt=F32):
                return c2.enter_context(nc.sbuf_tensor(name, shape, dt))

            def sem2(name):
                return c2.enter_context(nc.semaphore(name))

            ea = [sb2(f"ea{j}", [EP, CHUNK, D]) for j in range(SUB)]
            rowbuf = [sb2(f"rowbuf{j}", [EP, CHUNK, ROW], I32) for j in range(SUB)]
            rest = sb2("rest", [EP, CHUNK, D])
            posbuf = [sb2(f"posbuf{j}", [EP, CHUNK], I32) for j in range(SUB)]
            pad = sb2("pad", [128, 2, ROW], I32)
            pairs_n = (CHUNK + 1) // 2
            ea_t = sb2("ea_t", [128, pairs_n, 128])
            ps_t = c2.enter_context(nc.psum_tensor("ps_t", [128, 8, 128], F32))
            ps_q = c2.enter_context(nc.psum_tensor("ps_q", [EP, 8, 128], F32))
            ea_in = [sem2(f"ea_in{j}") for j in range(SUB)]
            moved = [sem2(f"moved{j}") for j in range(SUB)]
            w_in, pad_ready, pad_out, w_zero, tposed, tcopied, q_done, hi_done, row_done, chain, rowpad = (sem2(n) for n in (
                "w_in", "pad_ready", "pad_out", "w_zero", "tposed", "tcopied", "q_done", "hi_done", "row_done", "mv_chain", "rowpad"))
            ea_v = g["ea_in"].rearrange("(i t) d -> i t d", t=ET)
            wa2 = g["wa_bot2"]

            def parts(j, a):
                return rowbuf[j][:].bitcast(BF16)[:, :, a * D:(a + 1) * D]

            with nc.Block() as block:
                @block.sync
                def _(sp):
                    sp.wait_ge(w_zero, 1)
                    sp.dma_start(wa2[0:D, 0:D], g["W1a"][D:2 * D, :]).then_inc(w_in, 16)
                    sp.dma_start(wa2[D:128, D:128], g["W1a"][D:2 * D, :]).then_inc(w_in, 16)
                    with sp.Fori(0, ET // (CHUNK * SUB)) as it:
                        for j in range(SUB):
                            sp.wait_ge(row_done, it * SUB + 1)
                            sp.dma_start(ea[j][:], ea_v[:, bass.ds(it * SUB * CHUNK + j * CHUNK, CHUNK), :]).then_inc(ea_in[j], 16)
                    sp.wait_ge(pad_ready, 1)
                    sp.dma_start(g["rows"][N_EDGES:N_ROWS, :].rearrange("(i j) w -> i j w", j=2), pad[:]).then_inc(pad_out, 16)
                    sp.wait_ge(pad_out, 16)

                @block.scalar
                def _(act):
                    act.sem_inc(tcopied, 1)

                    def step(it, again):
                        for j in range(SUB):
                            n = it * SUB + j
                            act.wait_ge(ea_in[j], it * 16 + 16)
                            if again:
                                act.wait_ge(moved[j], it * 16 * CHUNK)
                            nc.scalar.activation(parts(j, 0), ea[j][:], ACT.Copy).then_inc(hi_done, 1)
                            act.wait_ge(tposed, n + 1)
                            act.wait_ge(q_done, n + 1)
                            nc.scalar.activation(ea_t[:, 0:pairs_n - 1, 0:EP], ps_t[:, 0:pairs_n - 1, 0:EP], ACT.Copy)
                            nc.scalar.activation(ea_t[0:D, pairs_n - 1, 0:EP], ps_t[0:D, pairs_n - 1, 0:EP], ACT.Copy).then_inc(tcopied, 1)

                    step(0, False)
                    with act.Fori(1, ET // (CHUNK * SUB)) as it:
                        step(it, True)

                @block.vector
                def _(dve):
                    dve.sem_inc(row_done, 1)
                    nc.vector.memset(wa2[:], 0.0).then_inc(w_zero, 1)
                    for j in range(SUB):
                        nc.vector.memset(rowbuf[j][:].bitcast(BF16)[:, :, 3 * D:3 * D + 1], 1.0)
                        nc.vector.memset(rowbuf[j][:].bitcast(BF16)[:, :, 3 * D + 1:3 * D + 2], 0.0)
                    nc.vector.memset(pad[:], 0).then_inc(chain, 1)
                    dve.wait_ge(chain, 1)
                    nc.vector.memset(pad[:].bitcast(F32)[:, :, EA_W:EA_W + META], -float(N_NODES)).then_inc(pad_ready, 1)
                    with dve.Fori(0, ET // (CHUNK * SUB)) as it:
                        for j in range(SUB):
                            n = it * SUB + j
                            tile0 = it * SUB * CHUNK + j * CHUNK
                            dve.wait_ge(hi_done, n + 1)
                            nc.vector.tensor_tensor(rest[:], ea[j][:], parts(j, 0), ALU.subtract).then_inc(chain, 1)
                            dve.wait_ge(chain, n * 3 + 2)
                            nc.vector.tensor_copy(parts(j, 1), rest[:]).then_inc(chain, 1)
                            dve.wait_ge(chain, n * 3 + 3)
                            nc.vector.tensor_tensor(parts(j, 2), rest[:], parts(j, 1), ALU.subtract).then_inc(chain, 1)
                            dve.wait_ge(chain, n * 3 + 4)
                            nc.vector.tensor_copy(rowbuf[j][:].bitcast(F32)[:, :, EA_W:EA_W + META],
                                                  meta[:, bass.ds(tile0, CHUNK), :])
                            nc.vector.tensor_copy(posbuf[j][:], pos_i[:, bass.ds(tile0, CHUNK)])
                            dve.wait_ge(q_done, n + 2)
                            nc.vector.tensor_tensor(
                                rowbuf[j][:].bitcast(F32)[:, :, EA_W + META:ROW],
                                ps_q[:].rearrange("p a (b d) -> p (a b) d", d=D)[:, 0:CHUNK, :],
                                g["b1a_bc"][:].unsqueeze(1).to_broadcast([EP, CHUNK, D]), ALU.add).then_inc(row_done, 1)

                @block.tensor
                def _(pe):
                    pe.sem_inc(q_done, 1)
                    pe.wait_ge(w_in, 32)
                    with pe.Fori(0, ET // (CHUNK * SUB)) as it:
                        for j in range(SUB):
                            n = it * SUB + j
                            pe.wait_ge(ea_in[j], it * 16 + 16)
                            pe.wait_ge(tcopied, n + 1)
                            flat = ea[j][:].rearrange("p t d -> p (t d)")
                            for a in range(pairs_n):
                                w = min(2, CHUNK - 2 * a) * D
                                last = nc.tensor.transpose(ps_t[0:w, a, 0:EP], flat[:, a * 128:a * 128 + w], ident[0:EP, 0:EP])
                            last.then_inc(tposed, 1)
                            pe.wait_ge(tcopied, n + 2)
                            pe.wait_ge(row_done, n + 1)
                            for a in range(pairs_n):
                                w = min(2, CHUNK - 2 * a) * D
                                last = nc.tensor.matmul(ps_q[:, a, 0:w], ea_t[0:w, a, 0:EP], wa2[0:w, 0:w], start=True, stop=True)
                            last.then_inc(q_done, 1)

                @block.gpsimd
                def _(pool):
                    with pool.Fori(0, ET // (CHUNK * SUB)) as it:
                        for j in range(SUB):
                            pool.wait_ge(row_done, it * SUB + j + 2)
                            alone(pool, g)
                            for t in range(CHUNK):
                                nc.gpsimd.indirect_dma_start(
                                    g["rows"], bass.IndirectOffsetOnAxis(ap=posbuf[j][:, t:t + 1], axis=0),
                                    rowbuf[j][:, t, :], None).then_inc(moved[j], 16)
                    for j in range(SUB):
                        pool.wait_ge(moved[j], 16 * CHUNK * (ET // (CHUNK * SUB)))



def clear(nc, sems):
    for s in sems:
        nc.sync.sem_clear(s)
    nc.all_engine_barrier()


def load_windows(sp, g, table, rnd, window, filled, freed, w0, w1):
    sp.sem_inc(freed, RING)
    with ExitStack() as ctx:
        starts = [ctx.enter_context(sp.register(f"start{w}_{w0}_{w1}")) for w in range(RING)]
        with sp.Fori(0, NT) as q:
            for half in range(2):
                sp.reg_load(starts, table[bass.ds(q, 1), half * HALF:half * HALF + RING])
                for slot in range(RING):
                    reg = starts[slot]
                    at = sp.snap(reg, min_val=0, max_val=N_EDGES + WIN)
                    sp.reg_alu(reg, at + rnd * WIN, N_EDGES, ALU.min)
                    at = sp.snap(reg, min_val=0, max_val=N_EDGES)
                    sp.wait_ge(freed, q * NW + half * RING + slot + 1)
                    sp.dma_start(window[:, slot, :, :],
                                 g["rows"][bass.ds(at, WIN), w0:w1].rearrange("(i j) e -> i j e", j=2)
                                 ).then_inc(filled[slot], 16)


def lagged(engine, now, later, lag):
    def outer(q, first):
        for w in range(NW):
            now(q, w)
            if w >= lag:
                later(q, w - lag)
            elif not first:
                later(q - 1, NW + w - lag)

    outer(0, True)
    with engine.Fori(1, NT) as q:
        outer(q, False)
    for w in range(NW - lag, NW):
        later(NT - 1, w)


def inner_tile(q, w):
    return w if w < NT else q


def at(tile, i, n=NP):
    return tile[:, bass.ds(i, 1), 0:n].rearrange("p o c -> p (o c)")


def alone(engine, g):
    engine.sem_inc(g["passed"], 1)


def step_of(g, q, w):
    return float(STEP * w) if w < NT else g["tile_steps"][:, bass.ds(q, 1)]


def pass_by_src(nc, g, rnd_count):
    h, agg_t, agg_e, cnt = g["h"], g["agg_t"], g["agg_e"], g["cnt_src"]
    iota = g["node_iota"]
    W0, W1 = 0, EA_W + META
    with ExitStack() as ctx:
        def sb(name, shape, dt=F32):
            return ctx.enter_context(nc.sbuf_tensor(name, shape, dt))

        def sem(name):
            return ctx.enter_context(nc.semaphore(name))

        window = sb("window0", [128, RING, 2, W1 - W0], I32)
        by_src = sb("by_src0", [128, RING, 2, 128], BF16)
        by_dst = sb("by_dst0", [128, RING, 2, 3, 128], BF16)
        mat = sb("mat0", [NP, 2, 128])
        staged_t, staged_e = sb("staged_t0", [D, NP]), sb("staged_e0", [NP, 3 * D + 1])
        h_diag = sb("h_diag", [NP, D])
        ps_mat = [ctx.enter_context(nc.psum_tensor(f"ps_mat{i}", [NP, 512], F32)) for i in range(2)]
        ps_t = ctx.enter_context(nc.psum_tensor("ps_agg_t", [D, 512], F32))
        ps_e = ctx.enter_context(nc.psum_tensor("ps_agg_e", [NP, 512], F32))
        filled = [sem(f"filled0_{i}") for i in range(RING)]
        freed, hots, built, copied, staged, added, pchain, diag_in = (sem(n) for n in (
            "freed0", "onehots0", "built0", "copied0", "staged0", "added0", "pool_chain0", "diag_in0"))

        with nc.Block() as block:
            @block.gpsimd
            def _(pool):
                nc.gpsimd.memset(agg_t[:], 0.0)
                nc.gpsimd.memset(agg_e[:], 0.0)
                nc.gpsimd.memset(cnt[:], 0.0)

        with nc.Fori(0, rnd_count) as rnd:
            with nc.Block() as block:
                @block.sync
                def _(sp):
                    load_windows(sp, g, g["tab"], rnd, window, filled, freed, W0, W1)

                @block.vector
                def _(dve):
                    with dve.Fori(0, NT) as q:
                        for w in range(NW):
                            slot = w % RING
                            dve.wait_ge(filled[slot], q * 32 + (w // RING) * 16 + 16)
                            dve.wait_ge(freed, q * NW + w + 1)
                            meta = window[:, slot].bitcast(F32)[:, :, EA_W:EA_W + META]
                            for j in range(2):
                                nc.vector.tensor_scalar(by_src[:, slot, j, :], at(iota, q, 128),
                                                        step_of(g, q, w), meta[:, j, M_KEY:M_KEY + 1],
                                                        ALU.add, ALU.is_equal)
                                for a in range(3):
                                    last = nc.vector.tensor_scalar(
                                        by_dst[:, slot, j, a, :], at(iota, inner_tile(q, w), 128),
                                        meta[:, j, M_DST:M_DST + 1], meta[:, j, M_W + a:M_W + a + 1],
                                        ALU.is_equal, ALU.mult)
                            last.then_inc(hots, 1)

                @block.tensor
                def _(pe):
                    def build_matrix(q, w):
                        slot = w % RING
                        n = q * NW + w
                        pe.wait_ge(hots, n + 1)
                        pe.wait_ge(copied, n + 1)
                        for j in range(2):
                            for a in range(3):
                                last = nc.tensor.matmul(ps_mat[w % 2][:, 0:NP], by_dst[:, slot, j, a, 0:NP],
                                                        by_src[:, slot, j, 0:NP], start=(j == 0 and a == 0),
                                                        stop=(j == 1 and a == 2))
                        last.then_inc(built, 1)

                    def use_matrix(q, w):
                        slot = w % RING
                        n = q * NW + w
                        pe.wait_ge(copied, n + 3)
                        if w == 0:
                            pe.wait_ge(staged, q)
                        first, final = w == 0, w == NW - 1
                        if final:
                            pe.wait_ge(diag_in, q + 1)
                        nc.tensor.matmul(ps_t[:, 0:NP], h_diag[:] if final else h[:, w, :], mat[:, w % 2, 0:NP],
                                         start=first, stop=final)
                        for j in range(2):
                            ends = dict(start=first and j == 0, stop=final and j == 1)
                            last = nc.tensor.matmul(ps_e[:, 0:3 * D + 1], by_src[:, slot, j, 0:NP],
                                                    window[:, slot, j, 0:EA_W].bitcast(BF16)[:, 0:3 * D + 1], **ends)
                        last.then_inc(freed, 1)

                    lagged(pe, build_matrix, use_matrix, 1)

                @block.scalar
                def _(act):
                    act.sem_inc(copied, 2)

                    def copy_matrix(q, w):
                        n = q * NW + w
                        act.wait_ge(built, n + 1)
                        act.wait_ge(freed, n + RING - 1)
                        nc.scalar.activation(mat[:, w % 2, 0:NP], ps_mat[w % 2][:, 0:NP], ACT.Copy).then_inc(copied, 1)

                    def stage(q, w):
                        if w == NW - 1:
                            act.wait_ge(freed, RING + (q + 1) * NW)
                            act.wait_ge(added, q + 1)
                            nc.scalar.activation(staged_t[:], ps_t[:, 0:NP], ACT.Copy)
                            nc.scalar.activation(staged_e[:], ps_e[:, 0:3 * D + 1], ACT.Copy).then_inc(staged, 1)

                    lagged(act, copy_matrix, stage, 1)

                @block.gpsimd
                def _(pool):
                    pool.sem_inc(added, 1)

                    def lay(q, w):
                        if w == NW // 2:
                            pool.wait_ge(staged, q)
                            nc.gpsimd.tensor_copy(h_diag[:], at(h, q, D)).then_inc(diag_in, 1)

                    def add(q, w):
                        if w < NW - 1:
                            return
                        pool.wait_ge(staged, q + 1)
                        alone(pool, g)
                        nc.gpsimd.tensor_tensor(at(agg_t, q), at(agg_t, q), staged_t[:], ALU.add)
                        for a in range(3):
                            nc.gpsimd.tensor_tensor(at(agg_e, q, D), at(agg_e, q, D), staged_e[:, a * D:(a + 1) * D],
                                                    ALU.add).then_inc(pchain, 1)
                            pool.wait_ge(pchain, q * 3 + a + 1)
                            alone(pool, g)
                        nc.gpsimd.tensor_tensor(cnt[:, bass.ds(q, 1)], cnt[:, bass.ds(q, 1)],
                                                staged_e[:, 3 * D:3 * D + 1], ALU.add).then_inc(added, 1)

                    lagged(pool, lay, add, 4)
            clear(nc, filled + [freed, hots, built, copied, staged, added, pchain, diag_in])


def pass_by_dst(nc, g, rnd_count):
    agg, cnt, hs, iota = g["agg_1"], g["cnt_dst"], g["hs"], g["node_iota"]
    W0, W1 = EA_W, EA_W + 2
    with ExitStack() as ctx:
        def sb(name, shape, dt=F32):
            return ctx.enter_context(nc.sbuf_tensor(name, shape, dt))

        def sem(name):
            return ctx.enter_context(nc.semaphore(name))

        window = sb("window1", [128, RING, 2, W1 - W0], I32)
        by_src = sb("by_src1", [128, RING, 2, 128], BF16)
        by_dst = sb("by_dst1", [128, RING, 2, 128], BF16)
        mat = sb("mat1", [NP, 2, 128], BF16)
        staged_e = sb("staged_e1", [NP, 3 * D + 1])
        ps_mat = [ctx.enter_context(nc.psum_tensor(f"ps_cnt_mat{i}", [NP, 512], F32)) for i in range(2)]
        ps_e = ctx.enter_context(nc.psum_tensor("ps_agg_1", [NP, 512], F32))
        filled = [sem(f"filled1_{i}") for i in range(RING)]
        freed, hots, built, copied, staged, added, pchain = (sem(n) for n in (
            "freed1", "onehots1", "built1", "copied1", "staged1", "added1", "pool_chain1"))

        with nc.Block() as block:
            @block.gpsimd
            def _(pool):
                nc.gpsimd.memset(agg[:], 0.0)
                nc.gpsimd.memset(cnt[:], 0.0)

        with nc.Fori(0, rnd_count) as rnd:
            with nc.Block() as block:
                @block.sync
                def _(sp):
                    load_windows(sp, g, g["tab_t"], rnd, window, filled, freed, W0, W1)

                @block.vector
                def _(dve):
                    with dve.Fori(0, NT) as q:
                        for w in range(NW):
                            slot = w % RING
                            dve.wait_ge(filled[slot], q * 32 + (w // RING) * 16 + 16)
                            dve.wait_ge(freed, q * NW + w + 1)
                            meta = window[:, slot].bitcast(F32)
                            for j in range(2):
                                nc.vector.tensor_scalar(by_dst[:, slot, j, :], at(iota, q, 128),
                                                        meta[:, j, M_DST:M_DST + 1], None, ALU.is_equal)
                                last = nc.vector.tensor_scalar(by_src[:, slot, j, :], at(iota, inner_tile(q, w), 128),
                                                               meta[:, j, M_SRC:M_SRC + 1], None, ALU.is_equal)
                            last.then_inc(hots, 1)

                @block.tensor
                def _(pe):
                    def build_matrix(q, w):
                        slot = w % RING
                        n = q * NW + w
                        pe.wait_ge(hots, n + 1)
                        pe.wait_ge(copied, n + 1)
                        for j in range(2):
                            last = nc.tensor.matmul(ps_mat[w % 2][:, 0:NP], by_src[:, slot, j, 0:NP],
                                                    by_dst[:, slot, j, 0:NP], start=j == 0, stop=j == 1)
                        last.then_inc(built, 1)

                    def use_matrix(q, w):
                        pe.wait_ge(copied, q * NW + w + 3)
                        if w == 0:
                            pe.wait_ge(staged, q)
                        nc.tensor.matmul(ps_e[:, 0:3 * D + 1], mat[:, w % 2, 0:NP], at(hs, inner_tile(q, w), 3 * D + 1),
                                         start=w == 0, stop=w == NW - 1).then_inc(freed, 1)

                    lagged(pe, build_matrix, use_matrix, 1)

                @block.scalar
                def _(act):
                    act.sem_inc(copied, 2)

                    def copy_matrix(q, w):
                        n = q * NW + w
                        act.wait_ge(built, n + 1)
                        act.wait_ge(freed, n + RING - 1)
                        nc.scalar.activation(mat[:, w % 2, 0:NP], ps_mat[w % 2][:, 0:NP], ACT.Copy).then_inc(copied, 1)

                    def stage(q, w):
                        if w == NW - 1:
                            act.wait_ge(freed, RING + (q + 1) * NW)
                            act.wait_ge(added, q + 1)
                            nc.scalar.activation(staged_e[:], ps_e[:, 0:3 * D + 1], ACT.Copy).then_inc(staged, 1)

                    lagged(act, copy_matrix, stage, 1)

                @block.gpsimd
                def _(pool):
                    pool.sem_inc(added, 1)
                    with pool.Fori(0, NT) as q:
                        pool.wait_ge(staged, q + 1)
                        alone(pool, g)
                        for a in range(3):
                            nc.gpsimd.tensor_tensor(at(agg, q, D), at(agg, q, D), staged_e[:, a * D:(a + 1) * D],
                                                    ALU.add).then_inc(pchain, 1)
                            pool.wait_ge(pchain, q * 3 + a + 1)
                            alone(pool, g)
                        nc.gpsimd.tensor_tensor(cnt[:, bass.ds(q, 1)], cnt[:, bass.ds(q, 1)],
                                                staged_e[:, 3 * D:3 * D + 1], ALU.add).then_inc(added, 1)
            clear(nc, filled + [freed, hots, built, copied, staged, added, pchain])


def pass_messages(nc, g, rnd_count):
    agg_t, hs, iota = g["agg_t"], g["hs"], g["node_iota"]
    W0, W1 = EA_W, ROW
    with ExitStack() as ctx:
        def sb(name, shape, dt=F32):
            return ctx.enter_context(nc.sbuf_tensor(name, shape, dt))

        def sem(name):
            return ctx.enter_context(nc.semaphore(name))

        window = sb("window3", [128, RING, 2, W1 - W0], I32)
        by_src = sb("by_src3", [128, RING, 2, 128])
        by_dst = sb("by_dst3", [128, RING, 2, 128], BF16)
        turned = sb("turned3", [NP, 2, 2, 128], BF16)
        pre, msg = sb("pre3", [128, 2, 2, D]), sb("msg3", [128, 2, 2, D])
        staged_t = sb("staged_t3", [D, NP])
        ident_b = sb("ident_b", [128, 128], BF16)
        ps_turn = [ctx.enter_context(nc.psum_tensor(f"ps_turn{i}", [NP, 2, 128], BF16)) for i in range(2)]
        ps_p = [ctx.enter_context(nc.psum_tensor(f"ps_p{i}", [128, 2, D], F32)) for i in range(2)]
        ps_t = ctx.enter_context(nc.psum_tensor("ps_msg_t", [D, 512], F32))
        filled = [sem(f"filled3_{i}") for i in range(RING)]
        freed, hots, turned_s, copied, gathered, pre_done, msg_done, staged, added = (sem(n) for n in (
            "freed3", "onehots3", "turned_sem3", "copied3", "gathered3", "pre_done3", "msg_done3", "staged3", "added3"))

        with nc.Block() as block:
            @block.gpsimd
            def _(pool):
                nc.gpsimd.memset(agg_t[:], 0.0)

            @block.vector
            def _(dve):
                nc.vector.tensor_copy(ident_b[:], g["ident"][:])

        with nc.Fori(0, rnd_count) as rnd:
            with nc.Block() as block:
                @block.sync
                def _(sp):
                    load_windows(sp, g, g["tab"], rnd, window, filled, freed, W0, W1)

                @block.vector
                def _(dve):
                    def one_hots(q, w):
                        slot = w % RING
                        dve.wait_ge(filled[slot], q * 32 + (w // RING) * 16 + 16)
                        dve.wait_ge(freed, q * NW + w + 1)
                        meta = window[:, slot].bitcast(F32)
                        for j in range(2):
                            nc.vector.tensor_scalar(by_dst[:, slot, j, :], at(iota, inner_tile(q, w), 128),
                                                    meta[:, j, M_DST:M_DST + 1], None, ALU.is_equal)
                            last = nc.vector.tensor_scalar(by_src[:, slot, j, :], at(iota, q, 128),
                                                           step_of(g, q, w), meta[:, j, M_KEY:M_KEY + 1],
                                                           ALU.add, ALU.is_equal)
                        last.then_inc(hots, 1)

                    def add_q(q, w):
                        n = q * NW + w
                        dve.wait_ge(gathered, n + 3)
                        dve.wait_ge(msg_done, n + 1)
                        nc.vector.tensor_tensor(pre[:, w % 2], ps_p[w % 2][:],
                                                window[:, w % RING].bitcast(F32)[:, :, META:META + D],
                                                ALU.add).then_inc(pre_done, 1)

                    lagged(dve, one_hots, add_q, 3)

                @block.tensor
                def _(pe):
                    def turn(q, w):
                        n = q * NW + w
                        pe.wait_ge(hots, n + 1)
                        pe.wait_ge(copied, n + 1)
                        for j in range(2):
                            last = nc.tensor.transpose(ps_turn[w % 2][:, j, :], by_dst[:, w % RING, j, 0:NP], ident_b[:])
                        last.then_inc(turned_s, 1)

                    def gather(q, w):
                        n = q * NW + w
                        pe.wait_ge(copied, n + 3)
                        pe.wait_ge(pre_done, n + 1)
                        part = at(hs, inner_tile(q, w), 3 * D)
                        for j in range(2):
                            for a in range(3):
                                last = nc.tensor.matmul(ps_p[w % 2][:, j, :], turned[:, w % 2, j, :],
                                                        part[:, a * D:(a + 1) * D], start=a == 0, stop=a == 2)
                        last.then_inc(gathered, 1)

                    def scatter(q, w):
                        n = q * NW + w
                        pe.wait_ge(msg_done, n + 3)
                        if w == 0:
                            pe.wait_ge(staged, q)
                        for j in range(2):
                            last = nc.tensor.matmul(ps_t[:, 0:NP], msg[:, w % 2, j, :], by_src[:, w % RING, j, 0:NP],
                                                    start=w == 0 and j == 0, stop=w == NW - 1 and j == 1)
                        last.then_inc(freed, 1)

                    def outer(q, first):
                        for w in range(NW):
                            turn(q, w)
                            for step, lag in ((gather, 1), (scatter, 3)):
                                if w >= lag:
                                    step(q, w - lag)
                                elif not first:
                                    step(q - 1, NW + w - lag)

                    pe.sem_inc(pre_done, 2)
                    pe.sem_inc(gathered, 2)
                    outer(0, True)
                    with pe.Fori(1, NT) as q:
                        outer(q, False)
                    gather(NT - 1, NW - 1)
                    for w in range(NW - 3, NW):
                        scatter(NT - 1, w)

                @block.scalar
                def _(act):
                    act.sem_inc(copied, 2)
                    act.sem_inc(msg_done, 2)

                    def copy_turned(q, w):
                        n = q * NW + w
                        act.wait_ge(turned_s, n + 1)
                        act.wait_ge(gathered, n + 1)
                        nc.scalar.activation(turned[:, w % 2], ps_turn[w % 2][:], ACT.Copy).then_inc(copied, 1)

                    def relu(q, w):
                        n = q * NW + w
                        act.wait_ge(pre_done, n + 3)
                        act.wait_ge(freed, n + RING - 1)
                        nc.scalar.activation(msg[:, w % 2], pre[:, w % 2], ACT.Relu).then_inc(msg_done, 1)
                        if w == NW - 1:
                            act.wait_ge(freed, RING + (q + 1) * NW)
                            act.wait_ge(added, q + 1)
                            nc.scalar.activation(staged_t[:], ps_t[:, 0:NP], ACT.Copy).then_inc(staged, 1)

                    lagged(act, copy_turned, relu, 2)

                @block.gpsimd
                def _(pool):
                    pool.sem_inc(added, 1)
                    with pool.Fori(0, NT) as q:
                        pool.wait_ge(staged, q + 1)
                        alone(pool, g)
                        nc.gpsimd.tensor_tensor(at(agg_t, q), at(agg_t, q), staged_t[:], ALU.add).then_inc(added, 1)
            clear(nc, filled + [freed, hots, turned_s, copied, gathered, pre_done, msg_done, staged, added])


GROUP = 4


def groups(size):
    return [(i, range(k, min(k + size, NT))) for i, k in enumerate(range(0, NT, size))]


def turn_nodes(nc, g, name, src, width, dst):
    with ExitStack() as ctx:
        ps = [ctx.enter_context(nc.psum_tensor(f"{name}_ps{i}", [width, 512], F32)) for i in range(2)]
        turned, emptied = (ctx.enter_context(nc.semaphore(f"{name}_{n}")) for n in ("turned", "emptied"))
        with nc.Block() as block:
            @block.tensor
            def _(pe):
                for i, tiles in groups(GROUP):
                    if i >= 2:
                        pe.wait_ge(emptied, i - 1)
                    for j, k in enumerate(tiles):
                        last = nc.tensor.transpose(ps[i % 2][:, j * NP:(j + 1) * NP], src[:, k, 0:width],
                                                   g["ident"][0:NP, 0:NP])
                    last.then_inc(turned, 1)

            @block.scalar
            def _(act):
                for i, tiles in groups(GROUP):
                    act.wait_ge(turned, i + 1)
                    n = len(tiles) * NP
                    nc.scalar.activation(dst[0:width, i * GROUP * NP:i * GROUP * NP + n], ps[i % 2][:, 0:n],
                                         ACT.Copy).then_inc(emptied, 1)


def dense(nc, name, terms, m, func, bias, dst):
    with ExitStack() as ctx:
        ps = [ctx.enter_context(nc.psum_tensor(f"{name}_ps{i}", [m, 512], F32)) for i in range(2)]
        product, emptied = (ctx.enter_context(nc.semaphore(f"{name}_{n}")) for n in ("product", "emptied"))
        with nc.Block() as block:
            @block.tensor
            def _(pe):
                for i, tiles in groups(GROUP):
                    if i >= 2:
                        pe.wait_ge(emptied, i - 1)
                    c0, n = i * GROUP * NP, len(tiles) * NP
                    for t, (weights, features) in enumerate(terms):
                        last = nc.tensor.matmul(ps[i % 2][:, 0:n], weights, features[:, c0:c0 + n],
                                                start=t == 0, stop=t == len(terms) - 1)
                    last.then_inc(product, 1)

            @block.scalar
            def _(act):
                for i, tiles in groups(GROUP):
                    act.wait_ge(product, i + 1)
                    c0, n = i * GROUP * NP, len(tiles) * NP
                    if bias is None:
                        done = nc.scalar.activation(dst[:, c0:c0 + n], ps[i % 2][:, 0:n], func)
                    else:
                        done = nc.scalar.activation(dst[:, c0:c0 + n], ps[i % 2][:, 0:n], func, bias=bias)
                    done.then_inc(emptied, 1)


def nodes_out(nc, name, product, vector_steps):
    with ExitStack() as ctx:
        ps = [ctx.enter_context(nc.psum_tensor(f"{name}_ps{i}", [NP, 8, D], F32)) for i in range(4)]
        made, chain = (ctx.enter_context(nc.semaphore(f"{name}_{n}")) for n in ("made", "chain"))
        sqrt_in, sqrt_out = (ctx.enter_context(nc.semaphore(f"{name}_{n}")) for n in ("sqrt_in", "sqrt_out"))
        with nc.Block() as block:
            yield block, sqrt_in, sqrt_out

            @block.tensor
            def _(pe):
                for i, tiles in groups(8):
                    for j, k in enumerate(tiles):
                        last = product(ps[i][:, j, :], k)
                    last.then_inc(made, 1)

            @block.vector
            def _(dve):
                link = linker(dve, chain)
                for i, tiles in groups(8):
                    dve.wait_ge(made, i + 1)
                    vector_steps(link, slice(tiles[0], tiles[-1] + 1), ps[i][:, 0:len(tiles), :])
                vector_steps(link, None, (dve, sqrt_in, sqrt_out))


def on_nodes(row, tiles):
    return row[:].unsqueeze(1).to_broadcast([NP, tiles.stop - tiles.start, D])


def sqrt_of_variance(nc, g, act, sqrt_in, sqrt_out):
    act.wait_ge(sqrt_in, 1)
    nc.scalar.activation(g["std"][:], g["stat"][:], ACT.Sqrt).then_inc(sqrt_out, 1)


def after_l0(nc, g):
    x, h, hs, agg_t, ident = g["x"], g["h"], g["hs"], g["agg_t"], g["ident"]

    def steps(link, tiles, what):
        if tiles is not None:
            link(nc.vector.tensor_tensor(x[:, tiles, :], x[:, tiles, :], what, ALU.add))
            return
        dve, sqrt_in, sqrt_out = what
        layer_norm_relu(nc, dve, link, sqrt_in, sqrt_out, 0, x, h, g["centred"], g["stat"], g["std"])
        split3(nc, link, h[:], hs[:, :, 0:D], hs[:, :, D:2 * D], hs[:, :, 2 * D:3 * D], g["centred"][:])
        link(nc.vector.memset(hs[:, :, 3 * D:3 * D + 1], 1.0))

    for block, sqrt_in, sqrt_out in nodes_out(
            nc, "n0", lambda ps, k: nc.tensor.transpose(ps, agg_t[:, k, 0:NP], ident[0:D, 0:D]), steps):
        @block.scalar
        def _(act):
            sqrt_of_variance(nc, g, act, sqrt_in, sqrt_out)


def after_l1(nc, g):
    x, h, hs, w = g["x"], g["h"], g["hs"], g["w"]
    agg, cnt, inv = g["agg_1"], g["cnt_dst"], g["stat"]
    with ExitStack() as ctx:
        def sb(name, shape, dt=F32):
            return ctx.enter_context(nc.sbuf_tensor(name, shape, dt))

        feat = sb("features_1", [D, N_NODES])
        chain = ctx.enter_context(nc.semaphore("mean1_chain"))
        with nc.Block() as block:
            @block.vector
            def _(dve):
                link = linker(dve, chain)
                link(nc.vector.tensor_scalar(inv[:], cnt[:], 1.0, None, ALU.max))
                link(nc.vector.reciprocal(inv[:], inv[:]))
                nc.vector.tensor_tensor(agg[:], agg[:], inv[:].unsqueeze(2).to_broadcast([NP, NT, D]), ALU.mult)
        turn_nodes(nc, g, "mean1", agg, D, feat)

        cat = sb("cat2", [NP, NT, 2 * D])

        def steps(link, tiles, what):
            if tiles is not None:
                t = g["centred"][:, tiles, :]
                link(nc.vector.tensor_tensor(t, what, on_nodes(w["gb"], tiles), ALU.add))
                link(nc.vector.tensor_scalar(t, t, 0.0, None, ALU.max))
                link(nc.vector.tensor_tensor(x[:, tiles, :], x[:, tiles, :], t, ALU.add))
                return
            dve, sqrt_in, sqrt_out = what
            layer_norm_relu(nc, dve, link, sqrt_in, sqrt_out, 0, x, h, g["centred"], g["stat"], g["std"])
            link(nc.vector.tensor_copy(cat[:, :, 0:D], h[:]))
            link(nc.vector.tensor_copy(cat[:, :, D:2 * D], g["agg_e"][:]))

        for block, sqrt_in, sqrt_out in nodes_out(
                nc, "n1", lambda ps, k: nc.tensor.matmul(ps, feat[:, k * NP:(k + 1) * NP], w["gW"][:], start=True, stop=True),
                steps):
            @block.scalar
            def _(act):
                sqrt_of_variance(nc, g, act, sqrt_in, sqrt_out)

        cat_t, hidden = sb("cat2_t", [2 * D, N_NODES]), sb("hidden2", [128, N_NODES])
        turn_nodes(nc, g, "cat2t", cat, 2 * D, cat_t)
        dense(nc, "mlp2", [(w["W1"][:], cat_t)], 128, ACT.Relu, w["b1"][:], hidden)

        def steps2(link, tiles, what):
            if tiles is not None:
                t = g["centred"][:, tiles, :]
                link(nc.vector.tensor_tensor(t, what, on_nodes(w["b2"], tiles), ALU.add))
                link(nc.vector.tensor_tensor(x[:, tiles, :], x[:, tiles, :], t, ALU.add))
                return
            dve, sqrt_in, sqrt_out = what
            layer_norm_relu(nc, dve, link, sqrt_in, sqrt_out, 0, x, h, g["centred"], g["stat"], g["std"])

        for block, sqrt_in, sqrt_out in nodes_out(
                nc, "n2", lambda ps, k: nc.tensor.matmul(ps, hidden[:, k * NP:(k + 1) * NP], w["W2"][:], start=True, stop=True),
                steps2):
            @block.scalar
            def _(act):
                sqrt_of_variance(nc, g, act, sqrt_in, sqrt_out)
    g["h_t"] = g["sb"]("h3_t", [D, N_NODES])
    turn_nodes(nc, g, "h3t", h, D, g["h_t"])

    def steps3(link, tiles, what):
        if tiles is not None:
            p, rest = hs[:, tiles, :], g["centred"][:, tiles, :]
            split3(nc, link, what, p[:, :, 0:D], p[:, :, D:2 * D], p[:, :, 2 * D:3 * D], rest)

    for block, _, _ in nodes_out(
            nc, "n3", lambda ps, k: nc.tensor.matmul(ps, g["h_t"][:, k * NP:(k + 1) * NP], w["W1a"][:], start=True, stop=True),
            steps3):
        pass


def finish(nc, g):
    x, w, agg_t, cnt, ident = g["x"], g["w"], g["agg_t"], g["cnt_src"], g["ident"]
    with ExitStack() as ctx:
        def sb(name, shape, dt=F32):
            return ctx.enter_context(nc.sbuf_tensor(name, shape, dt))

        inv = g["stat"]
        mean = sb("mean3", [NP, NT, D + 1])
        mean_t, agg_f, hidden = sb("mean3_t", [D + 1, N_NODES]), sb("agg3_f", [D, N_NODES]), sb("hidden3", [D, N_NODES])
        chain, stored = (ctx.enter_context(nc.semaphore(n)) for n in ("mean3_chain", "stored"))
        with nc.Block() as block:
            @block.vector
            def _(dve):
                link = linker(dve, chain)
                link(nc.vector.tensor_scalar(inv[:], cnt[:], 1.0, None, ALU.max))
                link(nc.vector.reciprocal(inv[:], inv[:]))
                link(nc.vector.tensor_tensor(mean[:, :, D:D + 1], cnt[:].unsqueeze(2), inv[:].unsqueeze(2), ALU.mult))

        def steps(link, tiles, what):
            if tiles is not None:
                n = tiles.stop - tiles.start
                link(nc.vector.tensor_tensor(mean[:, tiles, 0:D], what,
                                             inv[:, tiles].unsqueeze(2).to_broadcast([NP, n, D]), ALU.mult))

        for block, _, _ in nodes_out(nc, "m3", lambda ps, k: nc.tensor.transpose(ps, agg_t[:, k, 0:NP], ident[0:D, 0:D]), steps):
            pass
        turn_nodes(nc, g, "mean3t", mean, D + 1, mean_t)
        dense(nc, "agg3", [(w["W1b"][:], mean_t)], D, ACT.Copy, None, agg_f)
        dense(nc, "hid3", [(w["W2a_top"][:], g["h_t"]), (w["W2a_bot"][:], agg_f)], D, ACT.Relu, w["b2a"][:], hidden)

        def steps_out(link, tiles, what):
            if tiles is not None:
                t = g["centred"][:, tiles, :]
                link(nc.vector.tensor_tensor(t, what, on_nodes(w["b2b"], tiles), ALU.add))
                link(nc.vector.tensor_tensor(x[:, tiles, :], x[:, tiles, :], t, ALU.add))

        for block, _, _ in nodes_out(
                nc, "out3", lambda ps, k: nc.tensor.matmul(ps, hidden[:, k * NP:(k + 1) * NP], w["W2b"][:], start=True, stop=True),
                steps_out):
            pass
        with nc.Block() as block:
            @block.sync
            def _(sp):
                sp.dma_start(g["out"].rearrange("(k i) d -> i k d", i=NP), x[:]).then_inc(stored, 16)
                sp.wait_ge(stored, 16)


_INS = ["x", "src", "dst", "edge_attr_64", "edge_weight", "L1_gnn_W", "L1_gnn_b", "L2_gnn_W1", "L2_gnn_b1", "L2_gnn_W2",
        "L2_gnn_b2", "L3_gnn_W1a", "L3_gnn_b1a", "L3_gnn_W1b", "L3_gnn_b1b", "L3_gnn_W2a", "L3_gnn_b2a", "L3_gnn_W2b",
        "L3_gnn_b2b"]


def constants():
    import numpy as np

    node = np.full((1, NT, 128), -4000.0, np.float16)
    node[0, :, :NP] = np.arange(N_NODES).reshape(NT, NP) - CENTRE
    n = NT * HB
    at_block = np.arange(n)
    return {
        "identity": np.eye(128, dtype=np.float32),
        "node_numbers": node.reshape(1, NT * 128),
        "key_numbers": np.arange(KW, dtype=np.float32)[None],
        "tile_steps": STEP * np.arange(NT, dtype=np.float32)[None],
        "before": np.triu(np.ones((NP, NP), np.float32), 1),
        "same_column": (at_block[:, None] % HB == at_block % HB).astype(np.float32),
        "fold": (at_block[:, None] // HB == np.arange(NT)).astype(np.float32),
    }


def kernel(**inputs):
    import numpy as _np
    import concourse.bacc as _bacc
    from concourse import mybir as _mybir
    from concourse.bass_utils import run_bass_kernel_spmd as _run

    nc = _bacc.Bacc("TRN2", target_bir_lowering=False, num_devices=1)
    arrays, args = {}, []
    given = {name: inputs[name] for name in _INS}
    given.update(constants())
    for name, a in given.items():
        a = _np.ascontiguousarray(a)
        arrays[f"in_{name}_dram"] = a
        args.append(nc.dram_tensor(f"in_{name}_dram", a.shape, _mybir.dt.from_np(a.dtype), kind="ExternalInput").ap())
    args.append(nc.dram_tensor("out_0_dram", (N_NODES, D), F32, kind="ExternalOutput").ap())
    build(nc, *args)
    r = _run(nc, [arrays], core_ids=[0])
    return r.results[0]["out_0_dram"]
```

```python
from contextlib import ExitStack

import concourse.bass as bass
from concourse import mybir
from concourse.alu_op_type import AluOpType as ALU

F32 = mybir.dt.float32
BF16 = mybir.dt.bfloat16
F16 = mybir.dt.float16
I32 = mybir.dt.int32
U16 = mybir.dt.uint16
ACT = mybir.ActivationFunctionType
AX = mybir.AxisListType

N_NODES, N_EDGES, D = 3125, 103125, 64
NT = 25
NP = N_NODES // NT
EP = 125
ET = N_EDGES // EP
CENTRE = (N_NODES - 1) // 2
EPS = 1e-5
MAGIC = 12582912.0

EA_W = (3 * D + 2) // 2
M_DST, M_KEY, M_W = 0, 1, 2
META = 4
STEP = 8192
ROW = EA_W + META + D
PAD_ROWS = 256
N_ROWS = N_EDGES + PAD_ROWS

WIN = 256
NW = NT + 1
NG = NW // 2
CUTS = (0, 7, NG)
HALF = 16
MAX_ROUNDS = -(-N_EDGES // WIN)
OF_SRC, OF_DST = 0, 1
KW = 640
CHUNK, SUB = 11, 3
HB = 3


def layer_norm_relu(nc, dve, link, act_sqrt_ready, act_sqrt_done, n_before, x, h, centred, stat, std):
    link(nc.vector.tensor_reduce(stat[:], x[:], AX.X, ALU.add))
    link(nc.vector.tensor_scalar(stat[:], stat[:], 1.0 / D, None, ALU.mult))
    link(nc.vector.tensor_tensor(centred[:], x[:], stat[:].unsqueeze(2).to_broadcast([NP, NT, D]), ALU.subtract))
    link(nc.vector.tensor_tensor(h[:], centred[:], centred[:], ALU.mult))
    link(nc.vector.tensor_reduce(stat[:], h[:], AX.X, ALU.add))
    nc.vector.tensor_scalar(stat[:], stat[:], 1.0 / D, EPS, ALU.mult, ALU.add).then_inc(act_sqrt_ready, 1)
    dve.wait_ge(act_sqrt_done, n_before + 1)
    link(nc.vector.reciprocal(std[:], std[:]))
    link(nc.vector.tensor_tensor(centred[:], centred[:], std[:].unsqueeze(2).to_broadcast([NP, NT, D]), ALU.mult))
    link(nc.vector.tensor_scalar(h[:], centred[:], 0.0, None, ALU.max))


def split3(nc, link, whole, hi, mid, lo, rest):
    link(nc.vector.tensor_copy(hi, whole))
    link(nc.vector.tensor_tensor(rest, whole, hi, ALU.subtract))
    link(nc.vector.tensor_copy(mid, rest))
    link(nc.vector.tensor_tensor(lo, rest, mid, ALU.subtract))


def linker(engine, sem):
    count = [0]

    def link(ins):
        count[0] += 1
        ins.then_inc(sem, 1)
        engine.wait_ge(sem, count[0])

    return link


def build(nc, x_in, src_in, dst_in, ea_in, ew_in, gW, gb, W1, b1, W2, b2, W1a, b1a, W1b, b1b, W2a, b2a, W2b, b2b,
          c_ident, c_iota, c_key, c_step, c_base, c_adv, c_tri, c_hmask, c_hfold, out):
    ctx = ExitStack()
    with ctx:
        def sb(name, shape, dt=F32):
            return ctx.enter_context(nc.sbuf_tensor(name, shape, dt))

        def dram(name, shape, dt):
            return nc.dram_tensor(name, shape, dt, kind="Internal").ap()

        rows = dram("sorted_rows", [N_ROWS, ROW], I32)
        tab = dram("window_starts", [MAX_ROUNDS * NT, 32], I32)

        ident = sb("ident", [128, 128])
        iota4 = sb("iota4", [128, NP, 4], F16)
        tile_steps = sb("tile_steps", [128, NT])
        tile_bases = sb("tile_bases", [128, NT])
        keys = sb("keys_of_windows", [128, NT, 2, NW, 2], BF16)
        tri = sb("tri", [NP, NP])
        x = sb("x", [NP, NT, D])
        h = sb("h", [NP, NT, D])
        centred = sb("centred", [NP, NT, D])
        stat = sb("stat", [NP, NT])
        std = sb("std", [NP, NT])
        rounds_i = sb("rounds", [1, 1], I32)
        starts_f = sb("window_starts_f", [NT, 32])
        wa_bot2 = sb("w1a_bot_twice", [128, 128])
        b1a_bc = sb("b1a_on_all", [EP, D])

        w = {"gW": sb("gW", [D, D]), "W1": sb("W1", [2 * D, 128]), "W2": sb("W2", [128, D]), "W1a": sb("W1a_top", [D, D]),
             "W1b": sb("W1b_and_b1b", [D + 1, D]), "W2a_top": sb("W2a_top", [D, D]), "W2a_bot": sb("W2a_bot", [D, D]),
             "W2b": sb("W2b", [D, D]), "b1": sb("b1", [128, 1]), "b2a": sb("b2a", [D, 1]),
             "gb": sb("gb_on_all", [NP, D]), "b2": sb("b2_on_all", [NP, D]), "b2b": sb("b2b_on_all", [NP, D])}
        weights_in = ctx.enter_context(nc.semaphore("weights_in"))
        passed = ctx.enter_context(nc.semaphore("passed"))
        consts_in = ctx.enter_context(nc.semaphore("consts_in"))
        filled = [ctx.enter_context(nc.semaphore(f"filled{i}")) for i in range(NG)]

        g = dict(locals())
        prep(nc, g)
        g["agg_t"] = sb("agg_t", [D, NT, 128])
        g["agg_e"] = sb("agg_e", [NP, NT, D])
        g["agg_1"] = sb("agg_1", [NP, NT, D])
        g["cnt_src"] = sb("cnt_src", [NP, NT])
        g["cnt_dst"] = sb("cnt_dst", [NP, NT])
        g["hs"] = sb("h_parts", [NP, NT, 3 * D + 1], BF16)
        rounds = g["rounds"]
        pass_by_src(nc, g, rounds)
        after_l0(nc, g)
        pass_by_dst(nc, g, rounds)
        after_l1(nc, g)
        pass_messages(nc, g, rounds)
        finish(nc, g)


def prep(nc, g):
    tri, ident, x, h = g["tri"], g["ident"], g["x"], g["h"]
    with ExitStack() as ctx:
        def sb(name, shape, dt=F32):
            return ctx.enter_context(nc.sbuf_tensor(name, shape, dt))

        def sem(name):
            return ctx.enter_context(nc.semaphore(name))

        meta = sb("meta", [EP, ET, META])
        src_c = sb("src_c", [EP, ET])
        pos_i = sb("pos_i", [EP, ET], I32)

        with ExitStack() as c1:
            def sb1(name, shape, dt=F32):
                return c1.enter_context(nc.sbuf_tensor(name, shape, dt))

            def ps1(name, shape, dt=F32):
                return c1.enter_context(nc.psum_tensor(name, shape, dt))

            def sem1(name):
                return c1.enter_context(nc.semaphore(name))

            src_i, dst_i, nxt_i = (sb1(n, [EP, ET], I32) for n in ("src_i", "dst_i", "nxt_i"))
            ew = sb1("ew", [EP, ET])
            q_f, p_f, tmp = sb1("q_f", [EP, ET]), sb1("p_f", [EP, ET]), sb1("tmp", [EP, ET])
            q16, p16, key16 = sb1("q16", [EP, ET], F16), sb1("p16", [EP, ET], F16), sb1("key16", [EP, ET], F16)
            mask = sb1("mask", [EP, ET], BF16)
            ones_w = sb1("ones_w", [EP, ET], BF16)
            scan = sb1("scan", [EP, ET])
            keys = sb1("keys", [EP, KW])
            tot, col, incl, off = (sb1(n, [EP, KW]) for n in ("tot", "col", "incl", "off"))
            oh_q, oh_p = sb1("oh_q", [EP, NT, ET], BF16), sb1("oh_p", [EP, NT, ET], BF16)
            ones_m = sb1("ones_m", [EP, EP])
            viol, flag, mul, nkeys_f = (sb1(n, [EP, 1]) for n in ("viol", "flag", "mul", "nkeys_f"))
            nkeys_i = sb1("nkeys_i", [1, 1], I32)
            hmask, hfold = sb1("hmask", [NT * HB, NT * HB]), sb1("hfold", [NT * HB, NT])
            h75 = sb1("h75", [NT * HB, NT * HB])
            cnt, start, half = sb1("cnt", [NT, NT]), sb1("start", [NT, NT]), sb1("half", [NT, NT])
            row, base, diag = sb1("row", [NT, 1]), sb1("base", [NT, 1]), sb1("diag", [NT, 1])
            r_row, r_max = sb1("r_row", [1, NT]), sb1("r_max", [1, 1])

            ps_excl = ps1("ps_excl", [EP, 2, 512])
            ps_col = ps1("ps_col", [EP, 2, 512])
            ps_hist = ps1("ps_hist", [NT * HB, NT * HB])
            ps_small = ps1("ps_small", [EP, 512])

            ints_in, next_in, ew_in = (sem1(n) for n in ("ints_in", "next_in", "ew_in"))
            next_pad, exp_done, flag_in, flag_sum, tot_ready, off_ready, onehots, hist_done = (sem1(n) for n in (
                "next_pad", "exp_done", "flag_in", "flag_sum", "tot_ready", "off_ready", "onehots", "hist_done"))
            h75_ready, folded, row_ready, base_ready, rmax_ready, rmax_t = (
                sem1(n) for n in ("h75_ready", "folded", "row_ready", "base_ready", "rmax_ready", "rmax_t"))
            dch = sem1("dve_chain_order")
            sqrt_in, sqrt_out = sem1("sqrt_in0"), sem1("sqrt_out0")
            hoh = sem1("histogram_onehot")
            kcount = sem1("key_counted")
            with nc.Block() as block:
                @block.sync
                def _(sp):
                    sp.dma_start(src_i[:], g["src_in"].rearrange("(i t) -> i t", t=ET)).then_inc(ints_in, 16)
                    sp.dma_start(dst_i[:], g["dst_in"].rearrange("(i t) -> i t", t=ET)).then_inc(ints_in, 16)
                    sp.wait_ge(next_pad, 1)
                    body = (EP - 1) * ET
                    sp.dma_start(nxt_i[0:EP - 1, :], g["dst_in"][1:1 + body].rearrange("(i t) -> i t", t=ET)).then_inc(next_in, 16)
                    sp.dma_start(nxt_i[EP - 1:EP, 0:ET - 1], g["dst_in"][1 + body:N_EDGES].unsqueeze(0)).then_inc(next_in, 16)
                    sp.dma_start(ew[:], g["ew_in"].rearrange("(i t) -> i t", t=ET)).then_inc(ew_in, 16)
                    for to, of in ((ident[:], g["c_ident"]), (tri[:], g["c_tri"]), (hmask[:], g["c_hmask"]),
                                   (hfold[:], g["c_hfold"]), (keys[:], g["c_key"].to_broadcast([EP, KW])),
                                   (g["iota4"][:], g["c_iota"].rearrange("o (j s) -> o j s", s=4).to_broadcast([128, NP, 4])),
                                   (g["tile_bases"][:], g["c_base"].to_broadcast([128, NT])),
                                   (g["tile_steps"][:], g["c_step"].to_broadcast([128, NT])),
                                   (x[:], g["x_in"].rearrange("(k i) d -> i k d", i=NP)),
                                   (g["b1a_bc"][:], g["b1a"].unsqueeze(0).to_broadcast([EP, D]))):
                        sp.dma_start(to, of).then_inc(g["consts_in"], 16)
                    w = g["w"]
                    on_all = lambda b: b.unsqueeze(0).to_broadcast([NP, D])
                    for to, of in ((w["gW"][:], g["gW"]), (w["W1"][:], g["W1"]), (w["W2"][:], g["W2"]),
                                   (w["W1a"][:], g["W1a"][0:D, :]), (w["W1b"][0:D, :], g["W1b"]),
                                   (w["W1b"][D:D + 1, :], g["b1b"].unsqueeze(0)), (w["W2a_top"][:], g["W2a"][0:D, :]),
                                   (w["W2a_bot"][:], g["W2a"][D:2 * D, :]), (w["W2b"][:], g["W2b"]),
                                   (w["b1"][:], g["b1"].unsqueeze(1)), (w["b2a"][:], g["b2a"].unsqueeze(1)),
                                   (w["gb"][:], on_all(g["gb"])), (w["b2"][:], on_all(g["b2"])),
                                   (w["b2b"][:], on_all(g["b2b"]))):
                        sp.dma_start(to, of).then_inc(g["weights_in"], 16)
                    sp.wait_ge(g["weights_in"], 16 * 14)

                @block.scalar
                def _(act):
                    act.wait_ge(ew_in, 16)
                    nc.scalar.activation(ew[:], ew[:], ACT.Exp, scale=-1.0).then_inc(exp_done, 1)
                    act.wait_ge(sqrt_in, 1)
                    nc.scalar.activation(g["std"][:], g["stat"][:], ACT.Sqrt).then_inc(sqrt_out, 1)

                @block.vector
                def _(dve):
                    link = linker(dve, dch)
                    nc.vector.memset(nxt_i[:, ET - 1:ET], N_NODES - 1).then_inc(next_pad, 1)
                    nc.vector.memset(ones_m[:], 1.0)
                    nc.vector.memset(ones_w[:], 1.0)
                    nc.vector.memset(g["starts_f"][:], 0.0)
                    link(nc.vector.memset(tot[:], 0.0))
                    dve.wait_ge(ints_in, 32)

                    def tile_of(tile_f, node_i, centre_to=None):
                        link(nc.vector.tensor_copy(tmp[:], node_i[:]))
                        if centre_to is not None:
                            nc.vector.tensor_scalar(centre_to, tmp[:], -float(CENTRE), None, ALU.add)
                        link(nc.vector.tensor_scalar(tile_f[:], tmp[:], -float(NP // 2), 1.0 / NP, ALU.add, ALU.mult))
                        link(nc.vector.tensor_scalar(tile_f[:], tile_f[:], MAGIC, None, ALU.add))
                        link(nc.vector.tensor_scalar(tile_f[:], tile_f[:], -MAGIC, None, ALU.add))

                    tile_of(q_f, src_i, src_c[:])
                    tile_of(p_f, dst_i, meta[:, :, M_DST])
                    dve.wait_ge(next_in, 32)
                    tile_of(scan, nxt_i)
                    link(nc.vector.tensor_tensor(tmp[:], p_f[:], scan[:], ALU.is_gt))
                    nc.vector.tensor_reduce(viol[:], tmp[:], AX.X, ALU.max).then_inc(flag_in, 1)
                    nc.vector.tensor_copy(q16[:], q_f[:])
                    nc.vector.scalar_tensor_tensor(meta[:, :, M_KEY], p_f[:], float(STEP), src_c[:], ALU.mult, ALU.add)
                    link(nc.vector.tensor_copy(p16[:], p_f[:]))
                    dve.wait_ge(g["consts_in"], 16 * 10)
                    with dve.Fori(0, NT) as k:
                        nc.vector.tensor_scalar(oh_q[:, bass.ds(k, 1), :].rearrange("p o t -> p (o t)"), q16[:],
                                                keys[:, bass.ds(k, 1)], None, ALU.is_equal)
                        nc.vector.tensor_scalar(oh_p[:, bass.ds(k, 1), :].rearrange("p o t -> p (o t)"), p16[:],
                                                keys[:, bass.ds(k, 1)], None, ALU.is_equal).then_inc(hoh, 1)
                    dve.wait_ge(flag_sum, 1)
                    link(nc.vector.tensor_scalar(flag[:], ps_small[:, 0:1], 1.0, None, ALU.min))
                    nc.vector.tensor_scalar(nkeys_f[:], flag[:], float(NT * NT - NT), float(NT), ALU.mult, ALU.add)
                    link(nc.vector.tensor_scalar(mul[:], flag[:], float(NT - 1), 1.0, ALU.mult, ALU.add))
                    link(nc.vector.tensor_copy(nkeys_i[:], nkeys_f[0:1, :]))
                    link(nc.vector.tensor_scalar(tmp[:], p_f[:], flag[:], None, ALU.mult))
                    link(nc.vector.tensor_scalar(scan[:], q_f[:], mul[:], None, ALU.mult))
                    link(nc.vector.tensor_tensor(key16[:], tmp[:], scan[:], ALU.add))
                    n_keys = dve.value_load(nkeys_i[0:1, 0:1], min_val=NT, max_val=NT * NT)
                    with dve.Fori(0, n_keys) as k:
                        nc.vector.tensor_scalar(mask[:], key16[:], keys[:, bass.ds(k, 1)], 0.0, ALU.is_equal, ALU.add,
                                                accum_out=tot[:, bass.ds(k, 1)]).then_inc(kcount, 1)
                        dve.wait_ge(kcount, k + 1)
                    dve.sem_inc(tot_ready, 1)
                    dve.wait_ge(off_ready, 1)
                    for c in range(2):
                        link(nc.vector.tensor_copy(col[:, c * 320:c * 320 + 320], ps_col[:, c, 0:320]))
                    link(nc.vector.tensor_tensor_scan(incl[:], ones_w[:, 0:KW], col[:], 0.0, ALU.mult, ALU.add))
                    link(nc.vector.tensor_tensor(incl[:], incl[:], col[:], ALU.subtract))
                    for c in range(2):
                        sl = slice(c * 320, c * 320 + 320)
                        link(nc.vector.scalar_tensor_tensor(off[:, sl], incl[:, sl], -1.0, ps_excl[:, c, 0:320],
                                                            ALU.add, ALU.add))
                    with dve.Fori(0, n_keys) as k:
                        nc.vector.tensor_scalar(mask[:], key16[:], keys[:, bass.ds(k, 1)], None,
                                                ALU.is_equal).then_inc(kcount, 1)
                        dve.wait_ge(kcount, n_keys + k * 3 + 1)
                        nc.vector.tensor_tensor_scan(scan[:], ones_w[:], mask[:], off[:, bass.ds(k, 1)],
                                                     ALU.mult, ALU.add).then_inc(kcount, 1)
                        dve.wait_ge(kcount, n_keys + k * 3 + 2)
                        alone(dve, g)
                        nc.vector.copy_predicated(tmp[:], mask[:].bitcast(U16), scan[:]).then_inc(kcount, 1)
                        dve.wait_ge(kcount, n_keys + k * 3 + 3)
                    link(nc.vector.tensor_copy(pos_i[:], tmp[:]))
                    dve.wait_ge(exp_done, 1)
                    parts = meta[:].bitcast(BF16)[:, :, 2 * M_W:2 * M_W + 4]
                    nc.vector.memset(parts[:, :, 3:4], 0.0)
                    link(nc.vector.tensor_copy(parts[:, :, 0:1], ew[:].unsqueeze(2)))
                    link(nc.vector.tensor_tensor(tmp[:].unsqueeze(2), ew[:].unsqueeze(2), parts[:, :, 0:1], ALU.subtract))
                    link(nc.vector.tensor_copy(parts[:, :, 1:2], tmp[:].unsqueeze(2)))
                    link(nc.vector.tensor_tensor(parts[:, :, 2:3], tmp[:].unsqueeze(2), parts[:, :, 1:2], ALU.subtract))
                    dve.wait_ge(hist_done, 1)
                    nc.vector.tensor_tensor(h75[:], ps_hist[:], hmask[:], ALU.mult).then_inc(h75_ready, 1)
                    dve.wait_ge(folded, 1)
                    link(nc.vector.tensor_reduce(cnt[:], ps_small[0:NT, 128:128 + NT * HB].rearrange("q (p b) -> q p b", b=HB),
                                                 AX.X, ALU.add))
                    nc.vector.tensor_reduce(row[:], cnt[:], AX.X, ALU.add).then_inc(row_ready, 1)
                    dve.wait_ge(base_ready, 1)
                    link(nc.vector.tensor_copy(base[:], ps_small[0:NT, 256:257]))
                    link(nc.vector.tensor_tensor_scan(start[:], ones_w[0:NT, 0:NT], cnt[:], base[:], ALU.mult, ALU.add))
                    link(nc.vector.tensor_tensor(start[:], start[:], cnt[:], ALU.subtract))
                    link(nc.vector.tensor_tensor(half[:], start[:], ident[0:NT, 0:NT], ALU.mult))
                    link(nc.vector.tensor_reduce(diag[:], half[:], AX.X, ALU.add))
                    sf = g["starts_f"]
                    nc.vector.tensor_scalar(sf[:, HALF + NG - 1:HALF + NG], diag[:], float(WIN), float(N_EDGES), ALU.add, ALU.min)
                    nc.vector.tensor_copy(sf[:, 0:NG], start[:, 0:NG])
                    nc.vector.tensor_copy(sf[:, HALF:HALF + NT - NG], start[:, NG:NT])
                    link(nc.vector.tensor_scalar(half[:], ident[0:NT, 0:NT], -0.5, 1.0, ALU.mult, ALU.add))
                    link(nc.vector.tensor_tensor(half[:], half[:], cnt[:], ALU.mult))
                    nc.vector.tensor_reduce(row[:], half[:], AX.X, ALU.max).then_inc(rmax_ready, 1)
                    dve.wait_ge(rmax_t, 1)
                    link(nc.vector.tensor_reduce(r_max[:], ps_small[0:1, 384:384 + NT], AX.X, ALU.max))
                    link(nc.vector.tensor_scalar(r_max[:], r_max[:], WIN / 2 - 0.25, 1.0 / WIN, ALU.add, ALU.mult))
                    link(nc.vector.tensor_scalar(r_max[:], r_max[:], MAGIC, None, ALU.add))
                    link(nc.vector.tensor_scalar(r_max[:], r_max[:], -MAGIC, 1.0, ALU.add, ALU.max))
                    link(nc.vector.tensor_copy(g["rounds_i"][:], r_max[:]))
                    layer_norm_relu(nc, dve, link, sqrt_in, sqrt_out, 0, x, h, g["centred"], g["stat"], g["std"])

                @block.tensor
                def _(pe):
                    pe.wait_ge(flag_in, 1)
                    nc.tensor.matmul(ps_small[:, 0:1], ones_m[:], viol[:], start=True, stop=True).then_inc(flag_sum, 1)

                    def pairs(t, first, last):
                        one_q, one_p = (o[:].rearrange("i k (b t) -> i (k b) t", b=HB)[:, :, bass.ds(t, 1)]
                                        .rearrange("i m o -> i (m o)") for o in (oh_q, oh_p))
                        return nc.tensor.matmul(ps_hist[:], one_q, one_p, start=first, stop=last)

                    pe.wait_ge(hoh, NT)
                    per = ET // HB // NT
                    for j in range(per):
                        pairs(j, j == 0, False)
                    with pe.Fori(1, NT - 1) as i:
                        for j in range(per):
                            pairs(i * per + j, False, False)
                    for j in range(per):
                        hist = pairs((NT - 1) * per + j, False, j == per - 1)
                    hist.then_inc(hist_done, 1)
                    pe.wait_ge(tot_ready, 1)
                    for c in range(2):
                        nc.tensor.matmul(ps_excl[:, c, 0:320], tri[:], tot[:, c * 320:c * 320 + 320], start=True, stop=True)
                        last = nc.tensor.matmul(ps_col[:, c, 0:320], ones_m[:], tot[:, c * 320:c * 320 + 320], start=True, stop=True)
                    last.then_inc(off_ready, 1)
                    pe.wait_ge(h75_ready, 1)
                    nc.tensor.matmul(ps_small[0:NT, 128:128 + NT * HB], hfold[:], h75[:], start=True, stop=True).then_inc(folded, 1)
                    pe.wait_ge(row_ready, 1)
                    nc.tensor.matmul(ps_small[0:NT, 256:257], tri[0:NT, 0:NT], row[:], start=True, stop=True).then_inc(base_ready, 1)
                    pe.wait_ge(rmax_ready, 1)
                    nc.tensor.transpose(ps_small[0:1, 384:384 + NT], row[:], ident[0:NT, 0:NT]).then_inc(rmax_t, 1)

        with ExitStack() as c2:
            def sb2(name, shape, dt=F32):
                return c2.enter_context(nc.sbuf_tensor(name, shape, dt))

            def sem2(name):
                return c2.enter_context(nc.semaphore(name))

            ea = [sb2(f"ea{j}", [EP, CHUNK, D]) for j in range(SUB)]
            rowbuf = [sb2(f"rowbuf{j}", [EP, CHUNK, ROW], I32) for j in range(SUB)]
            rest = sb2("rest", [EP, CHUNK, D])
            posbuf = [sb2(f"posbuf{j}", [EP, CHUNK], I32) for j in range(SUB)]
            pad = sb2("pad", [128, 2, ROW], I32)
            pairs_n = (CHUNK + 1) // 2
            advance, starts_i = sb2("advance", [NT, 32]), sb2("starts_i", [NT, 32], I32)
            adv_in, starts_ready, starts_out, stored_once, table_chain = (sem2(n) for n in (
                "adv_in", "starts_ready", "starts_out", "stored_once", "table_chain"))
            rounds = nc.values_load(g["rounds_i"][0:1, 0:1], min_val=1, max_val=MAX_ROUNDS)
            g["rounds"] = rounds
            ea_t = sb2("ea_t", [128, pairs_n, 128])
            ps_t = c2.enter_context(nc.psum_tensor("ps_t", [128, 8, 128], F32))
            ps_q = c2.enter_context(nc.psum_tensor("ps_q", [EP, 8, 128], F32))
            ea_in = [sem2(f"ea_in{j}") for j in range(SUB)]
            moved = [sem2(f"moved{j}") for j in range(SUB)]
            w_in, pad_ready, pad_out, w_zero, tposed, tcopied, q_done, hi_done, row_done, chain, rowpad = (sem2(n) for n in (
                "w_in", "pad_ready", "pad_out", "w_zero", "tposed", "tcopied", "q_done", "hi_done", "row_done", "mv_chain", "rowpad"))
            ea_v = g["ea_in"].rearrange("(i t) d -> i t d", t=ET)
            wa2 = g["wa_bot2"]

            def parts(j, a):
                return rowbuf[j][:].bitcast(BF16)[:, :, a * D:(a + 1) * D]

            with nc.Block() as block:
                @block.sync
                def _(sp):
                    sp.sem_inc(stored_once, 1)
                    sp.dma_start(advance[:], g["c_adv"]).then_inc(adv_in, 16)
                    with sp.Fori(0, rounds) as r:
                        sp.wait_ge(starts_ready, r + 1)
                        sp.dma_start(g["tab"][bass.ds(r * NT, NT), :], starts_i[:]).then_inc(starts_out, 16)
                        sp.wait_ge(starts_out, r * 16 + 16)
                        sp.sem_inc(stored_once, 1)
                    sp.wait_ge(w_zero, 1)
                    sp.dma_start(wa2[0:D, 0:D], g["W1a"][D:2 * D, :]).then_inc(w_in, 16)
                    sp.dma_start(wa2[D:128, D:128], g["W1a"][D:2 * D, :]).then_inc(w_in, 16)
                    with sp.Fori(0, ET // (CHUNK * SUB)) as it:
                        for j in range(SUB):
                            sp.wait_ge(row_done, it * SUB + 1)
                            sp.dma_start(ea[j][:], ea_v[:, bass.ds(it * SUB * CHUNK + j * CHUNK, CHUNK), :]).then_inc(ea_in[j], 16)
                    sp.wait_ge(pad_ready, 1)
                    sp.dma_start(g["rows"][N_EDGES:N_ROWS, :].rearrange("(i j) w -> i j w", j=2), pad[:]).then_inc(pad_out, 16)
                    sp.wait_ge(pad_out, 16)

                @block.scalar
                def _(act):
                    act.sem_inc(tcopied, 1)

                    def step(it, again):
                        for j in range(SUB):
                            n = it * SUB + j
                            act.wait_ge(ea_in[j], it * 16 + 16)
                            if again:
                                act.wait_ge(moved[j], it * 16 * CHUNK)
                            nc.scalar.activation(parts(j, 0), ea[j][:], ACT.Copy).then_inc(hi_done, 1)
                            act.wait_ge(tposed, n + 1)
                            act.wait_ge(q_done, n + 1)
                            nc.scalar.activation(ea_t[:, 0:pairs_n - 1, 0:EP], ps_t[:, 0:pairs_n - 1, 0:EP], ACT.Copy)
                            nc.scalar.activation(ea_t[0:D, pairs_n - 1, 0:EP], ps_t[0:D, pairs_n - 1, 0:EP], ACT.Copy).then_inc(tcopied, 1)

                    step(0, False)
                    with act.Fori(1, ET // (CHUNK * SUB)) as it:
                        step(it, True)

                @block.vector
                def _(dve):
                    dve.sem_inc(row_done, 1)
                    sf = g["starts_f"]
                    dve.wait_ge(adv_in, 16)
                    with dve.Fori(0, rounds) as r:
                        dve.wait_ge(stored_once, r + 1)
                        nc.vector.tensor_copy(starts_i[:], sf[:]).then_inc(starts_ready, 1)
                        dve.wait_ge(starts_ready, r + 1)
                        nc.vector.tensor_tensor(sf[:], sf[:], advance[:], ALU.add).then_inc(table_chain, 1)
                        dve.wait_ge(table_chain, r * 2 + 1)
                        nc.vector.tensor_scalar(sf[:], sf[:], float(N_EDGES), None, ALU.min).then_inc(table_chain, 1)
                        dve.wait_ge(table_chain, r * 2 + 2)
                    nc.vector.memset(wa2[:], 0.0).then_inc(w_zero, 1)
                    for j in range(SUB):
                        nc.vector.memset(rowbuf[j][:].bitcast(BF16)[:, :, 3 * D:3 * D + 1], 1.0)
                        nc.vector.memset(rowbuf[j][:].bitcast(BF16)[:, :, 3 * D + 1:3 * D + 2], 0.0)
                    nc.vector.memset(pad[:], 0).then_inc(chain, 1)
                    dve.wait_ge(chain, 1)
                    nc.vector.memset(pad[:].bitcast(F32)[:, :, EA_W:EA_W + META], -float(N_NODES)).then_inc(pad_ready, 1)
                    with dve.Fori(0, ET // (CHUNK * SUB)) as it:
                        for j in range(SUB):
                            n = it * SUB + j
                            tile0 = it * SUB * CHUNK + j * CHUNK
                            dve.wait_ge(hi_done, n + 1)
                            nc.vector.tensor_tensor(rest[:], ea[j][:], parts(j, 0), ALU.subtract).then_inc(chain, 1)
                            dve.wait_ge(chain, n * 3 + 2)
                            nc.vector.tensor_copy(parts(j, 1), rest[:]).then_inc(chain, 1)
                            dve.wait_ge(chain, n * 3 + 3)
                            nc.vector.tensor_tensor(parts(j, 2), rest[:], parts(j, 1), ALU.subtract).then_inc(chain, 1)
                            dve.wait_ge(chain, n * 3 + 4)
                            nc.vector.tensor_copy(rowbuf[j][:].bitcast(F32)[:, :, EA_W:EA_W + META],
                                                  meta[:, bass.ds(tile0, CHUNK), :])
                            nc.vector.tensor_copy(posbuf[j][:], pos_i[:, bass.ds(tile0, CHUNK)])
                            dve.wait_ge(q_done, n + 2)
                            nc.vector.tensor_tensor(
                                rowbuf[j][:].bitcast(F32)[:, :, EA_W + META:ROW],
                                ps_q[:].rearrange("p a (b d) -> p (a b) d", d=D)[:, 0:CHUNK, :],
                                g["b1a_bc"][:].unsqueeze(1).to_broadcast([EP, CHUNK, D]), ALU.add).then_inc(row_done, 1)

                @block.tensor
                def _(pe):
                    pe.sem_inc(q_done, 1)
                    pe.wait_ge(w_in, 32)
                    with pe.Fori(0, ET // (CHUNK * SUB)) as it:
                        for j in range(SUB):
                            n = it * SUB + j
                            pe.wait_ge(ea_in[j], it * 16 + 16)
                            pe.wait_ge(tcopied, n + 1)
                            flat = ea[j][:].rearrange("p t d -> p (t d)")
                            for a in range(pairs_n):
                                w = min(2, CHUNK - 2 * a) * D
                                last = nc.tensor.transpose(ps_t[0:w, a, 0:EP], flat[:, a * 128:a * 128 + w], ident[0:EP, 0:EP])
                            last.then_inc(tposed, 1)
                            pe.wait_ge(tcopied, n + 2)
                            pe.wait_ge(row_done, n + 1)
                            for a in range(pairs_n):
                                w = min(2, CHUNK - 2 * a) * D
                                last = nc.tensor.matmul(ps_q[:, a, 0:w], ea_t[0:w, a, 0:EP], wa2[0:w, 0:w], start=True, stop=True)
                            last.then_inc(q_done, 1)

                @block.gpsimd
                def _(pool):
                    with pool.Fori(0, ET // (CHUNK * SUB)) as it:
                        for j in range(SUB):
                            pool.wait_ge(row_done, it * SUB + j + 2)
                            alone(pool, g)
                            for t in range(CHUNK):
                                nc.gpsimd.indirect_dma_start(
                                    g["rows"], bass.IndirectOffsetOnAxis(ap=posbuf[j][:, t:t + 1], axis=0),
                                    rowbuf[j][:, t, :], None).then_inc(moved[j], 16)
                    for j in range(SUB):
                        pool.wait_ge(moved[j], 16 * CHUNK * (ET // (CHUNK * SUB)))



def alone(engine, g):
    engine.sem_inc(g["passed"], 1)


def clear(nc, sems):
    for s in sems:
        nc.sync.sem_clear(s)
    nc.all_engine_barrier()


def load_windows(sp, g, name, rnd, window, filled, freed, w0, w1):
    sp.sem_inc(freed, NG)
    with ExitStack() as ctx:
        starts = [ctx.enter_context(sp.register(f"{name}_start{i}")) for i in range(NG)]
        with sp.Fori(0, NT) as q:
            for half in range(2):
                sp.reg_load(starts, g["tab"][bass.ds(rnd * NT + q, 1), half * HALF:half * HALF + NG])
                for i in range(NG):
                    w = half * NG + i
                    at_row = sp.snap(starts[i], min_val=0, max_val=N_EDGES)
                    if w % 2 == 0:
                        sp.wait_ge(freed, q * NG + w // 2 + 1)
                    sp.dma_start(window[:, w, :, :],
                                 g["rows"][bass.ds(at_row, WIN), w0:w1].rearrange("(i j) e -> i j e", j=2)
                                 ).then_inc(filled[w // 2], 16)


def lagged(engine, now, later):
    def outer(q, first):
        for n in range(NG):
            now(q, n)
            for lag, step in later:
                if n >= lag:
                    step(q, n - lag)
                elif not first:
                    step(q - 1, NG + n - lag)

    outer(0, True)
    with engine.Fori(1, NT) as q:
        outer(q, False)
    for n in range(NG, NG + max(lag for lag, _ in later)):
        for lag, step in later:
            if n - lag < NG:
                step(NT - 1, n - lag)


def ring(n):
    return 2 if n == NG - 1 else n % 2


def at(tile, i, n=NP):
    return tile[:, bass.ds(i, 1), 0:n].rearrange("p o c -> p (o c)")


def outer_keys(g, q, kind, w0, w1):
    return g["keys"][:, bass.ds(q, 1), kind, w0:w1, :].rearrange("p o w j -> p (o w) j")


def work_out_keys(nc, g, q, target, source, w0, w1):
    static = min(w1, NT)
    n = static - w0
    base, steps = g["tile_bases"], g["tile_steps"]
    nc.vector.scalar_tensor_tensor(outer_keys(g, q, OF_SRC, w0, static), source[:, 0:n, :], base[:, bass.ds(q, 1)],
                                   steps[:, w0:static].unsqueeze(2).to_broadcast([128, n, 2]), ALU.subtract, ALU.subtract)
    last = nc.vector.tensor_tensor(outer_keys(g, q, OF_DST, w0, static), target[:, 0:n, :],
                                   base[:, w0:static].unsqueeze(2).to_broadcast([128, n, 2]), ALU.subtract)
    if w1 == NW:
        nc.vector.tensor_scalar(outer_keys(g, q, OF_SRC, NT, NW), source[:, n:n + 1, :], base[:, bass.ds(q, 1)],
                                steps[:, bass.ds(q, 1)], ALU.subtract, ALU.subtract)
        last = nc.vector.tensor_scalar(outer_keys(g, q, OF_DST, NT, NW), target[:, n:n + 1, :], base[:, bass.ds(q, 1)],
                                       None, ALU.subtract)
    return last


def one_hots(nc, g, out, keys4):
    return nc.vector.tensor_tensor(out, g["iota4"][:], keys4.rearrange("p w j -> p (w j)").unsqueeze(1)
                                   .to_broadcast([128, NP, 4]), ALU.is_equal)


def keys_again(nc, g, rnd):
    with ExitStack() as ctx:
        numbers = ctx.enter_context(nc.sbuf_tensor(f"numbers_{nc.next_id()}", [128, NW, 2, 2], I32))
        filled = g["filled"]
        freed = ctx.enter_context(nc.semaphore(f"freed_k_{nc.next_id()}"))
        name = f"again{nc.next_id()}"
        with nc.Block() as block:
            @block.sync
            def _(sp):
                load_windows(sp, g, name, rnd, numbers, filled, freed, EA_W, EA_W + 2)

            @block.vector
            def _(dve):
                with dve.Fori(0, NT) as q:
                    for i in range(NG):
                        dve.wait_ge(filled[i], q * 32 + 32)
                    of = numbers[:].bitcast(F32)
                    work_out_keys(nc, g, q, of[:, :, :, M_DST], of[:, :, :, M_KEY], 0, NW).then_inc(freed, NG)
        clear(nc, filled + [freed])


def pass_by_src(nc, g, rnd_count):
    h, agg_t, agg_e, cnt = g["h"], g["agg_t"], g["agg_e"], g["cnt_src"]
    with ExitStack() as ctx:
        def sb(name, shape, dt=F32):
            return ctx.enter_context(nc.sbuf_tensor(name, shape, dt))

        def sem(name):
            return ctx.enter_context(nc.semaphore(name))

        window = sb("window0", [128, NW, 2, ROW], I32)
        weight = sb("weight0", [128, 2, NW, 2], BF16)
        by_src = sb("by_src0", [128, NG, NP, 4], BF16)
        by_dst = sb("by_dst0", [128, 3, NP, 4], BF16)
        low_w = sb("low_weights0", [128, NW, 2])
        weighted = sb("weighted0", [128, NG, 3, NP, 4], BF16)
        mat = sb("mat0", [NP, 3, 2, NP])
        staged_t, staged_e = sb("staged_t0", [D, NP]), sb("staged_e0", [NP, 3 * D + 1])
        h_diag = sb("h_diag", [NP, D])
        ps_mat = [ctx.enter_context(nc.psum_tensor(f"ps_mat{i}", [NP, 2, NP], F32)) for i in range(3)]
        ps_t = ctx.enter_context(nc.psum_tensor("ps_agg_t", [D, 512], F32))
        ps_e = ctx.enter_context(nc.psum_tensor("ps_agg_e", [NP, 512], F32))
        filled = g["filled"]
        freed, hots, built, copied, staged, added, pchain, diag_in, keyed, by_dst_done, low_done = (sem(n) for n in (
            "freed0", "onehots0", "built0", "copied0", "staged0", "added0", "pool_chain0", "diag_in0", "keyed0", "by_dst_done0",
            "low_done0"))

        with nc.Block() as block:
            @block.gpsimd
            def _(pool):
                nc.gpsimd.memset(agg_t[:], 0.0)
                nc.gpsimd.memset(agg_e[:], 0.0)
                nc.gpsimd.memset(cnt[:], 0.0)

        with nc.Fori(0, rnd_count) as rnd:
            with nc.Block() as block:
                @block.sync
                def _(sp):
                    load_windows(sp, g, "src", rnd, window, filled, freed, 0, ROW)

                @block.vector
                def _(dve):
                    dve.sem_inc(hots, 2)
                    with dve.Fori(0, NT) as q:
                        for c in range(len(CUTS) - 1):
                            g0, g1 = CUTS[c], CUTS[c + 1]
                            w0, w1 = 2 * g0, 2 * g1
                            for n in range(g0, g1):
                                dve.wait_ge(filled[n], q * 32 + 32)
                            dve.wait_ge(hots, q * NG + g0 + 2)
                            dve.wait_ge(low_done, q * NG + g0 + 1)
                            of = window[:, w0:w1].bitcast(F32)
                            work_out_keys(nc, g, q, of[:, :, :, EA_W + M_DST], of[:, :, :, EA_W + M_KEY], w0, w1)
                            w_parts = window[:, w0:w1].bitcast(BF16)[:, :, :, 2 * (EA_W + M_W):2 * (EA_W + M_W) + 3]
                            nc.vector.tensor_copy(weight[:, :, w0:w1, :].rearrange("p a w j -> p w j a"), w_parts[:, :, :, 0:2])
                            nc.vector.tensor_copy(low_w[:, w0:w1, :].unsqueeze(3), w_parts[:, :, :, 2:3]).then_inc(keyed, 1)
                            dve.wait_ge(keyed, q * (len(CUTS) - 1) + c + 1)
                            for n in range(g0, g1):
                                dve.wait_ge(freed, q * NG + n + 1)
                                dve.wait_ge(hots, q * NG + n + 1)
                                dve.wait_ge(low_done, q * NG + n + 1)
                                one_hots(nc, g, by_dst[:, ring(n)], outer_keys(g, q, OF_DST, 2 * n, 2 * n + 2)).then_inc(by_dst_done, 1)
                                one_hots(nc, g, by_src[:, n], outer_keys(g, q, OF_SRC, 2 * n, 2 * n + 2))
                                dve.wait_ge(by_dst_done, q * NG + n + 1)
                                for a in range(2):
                                    last = nc.vector.tensor_tensor(
                                        weighted[:, n, a], by_dst[:, ring(n)],
                                        weight[:, a, 2 * n:2 * n + 2, :].rearrange("p w j -> p (w j)").unsqueeze(1)
                                        .to_broadcast([128, NP, 4]), ALU.mult)
                                last.then_inc(hots, 1)

                @block.tensor
                def _(pe):
                    def build_matrix(q, n):
                        k = q * NG + n
                        pe.wait_ge(hots, k + 3)
                        pe.wait_ge(low_done, k + 3)
                        pe.wait_ge(copied, k + 1)
                        for w in range(2):
                            for j in range(2):
                                for a in range(3):
                                    s = 2 * w + j
                                    last = nc.tensor.matmul(ps_mat[ring(n)][:, w, :], weighted[:, n, a, :, s],
                                                            by_src[:, n, :, s], start=(j == 0 and a == 0),
                                                            stop=(j == 1 and a == 2))
                        last.then_inc(built, 1)

                    def use_matrix(q, n):
                        k = q * NG + n
                        pe.wait_ge(copied, k + 3)
                        if n == 0:
                            pe.wait_ge(staged, q + 1)
                        if n == NG - 1:
                            pe.wait_ge(diag_in, q + 1)
                        for w in range(2):
                            first, final = n == 0 and w == 0, n == NG - 1 and w == 1
                            nc.tensor.matmul(ps_t[:, 0:NP], h_diag[:] if final else h[:, 2 * n + w, :], mat[:, ring(n), w, :],
                                             start=first, stop=final)
                            for j in range(2):
                                last = nc.tensor.matmul(ps_e[:, 0:3 * D + 1], by_src[:, n, :, 2 * w + j],
                                                        window[:, 2 * n + w, j, 0:EA_W].bitcast(BF16)[:, 0:3 * D + 1],
                                                        start=first and j == 0, stop=final and j == 1)
                        last.then_inc(freed, 1)

                    lagged(pe, build_matrix, [(1, use_matrix)])

                @block.scalar
                def _(act):
                    act.sem_inc(copied, 2)
                    act.sem_inc(low_done, 2)

                    def weigh_low(q, n):
                        act.wait_ge(by_dst_done, q * NG + n + 1)
                        for t in range(4):
                            last = nc.scalar.activation(weighted[:, n, 2, :, t], by_dst[:, ring(n), :, t], ACT.Copy,
                                                        scale=low_w[:, 2 * n + t // 2, t % 2:t % 2 + 1])
                        last.then_inc(low_done, 1)

                    def copy_matrix(q, n):
                        k = q * NG + n
                        act.wait_ge(built, k + 1)
                        act.wait_ge(freed, k + NG - 1)
                        nc.scalar.activation(mat[:, ring(n)], ps_mat[ring(n)][:], ACT.Copy).then_inc(copied, 1)

                    def stage(q, n):
                        if n == NG - 1:
                            act.wait_ge(freed, NG + (q + 1) * NG)
                            act.wait_ge(added, q + 1)
                            nc.scalar.activation(staged_t[:], ps_t[:, 0:NP], ACT.Copy)
                            nc.scalar.activation(staged_e[:], ps_e[:, 0:3 * D + 1], ACT.Copy).then_inc(staged, 1)

                    lagged(act, weigh_low, [(1, copy_matrix), (2, stage)])

                @block.gpsimd
                def _(pool):
                    pool.sem_inc(added, 1)
                    pool.sem_inc(staged, 1)
                    with pool.Fori(0, NT) as q:
                        pool.wait_ge(staged, q + 1)
                        alone(pool, g)
                        nc.gpsimd.tensor_copy(h_diag[:], at(h, q, D)).then_inc(diag_in, 1)
                        pool.wait_ge(staged, q + 2)
                        alone(pool, g)
                        nc.gpsimd.tensor_tensor(at(agg_t, q), at(agg_t, q), staged_t[:], ALU.add)
                        for a in range(3):
                            nc.gpsimd.tensor_tensor(at(agg_e, q, D), at(agg_e, q, D), staged_e[:, a * D:(a + 1) * D],
                                                    ALU.add).then_inc(pchain, 1)
                            pool.wait_ge(pchain, q * 3 + a + 1)
                            alone(pool, g)
                        nc.gpsimd.tensor_tensor(cnt[:, bass.ds(q, 1)], cnt[:, bass.ds(q, 1)],
                                                staged_e[:, 3 * D:3 * D + 1], ALU.add).then_inc(added, 1)
            clear(nc, filled + [freed, hots, built, copied, staged, added, pchain, diag_in, keyed, by_dst_done, low_done])


def pass_by_dst(nc, g, rnd_count):
    agg, cnt, hs, keys = g["agg_1"], g["cnt_dst"], g["hs"], g["keys"]
    with ExitStack() as ctx:
        def sb(name, shape, dt=F32):
            return ctx.enter_context(nc.sbuf_tensor(name, shape, dt))

        def sem(name):
            return ctx.enter_context(nc.semaphore(name))

        turned = sb("keys_by_dst", [128, 2, NW, 2], BF16)
        by_src = sb("by_src1", [128, NG, NP, 4], BF16)
        by_dst = sb("by_dst1", [128, NG, NP, 4], BF16)
        mat = sb("mat1", [NP, 3, 2, NP], BF16)
        staged_e = sb("staged_e1", [NP, 3 * D + 1])
        ps_mat = [ctx.enter_context(nc.psum_tensor(f"ps_cnt_mat{i}", [NP, 2, NP], F32)) for i in range(3)]
        ps_e = ctx.enter_context(nc.psum_tensor("ps_agg_1", [NP, 512], F32))
        freed, hots, built, copied, staged, added, pchain, keyed = (sem(n) for n in (
            "freed1", "onehots1", "built1", "copied1", "staged1", "added1", "pool_chain1", "keyed1"))

        with nc.Block() as block:
            @block.gpsimd
            def _(pool):
                nc.gpsimd.memset(agg[:], 0.0)
                nc.gpsimd.memset(cnt[:], 0.0)

        with nc.Fori(0, rnd_count) as rnd:
            with nc.If(rnd_count > 1):
                keys_again(nc, g, rnd)
            with nc.Else():
                nc.all_engine_barrier()
            with nc.Block() as block:
                @block.vector
                def _(dve):
                    dve.sem_inc(freed, NG)
                    dve.sem_inc(hots, 1)
                    with dve.Fori(0, NT) as d:
                        dve.wait_ge(hots, d * NG + 1)
                        for kind in (OF_SRC, OF_DST):
                            nc.vector.tensor_copy(turned[:, kind, 0:NT, :],
                                                  keys[:, :, kind, bass.ds(d, 1), :].rearrange("p q o j -> p q (o j)"))
                            last = nc.vector.tensor_copy(turned[:, kind, NT:NW, :], outer_keys(g, d, kind, NT, NW))
                        last.then_inc(keyed, 1)
                        dve.wait_ge(keyed, d + 1)
                        for n in range(NG):
                            dve.wait_ge(freed, d * NG + n + 1)
                            one_hots(nc, g, by_dst[:, n], turned[:, OF_DST, 2 * n:2 * n + 2, :])
                            one_hots(nc, g, by_src[:, n], turned[:, OF_SRC, 2 * n:2 * n + 2, :]).then_inc(hots, 1)

                @block.tensor
                def _(pe):
                    def build_matrix(d, n):
                        k = d * NG + n
                        pe.wait_ge(hots, k + 2)
                        pe.wait_ge(copied, k + 1)
                        for w in range(2):
                            for j in range(2):
                                last = nc.tensor.matmul(ps_mat[ring(n)][:, w, :], by_src[:, n, :, 2 * w + j],
                                                        by_dst[:, n, :, 2 * w + j], start=j == 0, stop=j == 1)
                        last.then_inc(built, 1)

                    def use_matrix(d, n):
                        pe.wait_ge(copied, d * NG + n + 3)
                        if n == 0:
                            pe.wait_ge(staged, d)
                        for w in range(2):
                            inner = 2 * n + w if 2 * n + w < NT else d
                            last = nc.tensor.matmul(ps_e[:, 0:3 * D + 1], mat[:, ring(n), w, :], at(hs, inner, 3 * D + 1),
                                                    start=n == 0 and w == 0, stop=n == NG - 1 and w == 1)
                        last.then_inc(freed, 1)

                    lagged(pe, build_matrix, [(1, use_matrix)])

                @block.scalar
                def _(act):
                    act.sem_inc(copied, 2)

                    def copy_matrix(d, n):
                        k = d * NG + n
                        act.wait_ge(built, k + 1)
                        act.wait_ge(freed, k + NG - 1)
                        nc.scalar.activation(mat[:, ring(n)], ps_mat[ring(n)][:], ACT.Copy).then_inc(copied, 1)

                    def stage(d, n):
                        if n == NG - 1:
                            act.wait_ge(freed, NG + (d + 1) * NG)
                            act.wait_ge(added, d + 1)
                            nc.scalar.activation(staged_e[:], ps_e[:, 0:3 * D + 1], ACT.Copy).then_inc(staged, 1)

                    lagged(act, copy_matrix, [(1, stage)])

                @block.gpsimd
                def _(pool):
                    pool.sem_inc(added, 1)
                    with pool.Fori(0, NT) as d:
                        pool.wait_ge(staged, d + 1)
                        alone(pool, g)
                        for a in range(3):
                            nc.gpsimd.tensor_tensor(at(agg, d, D), at(agg, d, D), staged_e[:, a * D:(a + 1) * D],
                                                    ALU.add).then_inc(pchain, 1)
                            pool.wait_ge(pchain, d * 3 + a + 1)
                            alone(pool, g)
                        nc.gpsimd.tensor_tensor(cnt[:, bass.ds(d, 1)], cnt[:, bass.ds(d, 1)],
                                                staged_e[:, 3 * D:3 * D + 1], ALU.add).then_inc(added, 1)
            clear(nc, [freed, hots, built, copied, staged, added, pchain, keyed])


def pass_messages(nc, g, rnd_count):
    agg_t, hs = g["agg_t"], g["hs"]
    with ExitStack() as ctx:
        def sb(name, shape, dt=F32):
            return ctx.enter_context(nc.sbuf_tensor(name, shape, dt))

        def sem(name):
            return ctx.enter_context(nc.semaphore(name))

        window = sb("window3", [128, NW, 2, ROW], I32)
        iota_f = sb("iota_f", [128, NP])
        by_src = sb("by_src3", [128, NG, 4, NP])
        by_dst = sb("by_dst3", [128, NG, NP, 4], BF16)
        turned = sb("turned3", [NP, 3, 4, 128], BF16)
        pre, msg = sb("pre3", [128, 3, 4, D]), sb("msg3", [128, 3, 4, D])
        staged_t = sb("staged_t3", [D, NP])
        ident_b = sb("ident_b", [128, 128], BF16)
        ps_turn = [ctx.enter_context(nc.psum_tensor(f"ps_turn{i}", [NP, 4, 128], BF16)) for i in range(3)]
        ps_p = [ctx.enter_context(nc.psum_tensor(f"ps_p{i}", [128, 4, D], F32)) for i in range(3)]
        ps_t = ctx.enter_context(nc.psum_tensor("ps_msg_t", [D, 512], F32))
        filled = g["filled"]
        freed, hots, turned_s, copied, gathered, pre_done, msg_done, staged, added = (sem(n) for n in (
            "freed3", "onehots3", "turned_sem3", "copied3", "gathered3", "pre_done3", "msg_done3", "staged3", "added3"))

        with nc.Block() as block:
            @block.gpsimd
            def _(pool):
                nc.gpsimd.memset(agg_t[:], 0.0)

            @block.vector
            def _(dve):
                nc.vector.tensor_copy(ident_b[:], g["ident"][:])
                nc.vector.tensor_copy(iota_f[:], g["iota4"][:, :, 0])

        with nc.Fori(0, rnd_count) as rnd:
            with nc.If(rnd_count > 1):
                keys_again(nc, g, rnd)
            with nc.Else():
                nc.all_engine_barrier()
            with nc.Block() as block:
                @block.sync
                def _(sp):
                    load_windows(sp, g, "msg", rnd, window, filled, freed, 0, ROW)

                @block.vector
                def _(dve):
                    def both_one_hots(q, n):
                        dve.wait_ge(freed, q * NG + n + 1)
                        one_hots(nc, g, by_dst[:, n], outer_keys(g, q, OF_DST, 2 * n, 2 * n + 2))
                        of_src = outer_keys(g, q, OF_SRC, 2 * n, 2 * n + 2).rearrange("p w j -> p (w j)")
                        nc.vector.tensor_tensor(by_src[:, n], iota_f[:].unsqueeze(1).to_broadcast([128, 4, NP]),
                                                of_src.unsqueeze(2).to_broadcast([128, 4, NP]), ALU.is_equal).then_inc(hots, 1)

                    def add_q(q, n):
                        k = q * NG + n
                        dve.wait_ge(filled[n], q * 32 + 32)
                        dve.wait_ge(gathered, k + 3)
                        dve.wait_ge(msg_done, k + 1)
                        nc.vector.tensor_tensor(pre[:, ring(n)], ps_p[ring(n)][:],
                                                window[:, 2 * n:2 * n + 2, :, EA_W + META:ROW].bitcast(F32)
                                                .rearrange("p w j d -> p (w j) d"),
                                                ALU.add).then_inc(pre_done, 1)

                    lagged(dve, both_one_hots, [(2, add_q)])

                @block.tensor
                def _(pe):
                    pe.sem_inc(pre_done, 2)
                    pe.sem_inc(gathered, 2)

                    def turn(q, n):
                        k = q * NG + n
                        pe.wait_ge(hots, k + 1)
                        pe.wait_ge(copied, k + 1)
                        for s in range(4):
                            last = nc.tensor.transpose(ps_turn[ring(n)][:, s, :], by_dst[:, n, :, s], ident_b[:])
                        last.then_inc(turned_s, 1)

                    def gather(q, n):
                        k = q * NG + n
                        pe.wait_ge(copied, k + 3)
                        pe.wait_ge(pre_done, k + 1)
                        for w in range(2):
                            part = at(hs, 2 * n + w if 2 * n + w < NT else q, 3 * D)
                            for j in range(2):
                                for a in range(3):
                                    last = nc.tensor.matmul(ps_p[ring(n)][:, 2 * w + j, :], turned[:, ring(n), 2 * w + j, :],
                                                            part[:, a * D:(a + 1) * D], start=a == 0, stop=a == 2)
                        last.then_inc(gathered, 1)

                    def scatter(q, n):
                        k = q * NG + n
                        pe.wait_ge(msg_done, k + 3)
                        if n == 0:
                            pe.wait_ge(staged, q)
                        for s in range(4):
                            last = nc.tensor.matmul(ps_t[:, 0:NP], msg[:, ring(n), s, :], by_src[:, n, s, :],
                                                    start=n == 0 and s == 0, stop=n == NG - 1 and s == 3)
                        last.then_inc(freed, 1)

                    lagged(pe, turn, [(1, gather), (3, scatter)])

                @block.scalar
                def _(act):
                    act.sem_inc(copied, 2)
                    act.sem_inc(msg_done, 2)

                    def copy_turned(q, n):
                        k = q * NG + n
                        act.wait_ge(turned_s, k + 1)
                        act.wait_ge(gathered, k + 1)
                        nc.scalar.activation(turned[:, ring(n)], ps_turn[ring(n)][:], ACT.Copy).then_inc(copied, 1)

                    def relu(q, n):
                        k = q * NG + n
                        act.wait_ge(pre_done, k + 3)
                        act.wait_ge(freed, k + NG - 1)
                        nc.scalar.activation(msg[:, ring(n)], pre[:, ring(n)], ACT.Relu).then_inc(msg_done, 1)

                    def stage(q, n):
                        if n == NG - 1:
                            act.wait_ge(freed, NG + (q + 1) * NG)
                            act.wait_ge(added, q + 1)
                            nc.scalar.activation(staged_t[:], ps_t[:, 0:NP], ACT.Copy).then_inc(staged, 1)

                    lagged(act, copy_turned, [(2, relu), (3, stage)])

                @block.gpsimd
                def _(pool):
                    pool.sem_inc(added, 1)
                    with pool.Fori(0, NT) as q:
                        pool.wait_ge(staged, q + 1)
                        alone(pool, g)
                        nc.gpsimd.tensor_tensor(at(agg_t, q), at(agg_t, q), staged_t[:], ALU.add).then_inc(added, 1)
            clear(nc, filled + [freed, hots, turned_s, copied, gathered, pre_done, msg_done, staged, added])

GROUP = 4


def groups(size):
    return [(i, range(k, min(k + size, NT))) for i, k in enumerate(range(0, NT, size))]


def turn_nodes(nc, g, name, src, width, dst):
    with ExitStack() as ctx:
        ps = [ctx.enter_context(nc.psum_tensor(f"{name}_ps{i}", [width, 512], F32)) for i in range(2)]
        turned, emptied = (ctx.enter_context(nc.semaphore(f"{name}_{n}")) for n in ("turned", "emptied"))
        with nc.Block() as block:
            @block.tensor
            def _(pe):
                for i, tiles in groups(GROUP):
                    if i >= 2:
                        pe.wait_ge(emptied, i - 1)
                    for j, k in enumerate(tiles):
                        last = nc.tensor.transpose(ps[i % 2][:, j * NP:(j + 1) * NP], src[:, k, 0:width],
                                                   g["ident"][0:NP, 0:NP])
                    last.then_inc(turned, 1)

            @block.scalar
            def _(act):
                for i, tiles in groups(GROUP):
                    act.wait_ge(turned, i + 1)
                    n = len(tiles) * NP
                    nc.scalar.activation(dst[0:width, i * GROUP * NP:i * GROUP * NP + n], ps[i % 2][:, 0:n],
                                         ACT.Copy).then_inc(emptied, 1)


def dense(nc, name, terms, m, func, bias, dst):
    with ExitStack() as ctx:
        ps = [ctx.enter_context(nc.psum_tensor(f"{name}_ps{i}", [m, 512], F32)) for i in range(2)]
        product, emptied = (ctx.enter_context(nc.semaphore(f"{name}_{n}")) for n in ("product", "emptied"))
        with nc.Block() as block:
            @block.tensor
            def _(pe):
                for i, tiles in groups(GROUP):
                    if i >= 2:
                        pe.wait_ge(emptied, i - 1)
                    c0, n = i * GROUP * NP, len(tiles) * NP
                    for t, (weights, features) in enumerate(terms):
                        last = nc.tensor.matmul(ps[i % 2][:, 0:n], weights, features[:, c0:c0 + n],
                                                start=t == 0, stop=t == len(terms) - 1)
                    last.then_inc(product, 1)

            @block.scalar
            def _(act):
                for i, tiles in groups(GROUP):
                    act.wait_ge(product, i + 1)
                    c0, n = i * GROUP * NP, len(tiles) * NP
                    if bias is None:
                        done = nc.scalar.activation(dst[:, c0:c0 + n], ps[i % 2][:, 0:n], func)
                    else:
                        done = nc.scalar.activation(dst[:, c0:c0 + n], ps[i % 2][:, 0:n], func, bias=bias)
                    done.then_inc(emptied, 1)


def nodes_out(nc, name, product, vector_steps):
    with ExitStack() as ctx:
        ps = [ctx.enter_context(nc.psum_tensor(f"{name}_ps{i}", [NP, 8, D], F32)) for i in range(4)]
        made, chain = (ctx.enter_context(nc.semaphore(f"{name}_{n}")) for n in ("made", "chain"))
        sqrt_in, sqrt_out = (ctx.enter_context(nc.semaphore(f"{name}_{n}")) for n in ("sqrt_in", "sqrt_out"))
        with nc.Block() as block:
            yield block, sqrt_in, sqrt_out

            @block.tensor
            def _(pe):
                for i, tiles in groups(8):
                    for j, k in enumerate(tiles):
                        last = product(ps[i][:, j, :], k)
                    last.then_inc(made, 1)

            @block.vector
            def _(dve):
                link = linker(dve, chain)
                for i, tiles in groups(8):
                    dve.wait_ge(made, i + 1)
                    vector_steps(link, slice(tiles[0], tiles[-1] + 1), ps[i][:, 0:len(tiles), :])
                vector_steps(link, None, (dve, sqrt_in, sqrt_out))


def on_nodes(row, tiles):
    return row[:].unsqueeze(1).to_broadcast([NP, tiles.stop - tiles.start, D])


def sqrt_of_variance(nc, g, act, sqrt_in, sqrt_out):
    act.wait_ge(sqrt_in, 1)
    nc.scalar.activation(g["std"][:], g["stat"][:], ACT.Sqrt).then_inc(sqrt_out, 1)


def after_l0(nc, g):
    x, h, hs, agg_t, ident = g["x"], g["h"], g["hs"], g["agg_t"], g["ident"]

    def steps(link, tiles, what):
        if tiles is not None:
            link(nc.vector.tensor_tensor(x[:, tiles, :], x[:, tiles, :], what, ALU.add))
            return
        dve, sqrt_in, sqrt_out = what
        layer_norm_relu(nc, dve, link, sqrt_in, sqrt_out, 0, x, h, g["centred"], g["stat"], g["std"])
        split3(nc, link, h[:], hs[:, :, 0:D], hs[:, :, D:2 * D], hs[:, :, 2 * D:3 * D], g["centred"][:])
        link(nc.vector.memset(hs[:, :, 3 * D:3 * D + 1], 1.0))

    for block, sqrt_in, sqrt_out in nodes_out(
            nc, "n0", lambda ps, k: nc.tensor.transpose(ps, agg_t[:, k, 0:NP], ident[0:D, 0:D]), steps):
        @block.scalar
        def _(act):
            sqrt_of_variance(nc, g, act, sqrt_in, sqrt_out)


def after_l1(nc, g):
    x, h, hs, w = g["x"], g["h"], g["hs"], g["w"]
    agg, cnt, inv = g["agg_1"], g["cnt_dst"], g["stat"]
    with ExitStack() as ctx:
        def sb(name, shape, dt=F32):
            return ctx.enter_context(nc.sbuf_tensor(name, shape, dt))

        feat = sb("features_1", [D, N_NODES])
        chain = ctx.enter_context(nc.semaphore("mean1_chain"))
        with nc.Block() as block:
            @block.vector
            def _(dve):
                link = linker(dve, chain)
                link(nc.vector.tensor_scalar(inv[:], cnt[:], 1.0, None, ALU.max))
                link(nc.vector.reciprocal(inv[:], inv[:]))
                nc.vector.tensor_tensor(agg[:], agg[:], inv[:].unsqueeze(2).to_broadcast([NP, NT, D]), ALU.mult)
        turn_nodes(nc, g, "mean1", agg, D, feat)

        cat = sb("cat2", [NP, NT, 2 * D])

        def steps(link, tiles, what):
            if tiles is not None:
                t = g["centred"][:, tiles, :]
                link(nc.vector.tensor_tensor(t, what, on_nodes(w["gb"], tiles), ALU.add))
                link(nc.vector.tensor_scalar(t, t, 0.0, None, ALU.max))
                link(nc.vector.tensor_tensor(x[:, tiles, :], x[:, tiles, :], t, ALU.add))
                return
            dve, sqrt_in, sqrt_out = what
            layer_norm_relu(nc, dve, link, sqrt_in, sqrt_out, 0, x, h, g["centred"], g["stat"], g["std"])
            link(nc.vector.tensor_copy(cat[:, :, 0:D], h[:]))
            link(nc.vector.tensor_copy(cat[:, :, D:2 * D], g["agg_e"][:]))

        for block, sqrt_in, sqrt_out in nodes_out(
                nc, "n1", lambda ps, k: nc.tensor.matmul(ps, feat[:, k * NP:(k + 1) * NP], w["gW"][:], start=True, stop=True),
                steps):
            @block.scalar
            def _(act):
                sqrt_of_variance(nc, g, act, sqrt_in, sqrt_out)

        cat_t, hidden = sb("cat2_t", [2 * D, N_NODES]), sb("hidden2", [128, N_NODES])
        turn_nodes(nc, g, "cat2t", cat, 2 * D, cat_t)
        dense(nc, "mlp2", [(w["W1"][:], cat_t)], 128, ACT.Relu, w["b1"][:], hidden)

        def steps2(link, tiles, what):
            if tiles is not None:
                t = g["centred"][:, tiles, :]
                link(nc.vector.tensor_tensor(t, what, on_nodes(w["b2"], tiles), ALU.add))
                link(nc.vector.tensor_tensor(x[:, tiles, :], x[:, tiles, :], t, ALU.add))
                return
            dve, sqrt_in, sqrt_out = what
            layer_norm_relu(nc, dve, link, sqrt_in, sqrt_out, 0, x, h, g["centred"], g["stat"], g["std"])

        for block, sqrt_in, sqrt_out in nodes_out(
                nc, "n2", lambda ps, k: nc.tensor.matmul(ps, hidden[:, k * NP:(k + 1) * NP], w["W2"][:], start=True, stop=True),
                steps2):
            @block.scalar
            def _(act):
                sqrt_of_variance(nc, g, act, sqrt_in, sqrt_out)
    g["h_t"] = g["sb"]("h3_t", [D, N_NODES])
    turn_nodes(nc, g, "h3t", h, D, g["h_t"])

    def steps3(link, tiles, what):
        if tiles is not None:
            p, rest = hs[:, tiles, :], g["centred"][:, tiles, :]
            split3(nc, link, what, p[:, :, 0:D], p[:, :, D:2 * D], p[:, :, 2 * D:3 * D], rest)

    for block, _, _ in nodes_out(
            nc, "n3", lambda ps, k: nc.tensor.matmul(ps, g["h_t"][:, k * NP:(k + 1) * NP], w["W1a"][:], start=True, stop=True),
            steps3):
        pass


def finish(nc, g):
    x, w, agg_t, cnt, ident = g["x"], g["w"], g["agg_t"], g["cnt_src"], g["ident"]
    with ExitStack() as ctx:
        def sb(name, shape, dt=F32):
            return ctx.enter_context(nc.sbuf_tensor(name, shape, dt))

        inv = g["stat"]
        mean = sb("mean3", [NP, NT, D + 1])
        mean_t, agg_f, hidden = sb("mean3_t", [D + 1, N_NODES]), sb("agg3_f", [D, N_NODES]), sb("hidden3", [D, N_NODES])
        chain, stored = (ctx.enter_context(nc.semaphore(n)) for n in ("mean3_chain", "stored"))
        with nc.Block() as block:
            @block.vector
            def _(dve):
                link = linker(dve, chain)
                link(nc.vector.tensor_scalar(inv[:], cnt[:], 1.0, None, ALU.max))
                link(nc.vector.reciprocal(inv[:], inv[:]))
                link(nc.vector.tensor_tensor(mean[:, :, D:D + 1], cnt[:].unsqueeze(2), inv[:].unsqueeze(2), ALU.mult))

        def steps(link, tiles, what):
            if tiles is not None:
                n = tiles.stop - tiles.start
                link(nc.vector.tensor_tensor(mean[:, tiles, 0:D], what,
                                             inv[:, tiles].unsqueeze(2).to_broadcast([NP, n, D]), ALU.mult))

        for block, _, _ in nodes_out(nc, "m3", lambda ps, k: nc.tensor.transpose(ps, agg_t[:, k, 0:NP], ident[0:D, 0:D]), steps):
            pass
        turn_nodes(nc, g, "mean3t", mean, D + 1, mean_t)
        dense(nc, "agg3", [(w["W1b"][:], mean_t)], D, ACT.Copy, None, agg_f)
        dense(nc, "hid3", [(w["W2a_top"][:], g["h_t"]), (w["W2a_bot"][:], agg_f)], D, ACT.Relu, w["b2a"][:], hidden)

        def steps_out(link, tiles, what):
            if tiles is not None:
                t = g["centred"][:, tiles, :]
                link(nc.vector.tensor_tensor(t, what, on_nodes(w["b2b"], tiles), ALU.add))
                link(nc.vector.tensor_tensor(x[:, tiles, :], x[:, tiles, :], t, ALU.add))

        for block, _, _ in nodes_out(
                nc, "out3", lambda ps, k: nc.tensor.matmul(ps, hidden[:, k * NP:(k + 1) * NP], w["W2b"][:], start=True, stop=True),
                steps_out):
            pass
        with nc.Block() as block:
            @block.sync
            def _(sp):
                sp.dma_start(g["out"].rearrange("(k i) d -> i k d", i=NP), x[:]).then_inc(stored, 16)
                sp.wait_ge(stored, 16)


_INS = ["x", "src", "dst", "edge_attr_64", "edge_weight", "L1_gnn_W", "L1_gnn_b", "L2_gnn_W1", "L2_gnn_b1", "L2_gnn_W2",
        "L2_gnn_b2", "L3_gnn_W1a", "L3_gnn_b1a", "L3_gnn_W1b", "L3_gnn_b1b", "L3_gnn_W2a", "L3_gnn_b2a", "L3_gnn_W2b",
        "L3_gnn_b2b"]


def constants():
    import numpy as np

    tiles = np.arange(NT, dtype=np.float32)
    advance = np.zeros((NT, 32), np.float32)
    for w in range(NW):
        advance[:, w if w < NG else HALF + w - NG] = WIN * (1 + (tiles == w)) if w < NT else 2 * WIN
    n = NT * HB
    at_block = np.arange(n)
    return {
        "identity": np.eye(128, dtype=np.float32),
        "iota_four_times": np.repeat(np.arange(NP), 4).astype(np.float16)[None],
        "key_numbers": np.arange(KW, dtype=np.float32)[None],
        "tile_steps": STEP * tiles[None],
        "tile_bases": NP * tiles[None] - CENTRE,
        "advance": advance,
        "before": np.triu(np.ones((NP, NP), np.float32), 1),
        "same_column": (at_block[:, None] % HB == at_block % HB).astype(np.float32),
        "fold": (at_block[:, None] // HB == np.arange(NT)).astype(np.float32),
    }


def kernel(**inputs):
    import numpy as _np
    import concourse.bacc as _bacc
    from concourse import mybir as _mybir
    from concourse.bass_utils import run_bass_kernel_spmd as _run

    nc = _bacc.Bacc("TRN2", target_bir_lowering=False, num_devices=1)
    arrays, args = {}, []
    given = {name: inputs[name] for name in _INS}
    given.update(constants())
    for name, a in given.items():
        a = _np.ascontiguousarray(a)
        arrays[f"in_{name}_dram"] = a
        args.append(nc.dram_tensor(f"in_{name}_dram", a.shape, _mybir.dt.from_np(a.dtype), kind="ExternalInput").ap())
    args.append(nc.dram_tensor("out_0_dram", (N_NODES, D), F32, kind="ExternalOutput").ap())
    build(nc, *args)
    r = _run(nc, [arrays], core_ids=[0])
    return r.results[0]["out_0_dram"]
```

```python
from contextlib import ExitStack

import concourse.bass as bass
from concourse import mybir
from concourse.alu_op_type import AluOpType as ALU

F32 = mybir.dt.float32
BF16 = mybir.dt.bfloat16
F16 = mybir.dt.float16
I32 = mybir.dt.int32
U16 = mybir.dt.uint16
ACT = mybir.ActivationFunctionType
AX = mybir.AxisListType

N_NODES, N_EDGES, D = 3125, 103125, 64
NT = 25
NP = N_NODES // NT
EP = 125
ET = N_EDGES // EP
CENTRE = (N_NODES - 1) // 2
EPS = 1e-5
MAGIC = 12582912.0

EA_W = (3 * D + 2) // 2
M_DST, M_KEY, M_W = 0, 1, 2
META = 4
STEP = 8192
ROW = EA_W + META + D
PAD_ROWS = 256
N_ROWS = N_EDGES + PAD_ROWS

WIN = 256
NW = NT + 1
NG = NW // 2
CUTS = (0, 2, 7, NG)
HALF = 16
MAX_ROUNDS = -(-N_EDGES // WIN)
OF_SRC, OF_DST = 0, 1
KW = 640
UNROLL = 5
CHUNK, SUB = 11, 3
HB = 3


def layer_norm_relu(nc, dve, link, sqrt_in, sqrt_out, n_before, tiles, x, h, centred, stat, std):
    x, h, centred, stat, std = x[:, tiles, :], h[:, tiles, 0:D], centred[:, tiles, :], stat[:, tiles], std[:, tiles]
    per_node = lambda t: t.unsqueeze(2).to_broadcast([NP, tiles.stop - tiles.start, D])
    link(nc.vector.tensor_reduce(stat, x, AX.X, ALU.add))
    link(nc.vector.tensor_scalar(stat, stat, 1.0 / D, None, ALU.mult))
    link(nc.vector.tensor_tensor(centred, x, per_node(stat), ALU.subtract))
    link(nc.vector.tensor_tensor(h, centred, centred, ALU.mult))
    link(nc.vector.tensor_reduce(stat, h, AX.X, ALU.add))
    nc.vector.tensor_scalar(stat, stat, 1.0 / D, EPS, ALU.mult, ALU.add).then_inc(sqrt_in, 1)
    dve.wait_ge(sqrt_out, n_before + 1)
    link(nc.vector.reciprocal(std, std))
    link(nc.vector.scalar_tensor_tensor(h, centred, 0.0, per_node(std), ALU.max, ALU.mult))


def square_root(nc, act, g, sqrt_in, sqrt_out, n_before, tiles):
    act.wait_ge(sqrt_in, n_before + 1)
    nc.scalar.activation(g["std"][:, tiles], g["stat"][:, tiles], ACT.Sqrt).then_inc(sqrt_out, 1)


def split3(nc, link, whole, hi, mid, lo, rest):
    link(nc.vector.tensor_copy(hi, whole))
    link(nc.vector.tensor_tensor(rest, whole, hi, ALU.subtract))
    link(nc.vector.tensor_copy(mid, rest))
    link(nc.vector.tensor_tensor(lo, rest, mid, ALU.subtract))


def linker(engine, sem):
    count = [0]

    def link(ins):
        count[0] += 1
        ins.then_inc(sem, 1)
        engine.wait_ge(sem, count[0])

    return link


def build(nc, x_in, src_in, dst_in, ea_in, ew_in, gW, gb, W1, b1, W2, b2, W1a, b1a, W1b, b1b, W2a, b2a, W2b, b2b,
          c_ident, c_iota, c_key, c_step, c_base, c_adv, c_tri, c_hmask, c_hfold, out):
    ctx = ExitStack()
    with ctx:
        def sb(name, shape, dt=F32):
            return ctx.enter_context(nc.sbuf_tensor(name, shape, dt))

        def dram(name, shape, dt):
            return nc.dram_tensor(name, shape, dt, kind="Internal").ap()

        rows = dram("sorted_rows", [N_ROWS, ROW], I32)
        tab = dram("window_starts", [MAX_ROUNDS * NT, 32], I32)

        ident = sb("ident", [128, 128])
        iota4 = sb("iota4", [128, NP, 4], F16)
        tile_steps = sb("tile_steps", [128, NT])
        tile_bases = sb("tile_bases", [128, NT])
        keys = sb("keys_of_windows", [128, NT, 2, NW, 2], BF16)
        tri = sb("tri", [NP, NP])
        x = sb("x", [NP, NT, D])
        h = sb("h", [NP, NT, D])
        centred = sb("centred", [NP, NT, D])
        stat = sb("stat", [NP, NT])
        std = sb("std", [NP, NT])
        rounds_i = sb("rounds", [1, 1], I32)
        starts_f = sb("window_starts_f", [NT, 32])
        wa_bot2 = sb("w1a_bot_twice", [128, 128])
        b1a_bc = sb("b1a_on_all", [EP, D])

        w = {"gW": sb("gW", [D, D]), "W1": sb("W1", [2 * D, 128]), "W2": sb("W2", [128, D]), "W1a": sb("W1a_top", [D, D]),
             "W1b": sb("W1b_and_b1b", [D + 1, 2, D]), "W2a": sb("W2a", [2 * D, D]),
             "W2b": sb("W2b", [D, D]), "b1": sb("b1", [128, 1]), "b2a": sb("b2a", [D, 1]),
             "gb": sb("gb_on_all", [NP, D]), "b2": sb("b2_on_all", [NP, D]), "b2b": sb("b2b_on_all", [NP, D])}
        weights_in = ctx.enter_context(nc.semaphore("weights_in"))
        passed = ctx.enter_context(nc.semaphore("passed"))
        consts_in = ctx.enter_context(nc.semaphore("consts_in"))
        filled = [ctx.enter_context(nc.semaphore(f"filled{i}")) for i in range(NG)]

        g = dict(locals())
        g["agg_t"] = sb("agg_t", [D, NT, 128])
        g["agg_e"] = sb("agg_e", [NP, NT, D])
        g["agg_1"] = sb("agg_1", [NP, NT, D])
        g["cnt_src"] = sb("cnt_src", [NP, NT])
        g["cnt_dst"] = sb("cnt_dst", [NP, NT])
        prep(nc, g)
        g["hs"] = sb("h_parts", [NP, NT, 3 * D + 1], BF16)
        rounds = g["rounds"]
        pass_by_src(nc, g, rounds)
        after_l0(nc, g)
        pass_by_dst(nc, g, rounds)
        after_l1(nc, g)
        pass_messages(nc, g, rounds)
        finish(nc, g)


def prep(nc, g):
    tri, ident, x, h = g["tri"], g["ident"], g["x"], g["h"]
    with ExitStack() as ctx:
        def sb(name, shape, dt=F32):
            return ctx.enter_context(nc.sbuf_tensor(name, shape, dt))

        def ps(name, shape, dt=F32):
            return ctx.enter_context(nc.psum_tensor(name, shape, dt))

        def sem(name):
            return ctx.enter_context(nc.semaphore(name))

        steps_n, cols = ET // (CHUNK * SUB), CHUNK * SUB

        meta = sb("meta", [EP, ET, META])
        src_c = sb("src_c", [EP, ET])
        pos_i = sb("pos_i", [EP, ET], I32)
        src_i, dst_i, nxt_i = (sb(n, [EP, ET], I32) for n in ("src_i", "dst_i", "nxt_i"))
        ew = sb("ew", [EP, ET])
        q_f, p_f, tmp = sb("q_f", [EP, ET]), sb("p_f", [EP, ET]), sb("tmp", [EP, ET])
        q16, p16, key16 = sb("q16", [EP, ET], F16), sb("p16", [EP, ET], F16), sb("key16", [EP, ET], F16)
        mask = sb("mask", [EP, 2, ET], BF16)
        scan = sb("scan", [EP, 2, ET])
        ones_w = sb("ones_w", [EP, ET], BF16)
        keys, keys16 = sb("keys", [EP, KW]), sb("keys16", [EP, NT], F16)
        tot, col, incl, off = (sb(n, [EP, KW]) for n in ("tot", "col", "incl", "off"))
        ones_m = sb("ones_m", [EP, EP])
        viol, flag, mul, nkeys_f = (sb(n, [EP, 1]) for n in ("viol", "flag", "mul", "nkeys_f"))
        nkeys_i = sb("nkeys_i", [1, 1], I32)
        oh_q, oh_p = sb("oh_q", [EP, NT, cols], BF16), sb("oh_p", [EP, NT, cols], BF16)
        zeros = sb("zeros", [EP, NT * HB], BF16)
        hmask, hfold = sb("hmask", [NT * HB, NT * HB]), sb("hfold", [NT * HB, NT])
        h75 = sb("h75", [NT * HB, NT * HB])
        cnt, start, half = sb("cnt", [NT, NT]), sb("start", [NT, NT]), sb("half", [NT, NT])
        row, base, diag = sb("row", [NT, 1]), sb("base", [NT, 1]), sb("diag", [NT, 1])
        r_max = sb("r_max", [1, 1])
        advance, starts_i = sb("advance", [NT, 32]), sb("starts_i", [NT, 32], I32)
        ea = [sb(f"ea{j}", [EP, CHUNK, D]) for j in range(SUB)]
        rowbuf = [sb(f"rowbuf{j}", [EP, CHUNK, ROW], I32) for j in range(SUB)]
        posbuf = [sb(f"posbuf{j}", [EP, CHUNK], I32) for j in range(SUB)]
        rest = sb("rest", [EP, CHUNK, D])
        pad = sb("pad", [128, 2, ROW], I32)
        pairs_n = (CHUNK + 1) // 2
        ea_t = sb("ea_t", [128, pairs_n, 128])

        ps_t, ps_q = ps("ps_t", [128, 8, 128]), ps("ps_q", [EP, 8, 128])
        ps_excl = ps_t[0:EP].rearrange("p (c a) b -> p c (a b)", c=2)
        ps_col = ps_q[:].rearrange("p (c a) b -> p c (a b)", c=2)
        ps_hist = ps("ps_hist", [NT * HB, NT * HB])
        ps_small = ps("ps_small", [EP, 512])

        ints_in, next_in, ew_in, adv_in, w_in, pad_out, starts_out = (sem(n) for n in (
            "ints_in", "next_in", "ew_in", "adv_in", "w_in", "pad_out", "starts_out"))
        ea_in = [sem(f"ea_in{j}") for j in range(SUB)]
        moved = [sem(f"moved{j}") for j in range(SUB)]
        next_pad, w_zero, exp_done, flag_in, flag_sum, counted, tot_ready, off_ready, off_used, ranked = (sem(n) for n in (
            "next_pad", "w_zero", "exp_done", "flag_in", "flag_sum", "counted", "tot_ready", "off_ready", "off_used", "ranked"))
        tposed, tcopied, q_done, hi_done, row_done, chain, pad_ready, hist_onehots, hist_added, hist_done = (sem(n) for n in (
            "turned", "turned_copied", "q_done", "hi_done", "row_done", "row_chain", "pad_ready", "hist_onehots", "hist_added",
            "hist_done"))
        h75_ready, folded, row_ready, base_ready, rmax_ready, rmax_t, rounds_ready, starts_ready, stored_once, table_chain = (
            sem(n) for n in ("h75_ready", "folded", "row_ready", "base_ready", "rmax_ready", "rmax_t", "rounds_ready",
                             "starts_ready", "stored_once", "table_chain"))
        dch, sqrt_in, sqrt_out = sem("dve_chain_order"), sem("sqrt_in0"), sem("sqrt_out0")

        ea_v = g["ea_in"].rearrange("(i t) d -> i t d", t=ET)
        wa2 = g["wa_bot2"]

        def parts(j, a):
            return rowbuf[j][:].bitcast(BF16)[:, :, a * D:(a + 1) * D]

        with nc.Block() as block:
            @block.sync
            def _(sp):
                sp.dma_start(src_i[:], g["src_in"].rearrange("(i t) -> i t", t=ET)).then_inc(ints_in, 16)
                sp.dma_start(dst_i[:], g["dst_in"].rearrange("(i t) -> i t", t=ET)).then_inc(ints_in, 16)
                sp.wait_ge(next_pad, 1)
                body = (EP - 1) * ET
                sp.dma_start(nxt_i[0:EP - 1, :], g["dst_in"][1:1 + body].rearrange("(i t) -> i t", t=ET)).then_inc(next_in, 16)
                sp.dma_start(nxt_i[EP - 1:EP, 0:ET - 1], g["dst_in"][1 + body:N_EDGES].unsqueeze(0)).then_inc(next_in, 16)
                sp.dma_start(ew[:], g["ew_in"].rearrange("(i t) -> i t", t=ET)).then_inc(ew_in, 16)
                for to, of in ((ident[:], g["c_ident"]), (tri[:], g["c_tri"]), (hmask[:], g["c_hmask"]),
                               (hfold[:], g["c_hfold"]), (keys[:], g["c_key"].to_broadcast([EP, KW])),
                               (g["iota4"][:], g["c_iota"].rearrange("o (j s) -> o j s", s=4).to_broadcast([128, NP, 4])),
                               (g["tile_bases"][:], g["c_base"].to_broadcast([128, NT])),
                               (g["tile_steps"][:], g["c_step"].to_broadcast([128, NT])),
                               (x[:], g["x_in"].rearrange("(k i) d -> i k d", i=NP)),
                               (g["b1a_bc"][:], g["b1a"].unsqueeze(0).to_broadcast([EP, D]))):
                    sp.dma_start(to, of).then_inc(g["consts_in"], 16)
                sp.wait_ge(w_zero, 1)
                sp.dma_start(wa2[0:D, 0:D], g["W1a"][D:2 * D, :]).then_inc(w_in, 16)
                sp.dma_start(wa2[D:128, D:128], g["W1a"][D:2 * D, :]).then_inc(w_in, 16)
                w = g["w"]
                on_all = lambda b: b.unsqueeze(0).to_broadcast([NP, D])
                for to, of in ((w["gW"][:], g["gW"]), (w["W1"][:], g["W1"]), (w["W2"][:], g["W2"]),
                               (w["W1a"][:], g["W1a"][0:D, :]), (w["W1b"][0:D, 1, :], g["W1b"]),
                               (w["W1b"][D:D + 1, 1, :], g["b1b"].unsqueeze(0)), (w["W2a"][:], g["W2a"]), (w["W2b"][:], g["W2b"]),
                               (w["b1"][:], g["b1"].unsqueeze(1)), (w["b2a"][:], g["b2a"].unsqueeze(1)),
                               (w["gb"][:], on_all(g["gb"])), (w["b2"][:], on_all(g["b2"])),
                               (w["b2b"][:], on_all(g["b2b"]))):
                    sp.dma_start(to, of).then_inc(g["weights_in"], 16)
                sp.dma_start(advance[:], g["c_adv"]).then_inc(adv_in, 16)
                with sp.Fori(0, steps_n) as it:
                    for j in range(SUB):
                        sp.wait_ge(row_done, it * SUB + 1)
                        sp.dma_start(ea[j][:], ea_v[:, bass.ds(it * SUB * CHUNK + j * CHUNK, CHUNK), :]).then_inc(ea_in[j], 16)
                sp.wait_ge(pad_ready, 1)
                sp.dma_start(g["rows"][N_EDGES:N_ROWS, :].rearrange("(i j) w -> i j w", j=2), pad[:]).then_inc(pad_out, 16)
                sp.sem_inc(stored_once, 1)
                sp.wait_ge(rounds_ready, 1)
                rounds = sp.value_load(g["rounds_i"][0:1, 0:1], min_val=1, max_val=MAX_ROUNDS)
                with sp.Fori(0, rounds) as r:
                    sp.wait_ge(starts_ready, r + 1)
                    sp.dma_start(g["tab"][bass.ds(r * NT, NT), :], starts_i[:]).then_inc(starts_out, 16)
                    sp.wait_ge(starts_out, r * 16 + 16)
                    sp.sem_inc(stored_once, 1)
                sp.wait_ge(pad_out, 16)
                sp.wait_ge(g["weights_in"], 16 * 13)

            @block.scalar
            def _(act):
                act.wait_ge(ew_in, 16)
                nc.scalar.activation(ew[:], ew[:], ACT.Exp, scale=-1.0).then_inc(exp_done, 1)
                act.sem_inc(tcopied, 1)

                def step(it, again):
                    for j in range(SUB):
                        n = it * SUB + j
                        act.wait_ge(ea_in[j], it * 16 + 16)
                        if again:
                            act.wait_ge(moved[j], it * 16 * CHUNK)
                        nc.scalar.activation(parts(j, 0), ea[j][:], ACT.Copy).then_inc(hi_done, 1)
                        act.wait_ge(tposed, n + 1)
                        act.wait_ge(q_done, n + 1)
                        nc.scalar.activation(ea_t[:, 0:pairs_n - 1, 0:EP], ps_t[:, 0:pairs_n - 1, 0:EP], ACT.Copy)
                        nc.scalar.activation(ea_t[0:D, pairs_n - 1, 0:EP], ps_t[0:D, pairs_n - 1, 0:EP], ACT.Copy).then_inc(tcopied, 1)

                step(0, False)
                with act.Fori(1, steps_n) as it:
                    step(it, True)
                square_root(nc, act, g, sqrt_in, sqrt_out, 0, slice(0, NT))

            @block.vector
            def _(dve):
                link = linker(dve, dch)
                nc.vector.memset(nxt_i[:, ET - 1:ET], N_NODES - 1).then_inc(next_pad, 1)
                nc.vector.memset(wa2[:], 0.0).then_inc(w_zero, 1)
                nc.vector.memset(ones_m[:], 1.0)
                nc.vector.memset(ones_w[:], 1.0)
                nc.vector.memset(zeros[:], 0.0)
                nc.vector.memset(g["starts_f"][:], 0.0)
                nc.vector.memset(tot[:], 0.0)
                nc.vector.memset(g["w"]["W1b"][:, 0, :], 0.0)
                for j in range(SUB):
                    nc.vector.memset(rowbuf[j][:].bitcast(BF16)[:, :, 3 * D:3 * D + 1], 1.0)
                    nc.vector.memset(rowbuf[j][:].bitcast(BF16)[:, :, 3 * D + 1:3 * D + 2], 0.0)
                link(nc.vector.memset(pad[:], 0))
                nc.vector.memset(pad[:].bitcast(F32)[:, :, EA_W:EA_W + META], -float(N_NODES)).then_inc(pad_ready, 1)
                dve.sem_inc(row_done, 1)
                dve.sem_inc(counted, 1)
                dve.sem_inc(ranked, 1)
                dve.wait_ge(ints_in, 32)

                def tile_of(tile_f, node_i, centre_to=None):
                    link(nc.vector.tensor_copy(tmp[:], node_i[:]))
                    if centre_to is not None:
                        nc.vector.tensor_scalar(centre_to, tmp[:], -float(CENTRE), None, ALU.add)
                    link(nc.vector.tensor_scalar(tile_f, tmp[:], -float(NP // 2), 1.0 / NP, ALU.add, ALU.mult))
                    link(nc.vector.tensor_scalar(tile_f, tile_f, MAGIC, None, ALU.add))
                    link(nc.vector.tensor_scalar(tile_f, tile_f, -MAGIC, None, ALU.add))

                tile_of(p_f[:], dst_i, meta[:, :, M_DST])
                dve.wait_ge(next_in, 32)
                tile_of(scan[:, 0], nxt_i)
                link(nc.vector.tensor_tensor(tmp[:], p_f[:], scan[:, 0], ALU.is_gt))
                nc.vector.tensor_reduce(viol[:], tmp[:], AX.X, ALU.max).then_inc(flag_in, 1)
                dve.wait_ge(flag_in, 1)
                tile_of(q_f[:], src_i, src_c[:])
                nc.vector.tensor_copy(q16[:], q_f[:])
                nc.vector.scalar_tensor_tensor(meta[:, :, M_KEY], p_f[:], float(STEP), src_c[:], ALU.mult, ALU.add)
                nc.vector.tensor_copy(p16[:], p_f[:])
                dve.wait_ge(g["consts_in"], 16 * 10)
                nc.vector.tensor_copy(keys16[:], keys[:, 0:NT])
                dve.wait_ge(flag_sum, 1)
                link(nc.vector.tensor_scalar(flag[:], ps_small[:, 0:1], 1.0, None, ALU.min))
                fives = NT // UNROLL
                nc.vector.tensor_scalar(nkeys_f[:], flag[:], float((NT - 1) * fives), float(fives), ALU.mult, ALU.add)
                link(nc.vector.tensor_scalar(mul[:], flag[:], float(NT - 1), 1.0, ALU.mult, ALU.add))
                link(nc.vector.tensor_copy(nkeys_i[:], nkeys_f[0:1, :]))
                link(nc.vector.tensor_scalar(tmp[:], p_f[:], flag[:], None, ALU.mult))
                link(nc.vector.tensor_scalar(scan[:, 0], q_f[:], mul[:], None, ALU.mult))
                link(nc.vector.tensor_tensor(key16[:], tmp[:], scan[:, 0], ALU.add))
                key_steps = dve.value_load(nkeys_i[0:1, 0:1], min_val=fives, max_val=fives * NT)
                with dve.Fori(0, key_steps) as k:
                    for j in range(UNROLL):
                        if j:
                            dve.wait_ge(counted, k * UNROLL + j)
                        nc.vector.tensor_scalar(mask[:, j % 2], key16[:], keys[:, bass.ds(k * UNROLL + j, 1)], 0.0, ALU.is_equal,
                                                ALU.add, accum_out=tot[:, bass.ds(k * UNROLL + j, 1)]).then_inc(counted, 1)
                    dve.wait_ge(counted, k * UNROLL + UNROLL + 1)
                dve.sem_inc(tot_ready, 1)
                dve.wait_ge(exp_done, 1)
                w_parts = meta[:].bitcast(BF16)[:, :, 2 * M_W:2 * M_W + 4]
                nc.vector.memset(w_parts[:, :, 3:4], 0.0)
                link(nc.vector.tensor_copy(w_parts[:, :, 0:1], ew[:].unsqueeze(2)))
                link(nc.vector.tensor_tensor(tmp[:].unsqueeze(2), ew[:].unsqueeze(2), w_parts[:, :, 0:1], ALU.subtract))
                link(nc.vector.tensor_copy(w_parts[:, :, 1:2], tmp[:].unsqueeze(2)))
                link(nc.vector.tensor_tensor(w_parts[:, :, 2:3], tmp[:].unsqueeze(2), w_parts[:, :, 1:2], ALU.subtract))
                dve.wait_ge(off_ready, 1)
                for c in range(2):
                    link(nc.vector.tensor_copy(col[:, c * 320:c * 320 + 320], ps_col[:, c, 0:320]))
                link(nc.vector.tensor_tensor_scan(incl[:], ones_w[:, 0:KW], col[:], 0.0, ALU.mult, ALU.add))
                link(nc.vector.tensor_tensor(incl[:], incl[:], col[:], ALU.subtract))
                for c in range(2):
                    sl = slice(c * 320, c * 320 + 320)
                    link(nc.vector.scalar_tensor_tensor(off[:, sl], incl[:, sl], -1.0, ps_excl[:, c, 0:320],
                                                        ALU.add, ALU.add))
                dve.sem_inc(off_used, 1)

                def key_mask(k, j):
                    nc.vector.tensor_scalar(mask[:, j % 2], key16[:], keys[:, bass.ds(k * UNROLL + j, 1)], None,
                                            ALU.is_equal).then_inc(ranked, 1)

                def key_count(k, j):
                    nc.vector.tensor_tensor_scan(scan[:, j % 2], ones_w[:], mask[:, j % 2], off[:, bass.ds(k * UNROLL + j, 1)],
                                                 ALU.mult, ALU.add).then_inc(ranked, 1)

                def take(k, j):
                    alone(dve, g)
                    nc.vector.copy_predicated(tmp[:], mask[:, j % 2].bitcast(U16), scan[:, j % 2]).then_inc(ranked, 1)

                with dve.Fori(0, key_steps) as k:
                    n = k * (3 * UNROLL) + 1
                    dve.wait_ge(ranked, n)
                    key_mask(k, 0)
                    dve.wait_ge(ranked, n + 1)
                    key_count(k, 0)
                    for j in range(1, UNROLL):
                        dve.wait_ge(ranked, n + 3 * j - 2)
                        key_mask(k, j)
                        dve.wait_ge(ranked, n + 3 * j - 1)
                        take(k, j - 1)
                        dve.wait_ge(ranked, n + 3 * j)
                        key_count(k, j)
                    dve.wait_ge(ranked, n + 3 * UNROLL - 1)
                    take(k, UNROLL - 1)
                dve.wait_ge(ranked, key_steps * (3 * UNROLL) + 1)
                link(nc.vector.tensor_copy(pos_i[:], tmp[:]))

                with dve.Fori(0, steps_n) as it:
                    for j in range(SUB):
                        n = it * SUB + j
                        tile0 = it * cols + j * CHUNK
                        dve.wait_ge(hi_done, n + 1)
                        nc.vector.tensor_tensor(rest[:], ea[j][:], parts(j, 0), ALU.subtract).then_inc(chain, 1)
                        nc.vector.tensor_copy(rowbuf[j][:].bitcast(F32)[:, :, EA_W:EA_W + META],
                                              meta[:, bass.ds(tile0, CHUNK), :])
                        dve.wait_ge(chain, n * 3 + 1)
                        nc.vector.tensor_copy(parts(j, 1), rest[:]).then_inc(chain, 1)
                        nc.vector.tensor_copy(posbuf[j][:], pos_i[:, bass.ds(tile0, CHUNK)])
                        dve.wait_ge(chain, n * 3 + 2)
                        nc.vector.tensor_tensor(parts(j, 2), rest[:], parts(j, 1), ALU.subtract).then_inc(chain, 1)
                        dve.wait_ge(chain, n * 3 + 3)
                        dve.wait_ge(q_done, n + 2)
                        nc.vector.tensor_tensor(
                            rowbuf[j][:].bitcast(F32)[:, :, EA_W + META:ROW],
                            ps_q[:].rearrange("p a (b d) -> p (a b) d", d=D)[:, 0:CHUNK, :],
                            g["b1a_bc"][:].unsqueeze(1).to_broadcast([EP, CHUNK, D]), ALU.add).then_inc(row_done, 1)
                    dve.wait_ge(hist_added, it + 1)
                    for out, of in ((oh_q, q16), (oh_p, p16)):
                        last = nc.vector.tensor_tensor(out[:], of[:, bass.ds(it * cols, cols)].unsqueeze(1).to_broadcast([EP, NT, cols]),
                                                       keys16[:].unsqueeze(2).to_broadcast([EP, NT, cols]), ALU.is_equal)
                    last.then_inc(hist_onehots, 1)

                dve.wait_ge(hist_done, 1)
                nc.vector.tensor_tensor(h75[:], ps_hist[:], hmask[:], ALU.mult).then_inc(h75_ready, 1)
                dve.wait_ge(folded, 1)
                link(nc.vector.tensor_reduce(cnt[:], ps_small[0:NT, 128:128 + NT * HB].rearrange("q (p b) -> q p b", b=HB),
                                             AX.X, ALU.add))
                nc.vector.tensor_reduce(row[:], cnt[:], AX.X, ALU.add).then_inc(row_ready, 1)
                dve.wait_ge(base_ready, 1)
                link(nc.vector.tensor_copy(base[:], ps_small[0:NT, 256:257]))
                link(nc.vector.tensor_tensor_scan(start[:], ones_w[0:NT, 0:NT], cnt[:], base[:], ALU.mult, ALU.add))
                link(nc.vector.tensor_tensor(start[:], start[:], cnt[:], ALU.subtract))
                link(nc.vector.tensor_tensor(half[:], start[:], ident[0:NT, 0:NT], ALU.mult))
                link(nc.vector.tensor_reduce(diag[:], half[:], AX.X, ALU.add))
                sf = g["starts_f"]
                nc.vector.tensor_scalar(sf[:, HALF + NG - 1:HALF + NG], diag[:], float(WIN), float(N_EDGES), ALU.add, ALU.min)
                nc.vector.tensor_copy(sf[:, 0:NG], start[:, 0:NG])
                nc.vector.tensor_copy(sf[:, HALF:HALF + NT - NG], start[:, NG:NT])
                link(nc.vector.tensor_scalar(half[:], ident[0:NT, 0:NT], -0.5, 1.0, ALU.mult, ALU.add))
                link(nc.vector.tensor_tensor(half[:], half[:], cnt[:], ALU.mult))
                dve.wait_ge(row_ready, 1)
                nc.vector.tensor_reduce(row[:], half[:], AX.X, ALU.max).then_inc(rmax_ready, 1)
                dve.wait_ge(rmax_t, 1)
                link(nc.vector.tensor_reduce(r_max[:], ps_small[0:1, 384:384 + NT], AX.X, ALU.max))
                link(nc.vector.tensor_scalar(r_max[:], r_max[:], WIN / 2 - 0.25, 1.0 / WIN, ALU.add, ALU.mult))
                link(nc.vector.tensor_scalar(r_max[:], r_max[:], MAGIC, None, ALU.add))
                link(nc.vector.tensor_scalar(r_max[:], r_max[:], -MAGIC, 1.0, ALU.add, ALU.max))
                link(nc.vector.tensor_copy(g["rounds_i"][:], r_max[:]))
                dve.sem_inc(rounds_ready, 1)
                rounds = dve.value_load(g["rounds_i"][0:1, 0:1], min_val=1, max_val=MAX_ROUNDS)
                dve.wait_ge(adv_in, 16)
                with dve.Fori(0, rounds) as r:
                    dve.wait_ge(stored_once, r + 1)
                    nc.vector.tensor_copy(starts_i[:], sf[:]).then_inc(starts_ready, 1)
                    dve.wait_ge(starts_ready, r + 1)
                    nc.vector.tensor_tensor(sf[:], sf[:], advance[:], ALU.add).then_inc(table_chain, 1)
                    dve.wait_ge(table_chain, r * 2 + 1)
                    nc.vector.tensor_scalar(sf[:], sf[:], float(N_EDGES), None, ALU.min).then_inc(table_chain, 1)
                    dve.wait_ge(table_chain, r * 2 + 2)
                layer_norm_relu(nc, dve, link, sqrt_in, sqrt_out, 0, slice(0, NT), x, h, g["centred"], g["stat"], g["std"])
                for sums in ("agg_t", "agg_e", "agg_1", "cnt_src", "cnt_dst"):
                    nc.vector.memset(g[sums][:], 0.0)

            @block.tensor
            def _(pe):
                pe.wait_ge(flag_in, 1)
                nc.tensor.matmul(ps_small[:, 0:1], ones_m[:], viol[:], start=True, stop=True).then_inc(flag_sum, 1)
                pe.wait_ge(tot_ready, 1)
                for c in range(2):
                    nc.tensor.matmul(ps_excl[:, c, 0:320], tri[:], tot[:, c * 320:c * 320 + 320], start=True, stop=True)
                    last = nc.tensor.matmul(ps_col[:, c, 0:320], ones_m[:], tot[:, c * 320:c * 320 + 320], start=True, stop=True)
                last.then_inc(off_ready, 1)
                pe.wait_ge(off_used, 1)

                pe.sem_inc(q_done, 1)
                pe.sem_inc(hist_added, 1)
                pe.wait_ge(w_in, 32)
                nc.tensor.matmul(ps_hist[:], zeros[:], zeros[:], start=True, stop=False)
                with pe.Fori(0, steps_n) as it:
                    for j in range(SUB):
                        n = it * SUB + j
                        pe.wait_ge(ea_in[j], it * 16 + 16)
                        pe.wait_ge(tcopied, n + 1)
                        flat = ea[j][:].rearrange("p t d -> p (t d)")
                        for a in range(pairs_n):
                            w = min(2, CHUNK - 2 * a) * D
                            last = nc.tensor.transpose(ps_t[0:w, a, 0:EP], flat[:, a * 128:a * 128 + w], ident[0:EP, 0:EP])
                        last.then_inc(tposed, 1)
                        pe.wait_ge(tcopied, n + 2)
                        pe.wait_ge(row_done, n + 1)
                        for a in range(pairs_n):
                            w = min(2, CHUNK - 2 * a) * D
                            last = nc.tensor.matmul(ps_q[:, a, 0:w], ea_t[0:w, a, 0:EP], wa2[0:w, 0:w], start=True, stop=True)
                        last.then_inc(q_done, 1)
                    pe.wait_ge(hist_onehots, it + 1)
                    for t in range(cols // HB):
                        one_q, one_p = (o[:].rearrange("i k (b t) -> i (k b) t", b=HB)[:, :, t] for o in (oh_q, oh_p))
                        last = nc.tensor.matmul(ps_hist[:], one_q, one_p, start=False, stop=False)
                    last.then_inc(hist_added, 1)
                nc.tensor.matmul(ps_hist[:], zeros[:], zeros[:], start=False, stop=True).then_inc(hist_done, 1)
                pe.wait_ge(h75_ready, 1)
                nc.tensor.matmul(ps_small[0:NT, 128:128 + NT * HB], hfold[:], h75[:], start=True, stop=True).then_inc(folded, 1)
                pe.wait_ge(row_ready, 1)
                nc.tensor.matmul(ps_small[0:NT, 256:257], tri[0:NT, 0:NT], row[:], start=True, stop=True).then_inc(base_ready, 1)
                pe.wait_ge(rmax_ready, 1)
                nc.tensor.transpose(ps_small[0:1, 384:384 + NT], row[:], ident[0:NT, 0:NT]).then_inc(rmax_t, 1)

            @block.gpsimd
            def _(pool):
                with pool.Fori(0, steps_n) as it:
                    for j in range(SUB):
                        pool.wait_ge(row_done, it * SUB + j + 2)
                        alone(pool, g)
                        for t in range(CHUNK):
                            nc.gpsimd.indirect_dma_start(
                                g["rows"], bass.IndirectOffsetOnAxis(ap=posbuf[j][:, t:t + 1], axis=0),
                                rowbuf[j][:, t, :], None).then_inc(moved[j], 16)
                for j in range(SUB):
                    pool.wait_ge(moved[j], 16 * CHUNK * steps_n)
        g["rounds"] = nc.values_load(g["rounds_i"][0:1, 0:1], min_val=1, max_val=MAX_ROUNDS)


def alone(engine, g):
    engine.sem_inc(g["passed"], 1)


def clear(nc, sems):
    for s in sems:
        nc.sync.sem_clear(s)
    nc.all_engine_barrier()


def load_windows(sp, g, name, rnd, window, filled, freed, w0, w1):
    sp.sem_inc(freed, NG)
    with ExitStack() as ctx:
        starts = [ctx.enter_context(sp.register(f"{name}_start{i}")) for i in range(NG)]
        with sp.Fori(0, NT) as q:
            for half in range(2):
                sp.reg_load(starts, g["tab"][bass.ds(rnd * NT + q, 1), half * HALF:half * HALF + NG])
                for i in range(NG):
                    w = half * NG + i
                    at_row = sp.snap(starts[i], min_val=0, max_val=N_EDGES)
                    if w % 2 == 0:
                        sp.wait_ge(freed, q * NG + w // 2 + 1)
                    sp.dma_start(window[:, w, :, :],
                                 g["rows"][bass.ds(at_row, WIN), w0:w1].rearrange("(i j) e -> i j e", j=2)
                                 ).then_inc(filled[w // 2], 16)


def lagged(engine, now, later):
    def outer(q, first):
        for n in range(NG):
            now(q, n)
            for lag, step in later:
                if n >= lag:
                    step(q, n - lag)
                elif not first:
                    step(q - 1, NG + n - lag)

    outer(0, True)
    with engine.Fori(1, NT) as q:
        outer(q, False)
    for n in range(NG, NG + max(lag for lag, _ in later)):
        for lag, step in later:
            if n - lag < NG:
                step(NT - 1, n - lag)


def ring(n):
    return 2 if n == NG - 1 else n % 2


def at(tile, i, n=NP):
    return tile[:, bass.ds(i, 1), 0:n].rearrange("p o c -> p (o c)")


def outer_keys(g, q, kind, w0, w1):
    return g["keys"][:, bass.ds(q, 1), kind, w0:w1, :].rearrange("p o w j -> p (o w) j")


def work_out_keys(nc, g, q, target, source, w0, w1):
    static = min(w1, NT)
    n = static - w0
    base, steps = g["tile_bases"], g["tile_steps"]
    nc.vector.scalar_tensor_tensor(outer_keys(g, q, OF_SRC, w0, static), source[:, 0:n, :], base[:, bass.ds(q, 1)],
                                   steps[:, w0:static].unsqueeze(2).to_broadcast([128, n, 2]), ALU.subtract, ALU.subtract)
    last = nc.vector.tensor_tensor(outer_keys(g, q, OF_DST, w0, static), target[:, 0:n, :],
                                   base[:, w0:static].unsqueeze(2).to_broadcast([128, n, 2]), ALU.subtract)
    if w1 == NW:
        nc.vector.tensor_scalar(outer_keys(g, q, OF_SRC, NT, NW), source[:, n:n + 1, :], base[:, bass.ds(q, 1)],
                                steps[:, bass.ds(q, 1)], ALU.subtract, ALU.subtract)
        last = nc.vector.tensor_scalar(outer_keys(g, q, OF_DST, NT, NW), target[:, n:n + 1, :], base[:, bass.ds(q, 1)],
                                       None, ALU.subtract)
    return last


def one_hots(nc, g, out, keys4):
    return nc.vector.tensor_tensor(out, g["iota4"][:], keys4.rearrange("p w j -> p (w j)").unsqueeze(1)
                                   .to_broadcast([128, NP, 4]), ALU.is_equal)


def both_one_hots(nc, g, out, keys):
    return nc.vector.tensor_tensor(
        out, g["iota4"][:].unsqueeze(1).to_broadcast([128, 2, NP, 4]),
        keys.rearrange("p k w j -> p k (w j)").unsqueeze(2).to_broadcast([128, 2, NP, 4]), ALU.is_equal)


def keys_again(nc, g, rnd):
    with ExitStack() as ctx:
        numbers = ctx.enter_context(nc.sbuf_tensor(f"numbers_{nc.next_id()}", [128, NW, 2, 2], I32))
        filled = g["filled"]
        freed = ctx.enter_context(nc.semaphore(f"freed_k_{nc.next_id()}"))
        name = f"again{nc.next_id()}"
        with nc.Block() as block:
            @block.sync
            def _(sp):
                load_windows(sp, g, name, rnd, numbers, filled, freed, EA_W, EA_W + 2)

            @block.vector
            def _(dve):
                with dve.Fori(0, NT) as q:
                    for i in range(NG):
                        dve.wait_ge(filled[i], q * 32 + 32)
                    of = numbers[:].bitcast(F32)
                    work_out_keys(nc, g, q, of[:, :, :, M_DST], of[:, :, :, M_KEY], 0, NW).then_inc(freed, NG)
        clear(nc, filled + [freed])


def pass_by_src(nc, g, rnd_count):
    h, agg_t, agg_e, cnt = g["h"], g["agg_t"], g["agg_e"], g["cnt_src"]
    with ExitStack() as ctx:
        def sb(name, shape, dt=F32):
            return ctx.enter_context(nc.sbuf_tensor(name, shape, dt))

        def sem(name):
            return ctx.enter_context(nc.semaphore(name))

        window = sb("window0", [128, NW, 2, ROW], I32)
        weight = sb("weight0", [128, 2, NW, 2], BF16)
        hot = sb("one_hots_0", [128, NG, 2, NP, 4], BF16)
        low_w = sb("low_weights0", [128, NW, 2])
        weighted = sb("weighted0", [128, NG, 3, NP, 4], BF16)
        mat = sb("mat0", [NP, 3, 2, NP])
        staged_t, staged_e = sb("staged_t0", [D, NP]), sb("staged_e0", [NP, 3 * D + 1])
        h_diag = sb("h_diag", [NP, D])
        ps_mat = [ctx.enter_context(nc.psum_tensor(f"ps_mat{i}", [NP, 2, NP], F32)) for i in range(3)]
        ps_t = ctx.enter_context(nc.psum_tensor("ps_agg_t", [D, 512], F32))
        ps_e = ctx.enter_context(nc.psum_tensor("ps_agg_e", [NP, 512], F32))
        filled = g["filled"]
        freed, hots, built, copied, staged, added, pchain, diag_in, keyed, made, low_done = (sem(n) for n in (
            "freed0", "onehots0", "built0", "copied0", "staged0", "added0", "pool_chain0", "diag_in0", "keyed0", "made0",
            "low_done0"))

        with nc.Fori(0, rnd_count) as rnd:
            with nc.Block() as block:
                @block.sync
                def _(sp):
                    load_windows(sp, g, "src", rnd, window, filled, freed, 0, ROW)

                @block.vector
                def _(dve):
                    dve.sem_inc(hots, 2)

                    def make(q, n):
                        k = q * NG + n
                        if n in CUTS:
                            w0, w1 = 2 * n, 2 * CUTS[CUTS.index(n) + 1]
                            for i in range(w0 // 2, w1 // 2):
                                dve.wait_ge(filled[i], q * 32 + 32)
                            dve.wait_ge(hots, k + 1)
                            dve.wait_ge(low_done, q * NG + w1 // 2)
                            of = window[:, w0:w1].bitcast(F32)
                            work_out_keys(nc, g, q, of[:, :, :, EA_W + M_DST], of[:, :, :, EA_W + M_KEY], w0, w1)
                            w_parts = window[:, w0:w1].bitcast(BF16)[:, :, :, 2 * (EA_W + M_W):2 * (EA_W + M_W) + 3]
                            nc.vector.tensor_copy(weight[:, :, w0:w1, :].rearrange("p a w j -> p w j a"), w_parts[:, :, :, 0:2])
                            nc.vector.tensor_copy(low_w[:, w0:w1, :].unsqueeze(3), w_parts[:, :, :, 2:3]).then_inc(keyed, 1)
                            dve.wait_ge(keyed, q * (len(CUTS) - 1) + CUTS.index(n) + 1)
                        dve.wait_ge(freed, k + 1)
                        both_one_hots(nc, g, hot[:, n], g["keys"][:, bass.ds(q, 1), :, 2 * n:2 * n + 2, :]
                                      .rearrange("p o k w j -> p (o k) w j")).then_inc(made, 1)

                    def weigh(q, n):
                        dve.wait_ge(made, q * NG + n + 1)
                        nc.vector.tensor_tensor(
                            weighted[:, n, 0:2], hot[:, n, OF_DST].unsqueeze(1).to_broadcast([128, 2, NP, 4]),
                            weight[:, :, 2 * n:2 * n + 2, :].rearrange("p a w j -> p a (w j)").unsqueeze(2)
                            .to_broadcast([128, 2, NP, 4]), ALU.mult).then_inc(hots, 1)

                    lagged(dve, make, [(1, weigh)])

                @block.tensor
                def _(pe):
                    def build_matrix(q, n):
                        k = q * NG + n
                        pe.wait_ge(hots, k + 3)
                        pe.wait_ge(low_done, k + NG + 1)
                        pe.wait_ge(copied, k + 1)
                        for w in range(2):
                            for j in range(2):
                                for a in range(3):
                                    s = 2 * w + j
                                    last = nc.tensor.matmul(ps_mat[ring(n)][:, w, :], weighted[:, n, a, :, s],
                                                            hot[:, n, OF_SRC, :, s], start=(j == 0 and a == 0),
                                                            stop=(j == 1 and a == 2))
                        last.then_inc(built, 1)

                    def use_matrix(q, n):
                        k = q * NG + n
                        pe.wait_ge(copied, k + 3)
                        if n == 0:
                            pe.wait_ge(staged, q + 1)
                        if n == NG - 1:
                            pe.wait_ge(diag_in, q + 1)
                        for w in range(2):
                            first, final = n == 0 and w == 0, n == NG - 1 and w == 1
                            nc.tensor.matmul(ps_t[:, 0:NP], h_diag[:] if final else h[:, 2 * n + w, :], mat[:, ring(n), w, :],
                                             start=first, stop=final)
                            for j in range(2):
                                last = nc.tensor.matmul(ps_e[:, 0:3 * D + 1], hot[:, n, OF_SRC, :, 2 * w + j],
                                                        window[:, 2 * n + w, j, 0:EA_W].bitcast(BF16)[:, 0:3 * D + 1],
                                                        start=first and j == 0, stop=final and j == 1)
                        last.then_inc(freed, 1)

                    lagged(pe, build_matrix, [(1, use_matrix)])

                @block.scalar
                def _(act):
                    act.sem_inc(copied, 2)
                    act.sem_inc(low_done, NG)

                    def weigh_low(q, n):
                        act.wait_ge(made, q * NG + n + 1)
                        for t in range(4):
                            last = nc.scalar.activation(weighted[:, n, 2, :, t], hot[:, n, OF_DST, :, t], ACT.Copy,
                                                        scale=low_w[:, 2 * n + t // 2, t % 2:t % 2 + 1])
                        last.then_inc(low_done, 1)

                    def copy_matrix(q, n):
                        k = q * NG + n
                        act.wait_ge(built, k + 1)
                        act.wait_ge(freed, k + NG - 1)
                        nc.scalar.activation(mat[:, ring(n)], ps_mat[ring(n)][:], ACT.Copy).then_inc(copied, 1)

                    def stage(q, n):
                        if n == NG - 1:
                            act.wait_ge(freed, NG + (q + 1) * NG)
                            act.wait_ge(added, q + 1)
                            nc.scalar.activation(staged_t[:], ps_t[:, 0:NP], ACT.Copy)
                            nc.scalar.activation(staged_e[:], ps_e[:, 0:3 * D + 1], ACT.Copy).then_inc(staged, 1)

                    lagged(act, weigh_low, [(1, copy_matrix), (2, stage)])

                @block.gpsimd
                def _(pool):
                    pool.sem_inc(added, 1)
                    pool.sem_inc(staged, 1)
                    with pool.Fori(0, NT) as q:
                        pool.wait_ge(staged, q + 1)
                        alone(pool, g)
                        nc.gpsimd.tensor_copy(h_diag[:], at(h, q, D)).then_inc(diag_in, 1)
                        pool.wait_ge(staged, q + 2)
                        alone(pool, g)
                        nc.gpsimd.tensor_tensor(at(agg_t, q), at(agg_t, q), staged_t[:], ALU.add)
                        for a in range(3):
                            nc.gpsimd.tensor_tensor(at(agg_e, q, D), at(agg_e, q, D), staged_e[:, a * D:(a + 1) * D],
                                                    ALU.add).then_inc(pchain, 1)
                            pool.wait_ge(pchain, q * 3 + a + 1)
                            alone(pool, g)
                        nc.gpsimd.tensor_tensor(cnt[:, bass.ds(q, 1)], cnt[:, bass.ds(q, 1)],
                                                staged_e[:, 3 * D:3 * D + 1], ALU.add).then_inc(added, 1)
            clear(nc, filled + [freed, hots, built, copied, staged, added, pchain, diag_in, keyed, made, low_done])


def pass_by_dst(nc, g, rnd_count):
    agg, cnt, hs, keys = g["agg_1"], g["cnt_dst"], g["hs"], g["keys"]
    with ExitStack() as ctx:
        def sb(name, shape, dt=F32):
            return ctx.enter_context(nc.sbuf_tensor(name, shape, dt))

        def sem(name):
            return ctx.enter_context(nc.semaphore(name))

        by_target = sb("keys_by_target", [128, NT, 2, NW, 2], BF16)
        hot = sb("one_hots_1", [128, NG, 2, NP, 4], BF16)
        mat = sb("mat1", [NP, 3, 2, NP], BF16)
        staged_e = sb("staged_e1", [NP, 3 * D + 1])
        ps_mat = [ctx.enter_context(nc.psum_tensor(f"ps_cnt_mat{i}", [NP, 2, NP], F32)) for i in range(3)]
        ps_e = ctx.enter_context(nc.psum_tensor("ps_agg_1", [NP, 512], F32))
        freed, hots, built, copied, staged, added, pchain, keyed = (sem(n) for n in (
            "freed1", "onehots1", "built1", "copied1", "staged1", "added1", "pool_chain1", "keyed1"))

        with nc.Fori(0, rnd_count) as rnd:
            with nc.If(rnd_count > 1):
                keys_again(nc, g, rnd)
            with nc.Else():
                nc.all_engine_barrier()
            with nc.Block() as block:
                @block.vector
                def _(dve):
                    dve.sem_inc(freed, NG)
                    for kind in (OF_SRC, OF_DST):
                        nc.vector.tensor_copy(by_target[:, :, kind, 0:NT, :],
                                              keys[:, :, kind, 0:NT, :].rearrange("p q d j -> p d q j"))
                    nc.vector.tensor_copy(by_target[:, :, :, NT, :], keys[:, :, :, NT, :]).then_inc(keyed, 1)
                    dve.wait_ge(keyed, 1)
                    with dve.Fori(0, NT) as d:
                        for n in range(NG):
                            dve.wait_ge(freed, d * NG + n + 1)
                            both_one_hots(nc, g, hot[:, n], by_target[:, bass.ds(d, 1), :, 2 * n:2 * n + 2, :]
                                          .rearrange("p o k w j -> p (o k) w j")).then_inc(hots, 1)

                @block.tensor
                def _(pe):
                    def build_matrix(d, n):
                        k = d * NG + n
                        pe.wait_ge(hots, k + 1)
                        pe.wait_ge(copied, k + 1)
                        for w in range(2):
                            for j in range(2):
                                last = nc.tensor.matmul(ps_mat[ring(n)][:, w, :], hot[:, n, OF_SRC, :, 2 * w + j],
                                                        hot[:, n, OF_DST, :, 2 * w + j], start=j == 0, stop=j == 1)
                        last.then_inc(built, 1)

                    def use_matrix(d, n):
                        pe.wait_ge(copied, d * NG + n + 3)
                        if n == 0:
                            pe.wait_ge(staged, d)
                        for w in range(2):
                            inner = 2 * n + w if 2 * n + w < NT else d
                            last = nc.tensor.matmul(ps_e[:, 0:3 * D + 1], mat[:, ring(n), w, :], at(hs, inner, 3 * D + 1),
                                                    start=n == 0 and w == 0, stop=n == NG - 1 and w == 1)
                        last.then_inc(freed, 1)

                    lagged(pe, build_matrix, [(1, use_matrix)])

                @block.scalar
                def _(act):
                    act.sem_inc(copied, 2)

                    def copy_matrix(d, n):
                        k = d * NG + n
                        act.wait_ge(built, k + 1)
                        act.wait_ge(freed, k + NG - 1)
                        nc.scalar.activation(mat[:, ring(n)], ps_mat[ring(n)][:], ACT.Copy).then_inc(copied, 1)

                    def stage(d, n):
                        if n == NG - 1:
                            act.wait_ge(freed, NG + (d + 1) * NG)
                            act.wait_ge(added, d + 1)
                            nc.scalar.activation(staged_e[:], ps_e[:, 0:3 * D + 1], ACT.Copy).then_inc(staged, 1)

                    lagged(act, copy_matrix, [(1, stage)])

                @block.gpsimd
                def _(pool):
                    pool.sem_inc(added, 1)
                    with pool.Fori(0, NT) as d:
                        pool.wait_ge(staged, d + 1)
                        alone(pool, g)
                        for a in range(3):
                            nc.gpsimd.tensor_tensor(at(agg, d, D), at(agg, d, D), staged_e[:, a * D:(a + 1) * D],
                                                    ALU.add).then_inc(pchain, 1)
                            pool.wait_ge(pchain, d * 3 + a + 1)
                            alone(pool, g)
                        nc.gpsimd.tensor_tensor(cnt[:, bass.ds(d, 1)], cnt[:, bass.ds(d, 1)],
                                                staged_e[:, 3 * D:3 * D + 1], ALU.add).then_inc(added, 1)
            clear(nc, [freed, hots, built, copied, staged, added, pchain, keyed])


def pass_messages(nc, g, rnd_count):
    agg_t, hs = g["agg_t"], g["hs"]
    with ExitStack() as ctx:
        def sb(name, shape, dt=F32):
            return ctx.enter_context(nc.sbuf_tensor(name, shape, dt))

        def sem(name):
            return ctx.enter_context(nc.semaphore(name))

        window = sb("window3", [128, NW, 2, ROW], I32)
        iota_f = sb("iota_f", [128, NP])
        by_src = sb("by_src3", [128, NG, 4, NP])
        by_dst = sb("by_dst3", [128, NG, NP, 4], BF16)
        turned = sb("turned3", [NP, 3, 4, 128], BF16)
        pre, msg = sb("pre3", [128, 3, 4, D]), sb("msg3", [128, 3, 4, D])
        staged_t = sb("staged_t3", [D, NP])
        ident_b = sb("ident_b", [128, 128], BF16)
        ps_turn = [ctx.enter_context(nc.psum_tensor(f"ps_turn{i}", [NP, 4, 128], BF16)) for i in range(3)]
        ps_p = [ctx.enter_context(nc.psum_tensor(f"ps_p{i}", [128, 4, D], F32)) for i in range(3)]
        ps_t = ctx.enter_context(nc.psum_tensor("ps_msg_t", [D, 512], F32))
        filled = g["filled"]
        freed, hots, turned_s, copied, gathered, pre_done, msg_done, staged, added = (sem(n) for n in (
            "freed3", "onehots3", "turned_sem3", "copied3", "gathered3", "pre_done3", "msg_done3", "staged3", "added3"))

        with nc.Block() as block:
            @block.vector
            def _(dve):
                nc.vector.tensor_copy(ident_b[:], g["ident"][:])
                nc.vector.tensor_copy(iota_f[:], g["iota4"][:, :, 0])

        with nc.Fori(0, rnd_count) as rnd:
            with nc.If(rnd_count > 1):
                keys_again(nc, g, rnd)
            with nc.Else():
                nc.all_engine_barrier()
            with nc.Block() as block:
                @block.sync
                def _(sp):
                    load_windows(sp, g, "msg", rnd, window, filled, freed, 0, ROW)

                @block.vector
                def _(dve):
                    def make(q, n):
                        dve.wait_ge(freed, q * NG + n + 1)
                        one_hots(nc, g, by_dst[:, n], outer_keys(g, q, OF_DST, 2 * n, 2 * n + 2))
                        of_src = outer_keys(g, q, OF_SRC, 2 * n, 2 * n + 2).rearrange("p w j -> p (w j)")
                        nc.vector.tensor_tensor(by_src[:, n], iota_f[:].unsqueeze(1).to_broadcast([128, 4, NP]),
                                                of_src.unsqueeze(2).to_broadcast([128, 4, NP]), ALU.is_equal).then_inc(hots, 1)

                    def add_q(q, n):
                        k = q * NG + n
                        dve.wait_ge(filled[n], q * 32 + 32)
                        dve.wait_ge(gathered, k + 3)
                        dve.wait_ge(msg_done, k + 1)
                        nc.vector.tensor_tensor(pre[:, ring(n)], ps_p[ring(n)][:],
                                                window[:, 2 * n:2 * n + 2, :, EA_W + META:ROW].bitcast(F32)
                                                .rearrange("p w j d -> p (w j) d"),
                                                ALU.add).then_inc(pre_done, 1)

                    lagged(dve, make, [(2, add_q)])

                @block.tensor
                def _(pe):
                    pe.sem_inc(pre_done, 2)
                    pe.sem_inc(gathered, 2)

                    def turn(q, n):
                        k = q * NG + n
                        pe.wait_ge(hots, k + 1)
                        pe.wait_ge(copied, k + 1)
                        for s in range(4):
                            last = nc.tensor.transpose(ps_turn[ring(n)][:, s, :], by_dst[:, n, :, s], ident_b[:])
                        last.then_inc(turned_s, 1)

                    def gather(q, n):
                        k = q * NG + n
                        pe.wait_ge(copied, k + 3)
                        pe.wait_ge(pre_done, k + 1)
                        for w in range(2):
                            part = at(hs, 2 * n + w if 2 * n + w < NT else q, 3 * D)
                            for j in range(2):
                                for a in range(3):
                                    last = nc.tensor.matmul(ps_p[ring(n)][:, 2 * w + j, :], turned[:, ring(n), 2 * w + j, :],
                                                            part[:, a * D:(a + 1) * D], start=a == 0, stop=a == 2)
                        last.then_inc(gathered, 1)

                    def scatter(q, n):
                        k = q * NG + n
                        pe.wait_ge(msg_done, k + 3)
                        if n == 0:
                            pe.wait_ge(staged, q)
                        for s in range(4):
                            last = nc.tensor.matmul(ps_t[:, 0:NP], msg[:, ring(n), s, :], by_src[:, n, s, :],
                                                    start=n == 0 and s == 0, stop=n == NG - 1 and s == 3)
                        last.then_inc(freed, 1)

                    lagged(pe, turn, [(1, gather), (3, scatter)])

                @block.scalar
                def _(act):
                    act.sem_inc(copied, 2)
                    act.sem_inc(msg_done, 2)

                    def copy_turned(q, n):
                        k = q * NG + n
                        act.wait_ge(turned_s, k + 1)
                        act.wait_ge(gathered, k + 1)
                        nc.scalar.activation(turned[:, ring(n)], ps_turn[ring(n)][:], ACT.Copy).then_inc(copied, 1)

                    def relu(q, n):
                        k = q * NG + n
                        act.wait_ge(pre_done, k + 3)
                        act.wait_ge(freed, k + NG - 1)
                        nc.scalar.activation(msg[:, ring(n)], pre[:, ring(n)], ACT.Relu).then_inc(msg_done, 1)

                    def stage(q, n):
                        if n == NG - 1:
                            act.wait_ge(freed, NG + (q + 1) * NG)
                            act.wait_ge(added, q + 1)
                            nc.scalar.activation(staged_t[:], ps_t[:, 0:NP], ACT.Copy).then_inc(staged, 1)

                    lagged(act, copy_turned, [(2, relu), (3, stage)])

                @block.gpsimd
                def _(pool):
                    pool.sem_inc(added, 1)
                    with pool.Fori(0, NT) as q:
                        pool.wait_ge(staged, q + 1)
                        alone(pool, g)
                        nc.gpsimd.tensor_tensor(at(agg_t, q), at(agg_t, q), staged_t[:], ALU.add).then_inc(added, 1)
            clear(nc, filled + [freed, hots, turned_s, copied, gathered, pre_done, msg_done, staged, added])

GROUP = 4
BANK = 8


def groups(size):
    return [(i, range(k, min(k + size, NT))) for i, k in enumerate(range(0, NT, size))]


def on_nodes(row, tiles):
    return row[:].unsqueeze(1).to_broadcast([NP, tiles.stop - tiles.start, D])


def bank_tiles():
    return [(b, slice(tiles[0], tiles[-1] + 1)) for b, tiles in groups(BANK)]


def banks(nc, ctx, name, n, shape, dt=F32):
    return [ctx.enter_context(nc.psum_tensor(f"{name}{i}", shape, dt)) for i in range(n)]


def turn_group(nc, g, bank, src, width, tiles):
    for j, k in enumerate(tiles):
        last = nc.tensor.transpose(bank[0:width, j * NP:(j + 1) * NP], src[:, k, 0:width], g["ident"][0:NP, 0:NP])
    return last


def dense_group(nc, bank, terms, tiles):
    c0, n = tiles[0] * NP, len(tiles) * NP
    for t, (weights, features) in enumerate(terms):
        last = nc.tensor.matmul(bank[:, 0:n], weights, features[:, c0:c0 + n], start=t == 0, stop=t == len(terms) - 1)
    return last


def empty_group(nc, dst, bank, tiles, func, **more):
    c0, n = tiles[0] * NP, len(tiles) * NP
    m = dst.shape[0]
    return nc.scalar.activation(dst[:, c0:c0 + n], bank[0:m, 0:n], func, **more)


def by_node(nc, outs, features, weights, tiles, sem):
    for k in tiles:
        ins = nc.tensor.matmul(outs[k // BANK][:, k % BANK, :], features[:, k * NP:(k + 1) * NP], weights, start=True, stop=True)
        if k % BANK == BANK - 1 or k == NT - 1:
            ins.then_inc(sem, 1)


def after_l0(nc, g):
    x, h, hs, agg_t, centred = g["x"], g["h"], g["hs"], g["agg_t"], g["centred"]
    with ExitStack() as ctx:
        ps_out = banks(nc, ctx, "l0_out", 4, [NP, BANK, D])
        sums_out, chain, sqrt_in, sqrt_out = (ctx.enter_context(nc.semaphore(n)) for n in (
            "l0_sums_out", "l0_chain", "l0_sqrt_in", "l0_sqrt_out"))
        with nc.Block() as block:
            @block.tensor
            def _(pe):
                for b, t in bank_tiles():
                    for k in range(t.start, t.stop):
                        last = nc.tensor.transpose(ps_out[b][:, k % BANK, :], agg_t[:, k, 0:NP], g["ident"][0:D, 0:D])
                    last.then_inc(sums_out, 1)

            @block.scalar
            def _(act):
                square_root(nc, act, g, sqrt_in, sqrt_out, 0, slice(0, NT))

            @block.gpsimd
            def _(pool):
                nc.gpsimd.memset(hs[:, :, 3 * D:3 * D + 1], 1.0)

            @block.vector
            def _(dve):
                link = linker(dve, chain)
                for b, t in bank_tiles():
                    dve.wait_ge(sums_out, b + 1)
                    link(nc.vector.tensor_tensor(x[:, t, :], x[:, t, :], ps_out[b][:, 0:t.stop - t.start, :], ALU.add))
                layer_norm_relu(nc, dve, link, sqrt_in, sqrt_out, 0, slice(0, NT), x, h, centred, g["stat"], g["std"])
                split3(nc, link, h[:], hs[:, :, 0:D], hs[:, :, D:2 * D], hs[:, :, 2 * D:3 * D], centred[:])


def after_l1(nc, g):
    x, h, hs, w, centred = g["x"], g["h"], g["hs"], g["w"], g["centred"]
    agg, cnt, inv = g["agg_1"], g["cnt_dst"], g["stat"]
    g["cat3_t"] = g["sb"]("cat3_t", [2 * D, N_NODES])
    h_t = g["cat3_t"][0:D, :]
    with ExitStack() as ctx:
        def sb(name, shape, dt=F32):
            return ctx.enter_context(nc.sbuf_tensor(name, shape, dt))

        feat = sb("mean1_t", [D, N_NODES])
        cat, cat_t, hidden = sb("cat2", [NP, NT, 2 * D]), sb("cat2_t", [2 * D, N_NODES]), sb("hidden2", [128, N_NODES])
        ps_turn, ps_dense = banks(nc, ctx, "n_turn", 2, [128, 512]), banks(nc, ctx, "n_dense", 2, [128, 512])
        ps_out = banks(nc, ctx, "n_out", 4, [NP, BANK, D])
        (means, turned, emptied, made1, normed2, dense_done, dense_used, made2, normed3, made3, chain, sqrt_in, sqrt_out,
         edge_sums) = (ctx.enter_context(nc.semaphore(n)) for n in (
            "means", "n_turned", "n_emptied", "made1", "normed2", "dense_done", "dense_used", "made2", "normed3", "made3",
            "node_chain", "node_sqrt_in", "node_sqrt_out", "edge_sums"))
        fours, n4, n_banks = groups(GROUP), len(groups(GROUP)), len(groups(BANK))
        with nc.Block() as block:
            @block.gpsimd
            def _(pool):
                nc.gpsimd.tensor_copy(cat[:, :, D:2 * D], g["agg_e"][:]).then_inc(edge_sums, 1)
                nc.gpsimd.memset(g["agg_t"][:], 0.0)

            @block.vector
            def _(dve):
                link = linker(dve, chain)
                link(nc.vector.tensor_scalar(inv[:], cnt[:], 1.0, None, ALU.max))
                link(nc.vector.reciprocal(inv[:], inv[:]))
                for _, tiles in groups(BANK):
                    t = slice(tiles[0], tiles[-1] + 1)
                    nc.vector.tensor_tensor(agg[:, t, :], agg[:, t, :], inv[:, t].unsqueeze(2).to_broadcast([NP, len(tiles), D]),
                                            ALU.mult).then_inc(means, 1)
                for b, t in bank_tiles():
                    c = centred[:, t, :]
                    dve.wait_ge(made1, b + 1)
                    link(nc.vector.tensor_tensor(c, ps_out[b][:, 0:t.stop - t.start, :], on_nodes(w["gb"], t), ALU.add))
                    link(nc.vector.scalar_tensor_tensor(x[:, t, :], c, 0.0, x[:, t, :], ALU.max, ALU.add))
                    layer_norm_relu(nc, dve, link, sqrt_in, sqrt_out, b, t, x, cat, centred, g["stat"], g["std"])
                    dve.sem_inc(normed2, 1)
                for b, t in bank_tiles():
                    c = centred[:, t, :]
                    dve.wait_ge(made2, b + 1)
                    link(nc.vector.tensor_tensor(c, ps_out[b][:, 0:t.stop - t.start, :], on_nodes(w["b2"], t), ALU.add))
                    link(nc.vector.tensor_tensor(x[:, t, :], x[:, t, :], c, ALU.add))
                    layer_norm_relu(nc, dve, link, sqrt_in, sqrt_out, n_banks + b, t, x, h, centred, g["stat"], g["std"])
                    dve.sem_inc(normed3, 1)
                for b, t in bank_tiles():
                    p = hs[:, t, :]
                    dve.wait_ge(made3, b + 1)
                    split3(nc, link, ps_out[b][:, 0:t.stop - t.start, :], p[:, :, 0:D], p[:, :, D:2 * D], p[:, :, 2 * D:3 * D],
                           centred[:, t, :])

            @block.tensor
            def _(pe):
                for i in range(n4 + 1):
                    if i < n4:
                        pe.wait_ge(means, fours[i][1][-1] // BANK + 1)
                        if i >= 2:
                            pe.wait_ge(emptied, i - 1)
                        turn_group(nc, g, ps_turn[i % 2], agg, D, fours[i][1]).then_inc(turned, 1)
                    if i >= 1:
                        pe.wait_ge(emptied, i)
                        by_node(nc, ps_out, feat, w["gW"][:], fours[i - 1][1], made1)
                pe.wait_ge(edge_sums, 1)
                for i in range(n4 + 2):
                    if i < n4:
                        pe.wait_ge(normed2, fours[i][1][-1] // BANK + 1)
                        pe.wait_ge(emptied, n4 + i - 1)
                        turn_group(nc, g, ps_turn[(n4 + i) % 2], cat, 2 * D, fours[i][1]).then_inc(turned, 1)
                    if 1 <= i <= n4:
                        pe.wait_ge(emptied, n4 + i)
                        if i >= 3:
                            pe.wait_ge(dense_used, i - 2)
                        dense_group(nc, ps_dense[(i - 1) % 2], [(w["W1"][:], cat_t)], fours[i - 1][1]).then_inc(dense_done, 1)
                    if i >= 2:
                        pe.wait_ge(dense_used, i - 1)
                        by_node(nc, ps_out, hidden, w["W2"][:], fours[i - 2][1], made2)
                for i in range(n4 + 1):
                    if i < n4:
                        pe.wait_ge(normed3, fours[i][1][-1] // BANK + 1)
                        pe.wait_ge(emptied, 2 * n4 + i - 1)
                        turn_group(nc, g, ps_turn[(2 * n4 + i) % 2], h, D, fours[i][1]).then_inc(turned, 1)
                    if i >= 1:
                        pe.wait_ge(emptied, 2 * n4 + i)
                        by_node(nc, ps_out, h_t, w["W1a"][:], fours[i - 1][1], made3)

            @block.scalar
            def _(act):
                for i, tiles in fours:
                    act.wait_ge(turned, i + 1)
                    empty_group(nc, feat, ps_turn[i % 2], tiles, ACT.Copy).then_inc(emptied, 1)
                tiles_of = [t for _, t in bank_tiles()]
                root = lambda n: square_root(nc, act, g, sqrt_in, sqrt_out, n, tiles_of[n % n_banks])
                root(0)
                for i in range(n4 + 1):
                    if i % 2 == 1 and (i + 1) // 2 < n_banks:
                        root((i + 1) // 2)
                    if i < n4:
                        act.wait_ge(turned, n4 + i + 1)
                        empty_group(nc, cat_t, ps_turn[(n4 + i) % 2], fours[i][1], ACT.Copy).then_inc(emptied, 1)
                    if i >= 1:
                        act.wait_ge(dense_done, i)
                        empty_group(nc, hidden, ps_dense[(i - 1) % 2], fours[i - 1][1], ACT.Relu, bias=w["b1"][:]).then_inc(dense_used, 1)
                    if i >= 5 and i % 2 == 1:
                        root(n_banks + (i - 5) // 2)
                for i, tiles in fours:
                    if i % 2 == 1 and (i + 3) // 2 < n_banks:
                        root(n_banks + (i + 3) // 2)
                    act.wait_ge(turned, 2 * n4 + i + 1)
                    empty_group(nc, h_t, ps_turn[(2 * n4 + i) % 2], tiles, ACT.Copy).then_inc(emptied, 1)


def finish(nc, g):
    x, w, agg_t, cnt, centred, ident, cat_t = g["x"], g["w"], g["agg_t"], g["cnt_src"], g["centred"], g["ident"], g["cat3_t"]
    with ExitStack() as ctx:
        def sb(name, shape, dt=F32):
            return ctx.enter_context(nc.sbuf_tensor(name, shape, dt))

        inv = g["stat"]
        mean = sb("mean3", [NP, NT, D + 1])
        mean_t, hidden = sb("mean3_t", [D + 1, N_NODES]), sb("hidden3", [D, N_NODES])
        ps_turn, ps_out = banks(nc, ctx, "f_turn", 2, [128, 512]), banks(nc, ctx, "f_out", 4, [NP, BANK, D])
        (ps_agg,), (ps_hid,) = banks(nc, ctx, "f_agg", 1, [2 * D, 512]), banks(nc, ctx, "f_hid", 1, [D, 512])
        sums_out, means, turned, emptied, agg_done, agg_used, hid_done, hid_used, made, chain, ready, stored = (
            ctx.enter_context(nc.semaphore(n)) for n in (
                "sums_out", "f_means", "f_turned", "f_emptied", "agg_done", "agg_used", "hid_done", "hid_used", "f_made",
                "f_chain", "out_ready", "stored"))
        fours, n4 = groups(GROUP), len(groups(GROUP))
        out = g["out"].rearrange("(k i) d -> i k d", i=NP)
        with nc.Block() as block:
            @block.vector
            def _(dve):
                link = linker(dve, chain)
                link(nc.vector.tensor_scalar(inv[:], cnt[:], 1.0, None, ALU.max))
                link(nc.vector.reciprocal(inv[:], inv[:]))
                link(nc.vector.tensor_tensor(mean[:, :, D:D + 1], cnt[:].unsqueeze(2), inv[:].unsqueeze(2), ALU.mult))
                for b, tiles in groups(BANK):
                    t = slice(tiles[0], tiles[-1] + 1)
                    dve.wait_ge(sums_out, b + 1)
                    nc.vector.tensor_tensor(mean[:, t, 0:D], ps_out[b][:, 0:len(tiles), :],
                                            inv[:, t].unsqueeze(2).to_broadcast([NP, len(tiles), D]), ALU.mult).then_inc(means, 1)
                for b, tiles in groups(BANK):
                    t = slice(tiles[0], tiles[-1] + 1)
                    dve.wait_ge(made, b + 1)
                    link(nc.vector.tensor_tensor(centred[:, t, :], ps_out[b][:, 0:len(tiles), :], on_nodes(w["b2b"], t), ALU.add))
                    nc.vector.tensor_tensor(x[:, t, :], x[:, t, :], centred[:, t, :], ALU.add).then_inc(ready, 1)

            @block.tensor
            def _(pe):
                for b, tiles in groups(BANK):
                    for k in tiles:
                        last = nc.tensor.transpose(ps_out[b][:, k % BANK, :], agg_t[:, k, 0:NP], ident[0:D, 0:D])
                    last.then_inc(sums_out, 1)
                for i in range(n4 + 3):
                    if i < n4:
                        pe.wait_ge(means, fours[i][1][-1] // BANK + 1)
                        if i >= 2:
                            pe.wait_ge(emptied, i - 1)
                        turn_group(nc, g, ps_turn[i % 2], mean, D + 1, fours[i][1]).then_inc(turned, 1)
                    if 1 <= i <= n4:
                        pe.wait_ge(emptied, i)
                        if i >= 2:
                            pe.wait_ge(agg_used, i - 1)
                        dense_group(nc, ps_agg, [(w["W1b"][:].rearrange("k z d -> k (z d)"), mean_t)], fours[i - 1][1]).then_inc(agg_done, 1)
                    if 2 <= i <= n4 + 1:
                        pe.wait_ge(agg_used, i - 1)
                        if i >= 3:
                            pe.wait_ge(hid_used, i - 2)
                        dense_group(nc, ps_hid, [(w["W2a"][:], cat_t)], fours[i - 2][1]).then_inc(hid_done, 1)
                    if i >= 3:
                        pe.wait_ge(hid_used, i - 2)
                        by_node(nc, ps_out, hidden, w["W2b"][:], fours[i - 3][1], made)

            @block.scalar
            def _(act):
                for i in range(n4 + 2):
                    if i < n4:
                        act.wait_ge(turned, i + 1)
                        empty_group(nc, mean_t, ps_turn[i % 2], fours[i][1], ACT.Copy).then_inc(emptied, 1)
                    if 1 <= i <= n4:
                        act.wait_ge(agg_done, i)
                        empty_group(nc, cat_t[D:2 * D, :], ps_agg[D:2 * D, :], fours[i - 1][1], ACT.Copy).then_inc(agg_used, 1)
                    if i >= 2:
                        act.wait_ge(hid_done, i - 1)
                        empty_group(nc, hidden, ps_hid, fours[i - 2][1], ACT.Relu, bias=w["b2a"][:]).then_inc(hid_used, 1)

            @block.sync
            def _(sp):
                for b, tiles in groups(BANK):
                    t = slice(tiles[0], tiles[-1] + 1)
                    sp.wait_ge(ready, b + 1)
                    sp.dma_start(out[:, t, :], x[:, t, :]).then_inc(stored, 16)
                sp.wait_ge(stored, 16 * len(groups(BANK)))


_INS = ["x", "src", "dst", "edge_attr_64", "edge_weight", "L1_gnn_W", "L1_gnn_b", "L2_gnn_W1", "L2_gnn_b1", "L2_gnn_W2",
        "L2_gnn_b2", "L3_gnn_W1a", "L3_gnn_b1a", "L3_gnn_W1b", "L3_gnn_b1b", "L3_gnn_W2a", "L3_gnn_b2a", "L3_gnn_W2b",
        "L3_gnn_b2b"]


def constants():
    import numpy as np

    tiles = np.arange(NT, dtype=np.float32)
    advance = np.zeros((NT, 32), np.float32)
    for w in range(NW):
        advance[:, w if w < NG else HALF + w - NG] = WIN * (1 + (tiles == w)) if w < NT else 2 * WIN
    n = NT * HB
    at_block = np.arange(n)
    return {
        "identity": np.eye(128, dtype=np.float32),
        "iota_four_times": np.repeat(np.arange(NP), 4).astype(np.float16)[None],
        "key_numbers": np.arange(KW, dtype=np.float32)[None],
        "tile_steps": STEP * tiles[None],
        "tile_bases": NP * tiles[None] - CENTRE,
        "advance": advance,
        "before": np.triu(np.ones((NP, NP), np.float32), 1),
        "same_column": (at_block[:, None] % HB == at_block % HB).astype(np.float32),
        "fold": (at_block[:, None] // HB == np.arange(NT)).astype(np.float32),
    }


def kernel(**inputs):
    import numpy as _np
    import concourse.bacc as _bacc
    from concourse import mybir as _mybir
    from concourse.bass_utils import run_bass_kernel_spmd as _run

    nc = _bacc.Bacc("TRN2", target_bir_lowering=False, num_devices=1)
    arrays, args = {}, []
    given = {name: inputs[name] for name in _INS}
    given.update(constants())
    for name, a in given.items():
        a = _np.ascontiguousarray(a)
        arrays[f"in_{name}_dram"] = a
        args.append(nc.dram_tensor(f"in_{name}_dram", a.shape, _mybir.dt.from_np(a.dtype), kind="ExternalInput").ap())
    args.append(nc.dram_tensor("out_0_dram", (N_NODES, D), F32, kind="ExternalOutput").ap())
    build(nc, *args)
    r = _run(nc, [arrays], core_ids=[0])
    return r.results[0]["out_0_dram"]
```
